# Optimizing a Trainium2 kernel written in Bass

```python
import numpy as np
import jax
import jax.numpy as jnp

def _softmax(x, axis=-1):
    return jax.nn.softmax(x, axis=axis)

def _gelu(x):
    return jax.nn.gelu(x, approximate=True)

def _silu(x):
    return jax.nn.silu(x)

def _sigmoid(x):
    return jax.nn.sigmoid(x)

def _layernorm(x, axis=-1, eps=1e-05):
    m = jnp.mean(x, axis=axis, keepdims=True)
    v = jnp.var(x, axis=axis, keepdims=True)
    return (x - m) / jnp.sqrt(v + eps)

def _scatter_add(tgt, idx, src, axis=0):
    return tgt.at[idx].add(src)

def _segment_sum(src, seg, n):
    return jax.ops.segment_sum(src, seg, n)
kernel_name = 'mk_hybrid_d1_jaxref_r4_8c7cec'

def setup_inputs(seed: int=0):
    np.random.seed(seed)
    _w = jnp.asarray

    def _L0_attn_a_setup():
        import jax, jax.numpy as jnp
        import numpy as np
        NUM_HEAD = 16
        D_Q = 128
        D_KV = 128
        ROPE_BASE = 10000.0

        def _cos_sin(seq_len, dim):
            pos = jnp.arange(seq_len, dtype=jnp.float32)[:, None]
            ids = jnp.arange(dim // 2, dtype=jnp.float32)
            theta = ROPE_BASE ** (-2.0 * ids) / (dim // 2)
            r = pos * theta[None, :]
            return (jnp.cos(r), jnp.sin(r))

        def _rope(x, cos, sin):
            b, s, d = x.shape
            xv = x.reshape(b, s, d // 2, 2)
            x0, x1 = (xv[..., 0], xv[..., 1])
            out = jnp.stack([x0 * cos - x1 * sin, x1 * cos + x0 * sin], axis=-1)
            return out.reshape(b, s, d)
        key = jax.random.key(seed)
        ks = jax.random.split(key, 10)
        d_model, d_q, d_kv = (256, D_Q, D_KV)
        b, s = (2, 512)
        w = lambda k, i, o: jax.random.normal(k, (i, o), dtype=jnp.float32) * 0.02
        return {'x': jax.random.normal(ks[0], (b, s, d_model), dtype=jnp.float32), 'Wd_q_w': w(ks[1], d_model, d_q), 'Wd_q_b': jnp.zeros((d_q,), jnp.float32), 'Wu_q_w': w(ks[2], d_q, d_model), 'Wu_q_b': jnp.zeros((d_model,), jnp.float32), 'Wq_r_w': w(ks[3], d_q, d_model), 'Wq_r_b': jnp.zeros((d_model,), jnp.float32), 'Wk_r_w': w(ks[4], d_model, d_model), 'Wk_r_b': jnp.zeros((d_model,), jnp.float32), 'Wd_kv_w': w(ks[5], d_model, d_kv), 'Wd_kv_b': jnp.zeros((d_kv,), jnp.float32), 'Wu_k_w': w(ks[6], d_kv, d_model), 'Wu_k_b': jnp.zeros((d_model,), jnp.float32), 'Wu_v_w': w(ks[7], d_kv, d_model), 'Wu_v_b': jnp.zeros((d_model,), jnp.float32), 'Wo_w': w(ks[8], d_model, d_model), 'Wo_b': jnp.zeros((d_model,), jnp.float32)}
    _L0_attn_a_in = _L0_attn_a_setup()

    def _L0_attn_b_setup():
        import jax, jax.numpy as jnp
        import numpy as np
        import math
        B, L, D, N, K, R = (2, 512, 256, 16, 4, 64)

        def _selective_scan(x, W_x, W_z, W_params, conv_w, W_dt, b_dt, A_log, D_param, W_out):
            b, l, d = x.shape
            x_res = x @ W_x.T
            z = x @ W_z.T
            params = x @ W_params.T
            dt_unproj = params[..., :R]
            B_proj = params[..., R:R + N]
            C_proj = params[..., R + N:]
            dt = jax.nn.softplus(dt_unproj @ W_dt.T + b_dt)
            xc = jnp.swapaxes(x_res, 1, 2)
            conv = jax.lax.conv_general_dilated(xc, conv_w, window_strides=(1,), padding=[(K - 1, 0)], dimension_numbers=('NCH', 'OIH', 'NCH'), feature_group_count=d)
            u = jax.nn.silu(jnp.swapaxes(conv, 1, 2))
            A = -jnp.exp(A_log)
            A_tilde = jnp.exp(dt[..., None] * A)
            B_tilde = jnp.where(jnp.abs(A) < 1e-08, dt[..., None], (A_tilde - 1.0) / (A + 1e-10))
            Am = jnp.moveaxis(A_tilde, 1, 0)
            Bm = jnp.moveaxis(B_tilde, 1, 0)
            Bp = jnp.moveaxis(B_proj, 1, 0)
            Cp = jnp.moveaxis(C_proj, 1, 0)
            um = jnp.moveaxis(u, 1, 0)

            def step(h, ins):
                A_t, B_t, Bp_t, Cp_t, u_t = ins
                h = A_t * h + B_t * Bp_t[:, None, :] * u_t[:, :, None]
                y_t = jnp.einsum('bn,bdn->bd', Cp_t, h)
                return (h, y_t)
            h0 = jnp.zeros((b, d, N), dtype=A_tilde.dtype)
            _, ys = jax.lax.scan(step, h0, (Am, Bm, Bp, Cp, um))
            y = jnp.moveaxis(ys, 0, 1)
            y = y + u * D_param
            y = y * jax.nn.silu(z)
            return y @ W_out.T
        key = jax.random.key(seed)
        ks = jax.random.split(key, 8)
        s = 0.02
        inv_softplus_001 = math.log(math.expm1(0.01))
        return {'x': jax.random.normal(ks[0], (B, L, D), dtype=jnp.float32), 'W_x': jax.random.normal(ks[1], (D, D), dtype=jnp.float32) * s, 'W_z': jax.random.normal(ks[2], (D, D), dtype=jnp.float32) * s, 'W_params': jax.random.normal(ks[3], (R + 2 * N, D), dtype=jnp.float32) * s, 'conv_w': jax.random.normal(ks[4], (D, 1, K), dtype=jnp.float32) * s, 'W_dt': jax.random.uniform(ks[5], (D, R), dtype=jnp.float32, minval=-R ** (-0.5), maxval=R ** (-0.5)), 'b_dt': jnp.full((D,), inv_softplus_001, dtype=jnp.float32), 'A_log': jnp.tile(jnp.log(jnp.arange(1, N + 1, dtype=jnp.float32))[None, :], (D, 1)), 'D_param': jnp.ones((D,), dtype=jnp.float32), 'W_out': jax.random.normal(ks[6], (D, D), dtype=jnp.float32) * s}
    _L0_attn_b_in = _L0_attn_b_setup()

    def _L0_ffn_setup():
        import jax, jax.numpy as jnp
        import numpy as np
        import math
        BETA = 0.9
        THRESHOLD = 1.0
        NUM_STEPS = 5
        ALPHA = 2.0

        @jax.custom_vjp
        def spike_fn(u):
            return (u > 0).astype(u.dtype)

        def _spike_fwd(u):
            return (spike_fn(u), u)

        def _spike_bwd(u, g):
            s = jnp.pi / 2.0 * ALPHA * u
            return (g * (ALPHA / 2.0) / (1.0 + s * s),)
        spike_fn.defvjp(_spike_fwd, _spike_bwd)
        key = jax.random.key(seed)
        k1, k2, k3 = jax.random.split(key, 3)
        n_embd = 256
        x = jax.random.normal(k1, (4, 512, n_embd), dtype=jnp.float32)
        W_fc = jax.random.normal(k2, (4 * n_embd, n_embd), dtype=jnp.float32) / math.sqrt(n_embd)
        W_proj = jax.random.normal(k3, (n_embd, 4 * n_embd), dtype=jnp.float32) / math.sqrt(4 * n_embd)
        return {'x': x, 'W_fc': W_fc, 'W_proj': W_proj}
    _L0_ffn_in = _L0_ffn_setup()
    _d = {'L0_attn_a_x': _L0_attn_a_in['x'], 'L0_attn_a_Wd_q_w': _L0_attn_a_in['Wd_q_w'], 'L0_attn_a_Wd_q_b': _L0_attn_a_in['Wd_q_b'], 'L0_attn_a_Wu_q_w': _L0_attn_a_in['Wu_q_w'], 'L0_attn_a_Wu_q_b': _L0_attn_a_in['Wu_q_b'], 'L0_attn_a_Wq_r_w': _L0_attn_a_in['Wq_r_w'], 'L0_attn_a_Wq_r_b': _L0_attn_a_in['Wq_r_b'], 'L0_attn_a_Wk_r_w': _L0_attn_a_in['Wk_r_w'], 'L0_attn_a_Wk_r_b': _L0_attn_a_in['Wk_r_b'], 'L0_attn_a_Wd_kv_w': _L0_attn_a_in['Wd_kv_w'], 'L0_attn_a_Wd_kv_b': _L0_attn_a_in['Wd_kv_b'], 'L0_attn_a_Wu_k_w': _L0_attn_a_in['Wu_k_w'], 'L0_attn_a_Wu_k_b': _L0_attn_a_in['Wu_k_b'], 'L0_attn_a_Wu_v_w': _L0_attn_a_in['Wu_v_w'], 'L0_attn_a_Wu_v_b': _L0_attn_a_in['Wu_v_b'], 'L0_attn_a_Wo_w': _L0_attn_a_in['Wo_w'], 'L0_attn_a_Wo_b': _L0_attn_a_in['Wo_b'], 'L0_attn_b_W_x': _L0_attn_b_in['W_x'], 'L0_attn_b_W_z': _L0_attn_b_in['W_z'], 'L0_attn_b_W_params': _L0_attn_b_in['W_params'], 'L0_attn_b_conv_w': _L0_attn_b_in['conv_w'], 'L0_attn_b_W_dt': _L0_attn_b_in['W_dt'], 'L0_attn_b_b_dt': _L0_attn_b_in['b_dt'], 'L0_attn_b_A_log': _L0_attn_b_in['A_log'], 'L0_attn_b_D_param': _L0_attn_b_in['D_param'], 'L0_attn_b_W_out': _L0_attn_b_in['W_out'], 'L0_ffn_W_fc': _L0_ffn_in['W_fc'], 'L0_ffn_W_proj': _L0_ffn_in['W_proj']}
    _x0 = _d['L0_attn_a_x']
    _d['L0_attn_a_x'] = jax.random.normal(jax.random.fold_in(jax.random.key(seed), 1), (4, 1024, 256), dtype=_x0.dtype)
    del _x0
    return _d

def reference(L0_attn_a_x, L0_attn_a_Wd_q_w, L0_attn_a_Wd_q_b, L0_attn_a_Wu_q_w, L0_attn_a_Wu_q_b, L0_attn_a_Wq_r_w, L0_attn_a_Wq_r_b, L0_attn_a_Wk_r_w, L0_attn_a_Wk_r_b, L0_attn_a_Wd_kv_w, L0_attn_a_Wd_kv_b, L0_attn_a_Wu_k_w, L0_attn_a_Wu_k_b, L0_attn_a_Wu_v_w, L0_attn_a_Wu_v_b, L0_attn_a_Wo_w, L0_attn_a_Wo_b, L0_attn_b_W_x, L0_attn_b_W_z, L0_attn_b_W_params, L0_attn_b_conv_w, L0_attn_b_W_dt, L0_attn_b_b_dt, L0_attn_b_A_log, L0_attn_b_D_param, L0_attn_b_W_out, L0_ffn_W_fc, L0_ffn_W_proj):

    def _L0_attn_a_ref(x, Wd_q_w, Wd_q_b, Wu_q_w, Wu_q_b, Wq_r_w, Wq_r_b, Wk_r_w, Wk_r_b, Wd_kv_w, Wd_kv_b, Wu_k_w, Wu_k_b, Wu_v_w, Wu_v_b, Wo_w, Wo_b):
        import jax, jax.numpy as jnp
        import numpy as np
        NUM_HEAD = 16
        D_Q = 128
        D_KV = 128
        ROPE_BASE = 10000.0

        def _cos_sin(seq_len, dim):
            pos = jnp.arange(seq_len, dtype=jnp.float32)[:, None]
            ids = jnp.arange(dim // 2, dtype=jnp.float32)
            theta = ROPE_BASE ** (-2.0 * ids) / (dim // 2)
            r = pos * theta[None, :]
            return (jnp.cos(r), jnp.sin(r))

        def _rope(x, cos, sin):
            b, s, d = x.shape
            xv = x.reshape(b, s, d // 2, 2)
            x0, x1 = (xv[..., 0], xv[..., 1])
            out = jnp.stack([x0 * cos - x1 * sin, x1 * cos + x0 * sin], axis=-1)
            return out.reshape(b, s, d)
        b, s, d_model = x.shape
        h = NUM_HEAD
        hd = d_model // h
        scale = jnp.sqrt(jnp.float32(h + D_KV + D_Q))

        def heads(t):
            return t.reshape(b, s, h, hd).transpose(0, 2, 1, 3)
        cos, sin = _cos_sin(s, d_model)
        ct_q = x @ Wd_q_w + Wd_q_b
        qt_c = heads(ct_q @ Wu_q_w + Wu_q_b)
        qt_r = heads(_rope(ct_q @ Wq_r_w + Wq_r_b, cos, sin))
        query = qt_c + qt_r
        ct_kv = x @ Wd_kv_w + Wd_kv_b
        kt_c = heads(ct_kv @ Wu_k_w + Wu_k_b)
        kt_r = heads(_rope(x @ Wk_r_w + Wk_r_b, cos, sin))
        key = kt_c + kt_r
        value = heads(ct_kv @ Wu_v_w + Wu_v_b)
        attn = jnp.einsum('bhqd,bhkd->bhqk', query, key) / scale
        attn = jax.nn.softmax(attn, axis=-1)
        out = jnp.einsum('bhqk,bhkd->bhqd', attn, value)
        out = out.transpose(0, 2, 1, 3).reshape(b, s, d_model)
        return out @ Wo_w + Wo_b

    def _L0_attn_b_ref(x, W_x, W_z, W_params, conv_w, W_dt, b_dt, A_log, D_param, W_out):
        import jax, jax.numpy as jnp
        import numpy as np
        import math
        B, L, D, N, K, R = (2, 512, 256, 16, 4, 64)

        def _selective_scan(x, W_x, W_z, W_params, conv_w, W_dt, b_dt, A_log, D_param, W_out):
            b, l, d = x.shape
            x_res = x @ W_x.T
            z = x @ W_z.T
            params = x @ W_params.T
            dt_unproj = params[..., :R]
            B_proj = params[..., R:R + N]
            C_proj = params[..., R + N:]
            dt = jax.nn.softplus(dt_unproj @ W_dt.T + b_dt)
            xc = jnp.swapaxes(x_res, 1, 2)
            conv = jax.lax.conv_general_dilated(xc, conv_w, window_strides=(1,), padding=[(K - 1, 0)], dimension_numbers=('NCH', 'OIH', 'NCH'), feature_group_count=d)
            u = jax.nn.silu(jnp.swapaxes(conv, 1, 2))
            A = -jnp.exp(A_log)
            A_tilde = jnp.exp(dt[..., None] * A)
            B_tilde = jnp.where(jnp.abs(A) < 1e-08, dt[..., None], (A_tilde - 1.0) / (A + 1e-10))
            Am = jnp.moveaxis(A_tilde, 1, 0)
            Bm = jnp.moveaxis(B_tilde, 1, 0)
            Bp = jnp.moveaxis(B_proj, 1, 0)
            Cp = jnp.moveaxis(C_proj, 1, 0)
            um = jnp.moveaxis(u, 1, 0)

            def step(h, ins):
                A_t, B_t, Bp_t, Cp_t, u_t = ins
                h = A_t * h + B_t * Bp_t[:, None, :] * u_t[:, :, None]
                y_t = jnp.einsum('bn,bdn->bd', Cp_t, h)
                return (h, y_t)
            h0 = jnp.zeros((b, d, N), dtype=A_tilde.dtype)
            _, ys = jax.lax.scan(step, h0, (Am, Bm, Bp, Cp, um))
            y = jnp.moveaxis(ys, 0, 1)
            y = y + u * D_param
            y = y * jax.nn.silu(z)
            return y @ W_out.T
        return _selective_scan(x, W_x, W_z, W_params, conv_w, W_dt, b_dt, A_log, D_param, W_out)

    def _L0_ffn_ref(x, W_fc, W_proj):
        import jax, jax.numpy as jnp
        import numpy as np
        import math
        BETA = 0.9
        THRESHOLD = 1.0
        NUM_STEPS = 5
        ALPHA = 2.0

        @jax.custom_vjp
        def spike_fn(u):
            return (u > 0).astype(u.dtype)

        def _spike_fwd(u):
            return (spike_fn(u), u)

        def _spike_bwd(u, g):
            s = jnp.pi / 2.0 * ALPHA * u
            return (g * (ALPHA / 2.0) / (1.0 + s * s),)
        spike_fn.defvjp(_spike_fwd, _spike_bwd)
        h = jnp.square(jax.nn.relu(jnp.einsum('bsd,fd->bsf', x, W_fc)))
        y = jnp.einsum('bsf,df->bsd', h, W_proj)

        def step(mem, _):
            reset = jax.lax.stop_gradient(spike_fn(mem - THRESHOLD))
            mem_new = BETA * mem + y - reset * THRESHOLD
            spk = spike_fn(mem_new - THRESHOLD)
            return (mem_new, spk)
        mem0 = jnp.zeros_like(y)
        _, spks = jax.lax.scan(step, mem0, None, length=NUM_STEPS)
        return jnp.sum(spks, axis=0) / NUM_STEPS
    x = L0_attn_a_x
    x = x + _L0_attn_a_ref(_layernorm(x, axis=-1), L0_attn_a_Wd_q_w, L0_attn_a_Wd_q_b, L0_attn_a_Wu_q_w, L0_attn_a_Wu_q_b, L0_attn_a_Wq_r_w, L0_attn_a_Wq_r_b, L0_attn_a_Wk_r_w, L0_attn_a_Wk_r_b, L0_attn_a_Wd_kv_w, L0_attn_a_Wd_kv_b, L0_attn_a_Wu_k_w, L0_attn_a_Wu_k_b, L0_attn_a_Wu_v_w, L0_attn_a_Wu_v_b, L0_attn_a_Wo_w, L0_attn_a_Wo_b)
    x = x + _L0_ffn_ref(_layernorm(x, axis=-1), L0_ffn_W_fc, L0_ffn_W_proj)
    x = x + _L0_attn_b_ref(_layernorm(x, axis=-1), L0_attn_b_W_x, L0_attn_b_W_z, L0_attn_b_W_params, L0_attn_b_conv_w, L0_attn_b_W_dt, L0_attn_b_b_dt, L0_attn_b_A_log, L0_attn_b_D_param, L0_attn_b_W_out)
    x = x + _L0_ffn_ref(_layernorm(x, axis=-1), L0_ffn_W_fc, L0_ffn_W_proj)
    return x

_drawn_inputs = setup_inputs


def setup_inputs(seed=0):
    import zlib

    import numpy as np

    out = dict(_drawn_inputs(seed))
    spreads = {'L0_attn_a_Wd_q_b': (0.0, 0.8),
     'L0_attn_a_Wu_q_b': (0.0, 0.8),
     'L0_attn_a_Wq_r_b': (0.0, 0.8),
     'L0_attn_a_Wk_r_b': (0.0, 0.8),
     'L0_attn_a_Wd_kv_b': (0.0, 0.32),
     'L0_attn_a_Wu_k_b': (0.0, 0.8),
     'L0_attn_a_Wu_v_b': (0.0, 0.1),
     'L0_attn_a_Wo_b': (0.0, 0.1),
     'L0_attn_b_b_dt': (-4.600165843963623, 0.6),
     'L0_attn_b_D_param': (1.0, 0.6)}
    factors = {'L0_attn_a_Wd_q_w': 8.0,
     'L0_attn_a_Wu_q_w': 8.0,
     'L0_attn_a_Wq_r_w': 8.0,
     'L0_attn_a_Wk_r_w': 8.0,
     'L0_attn_a_Wd_kv_w': 7.114,
     'L0_attn_a_Wu_k_w': 8.0,
     'L0_attn_a_Wu_v_w': 2.819,
     'L0_attn_b_W_x': 8.0,
     'L0_attn_b_W_z': 8.0,
     'L0_attn_b_W_params': 8.0,
     'L0_attn_b_conv_w': 8.0,
     'L0_attn_b_W_dt': 8.0,
     'L0_attn_b_A_log': 8.0,
     'L0_attn_b_W_out': 8.0}
    for name, (base, spread) in spreads.items():
        noise = np.random.default_rng([zlib.crc32(name.encode()), seed]).standard_normal(out[name].shape)
        drawn = base * np.exp(spread * noise) if base else spread * noise
        out[name] = jnp.asarray(drawn.astype(out[name].dtype))
    for name, factor in factors.items():
        out[name] = (out[name] * factor).astype(out[name].dtype)
    return out
```

```python
import numpy as np
from contextlib import ExitStack

import concourse.bass as bass
from concourse import mybir

F32 = mybir.dt.float32
BF16 = mybir.dt.bfloat16
I32 = mybir.dt.int32
ALU = mybir.AluOpType
ACT = mybir.ActivationFunctionType
AX_X = mybir.AxisListType.X

P = 128
B, S, D = 4, 1024, 256
T = B * S
TW = 512
NT = T // TW
TPB = S // TW
DC = D // P
H = 16
HD = D // H
LAT = 128
G = 4
NG = H // G
QT = S // P
FF = 4 * D
FC = FF // P
R = 64
NS = 16
TAPS = 4
EPS = 1e-5
SOFTMAX_SCALE = 1.0 / float(np.sqrt(np.float32(H + LAT + LAT)))
Q_PARTS = (0, 0, 1, 1, 0, 2)
K_PARTS = (0, 1, 0, 1, 2, 0)
SROWS = len(Q_PARTS) * HD
MROWS = SROWS + 3
LIF_STEPS, BETA, THRESHOLD = 5, 0.9, 1.0


def spike_thresholds():
    f = np.float32

    def spikes(y):
        mem, count = f(0), 0
        for _ in range(LIF_STEPS):
            reset = f(mem - f(THRESHOLD) > 0)
            mem = f(f(f(f(BETA) * mem) + y) - f(reset * f(THRESHOLD)))
            count += int(mem - f(THRESHOLD) > 0)
        return count

    found = []
    for k in range(1, LIF_STEPS + 1):
        low, high = (int(np.array(v, f).view(np.int32)) for v in (0.0, 64.0))
        while high - low > 1:
            mid = (low + high) // 2
            if spikes(np.array(mid, np.int32).view(f)[()]) >= k:
                high = mid
            else:
                low = mid
        found.append(float(np.array(low, np.int32).view(f)))
    return found


THETA = spike_thresholds()


def by_itself(eng, waited):
    eng.sem_inc(waited, 1)


class Mem:

    def __init__(self, nc, ctx):
        self.nc, self.ctx = nc, ctx

    def sb(self, name, shape, dt=F32):
        return self.ctx.enter_context(self.nc.sbuf_tensor(name, shape, dt))

    def bank(self, name):
        return self.ctx.enter_context(self.nc.psum_tensor(name, [P, TW], F32))

    def sem(self, name):
        return self.ctx.enter_context(self.nc.semaphore(name))


def project(nc, io, xT, vT, split_scr):
    with ExitStack() as ctx:
        m = Mem(nc, ctx)
        ident = m.sb("ident", [P, P])
        mean_w = m.sb("mean_w", [P, P])
        eps_col = m.sb("eps_col", [P, 1])
        cosT = m.sb("cosT", [P, DC, S])
        sinT = m.sb("sinT", [P, DC, S])
        wdq = m.sb("wdq", [P, DC, LAT])
        wdkv = m.sb("wdkv", [P, DC, LAT])
        wq = m.sb("wq", [P, 3, D])
        wkc = m.sb("wkc", [P, D])
        wkr = m.sb("wkr", [P, 2, DC, D])
        wv = m.sb("wv", [P, D])
        bv = m.sb("bv", [P, D])
        bcol = m.sb("bcol", [P, 14])
        xin = m.sb("xin", [P, 2, TW // P, D])
        xc = m.sb("xc", [P, DC, TW])
        sq = m.sb("sq", [P, DC, TW])
        rs = m.sb("rs", [P, 3, TW])
        xn = m.sb("xn", [P, DC, TW])
        ct = m.sb("ct", [P, 2, TW])
        rot = m.sb("rot", [P, 3, TW])
        full = m.sb("full", [P, 2, TW])
        rest = m.sb("rest", [P, 2, TW])
        parts = m.sb("parts", [P, 2, 3, TW], BF16)
        tr_bank = [m.bank(f"tr_bank{c}") for c in range(DC)]
        mean_bank, var_bank = m.bank("mean_bank"), m.bank("var_bank")
        proj = [m.bank(f"proj{i}") for i in range(4)]

        consts_in = m.sem("consts_in")
        x_in = [m.sem("x_in0"), m.sem("x_in1")]
        consts_set = m.sem("consts_set")
        transposed, x_kept = m.sem("transposed"), m.sem("x_kept")
        mean_ready, centred, squared = m.sem("mean_ready"), m.sem("centred"), m.sem("squared")
        var_ready, rs_guess, rs_step, normed = m.sem("var_ready"), m.sem("rs_guess"), m.sem("rs_step"), m.sem("normed")
        proj_ready, latent_kept, rotated = m.sem("proj_ready"), m.sem("latent_kept"), m.sem("rotated")
        summed, high_kept, mid_kept = m.sem("summed"), m.sem("high_kept"), m.sem("mid_kept")
        rest_ready, low_kept, v_kept = m.sem("rest_ready"), m.sem("low_kept"), m.sem("v_kept")
        parts_out = [m.sem("parts_out0"), m.sem("parts_out1")]

        loads = [(ident[:], io["ident"]), (cosT[:], io["cos"].rearrange("(c p) t -> p c t", p=P)),
                 (sinT[:], io["sin"].rearrange("(c p) t -> p c t", p=P)),
                 (wdq[:], io["Wd_q"].rearrange("(c p) n -> p c n", p=P)),
                 (wdkv[:], io["Wd_kv"].rearrange("(c p) n -> p c n", p=P)),
                 (wq[:, 0, :], io["Wu_q"]), (wq[:, 1, :], io["Wq_r"]), (wq[:, 2, :], io["Wq_r_swap"]),
                 (wkc[:], io["Wu_k"]), (wkr[:, 0], io["Wk_r"].rearrange("(c p) n -> p c n", p=P)),
                 (wkr[:, 1], io["Wk_r_swap"].rearrange("(c p) n -> p c n", p=P)),
                 (wv[:], io["Wu_v"]), (bv[:], io["bv"]), (bcol[:], io["bcol_attn"])]
        CONSTS = 16 * len(loads)
        x_dram = io["x"].rearrange("b (i j p) d -> (b i) p j d", j=TW // P, p=P)
        UNITS = 16

        act_waited = m.sem("act_waited_project")
        block = ctx.enter_context(nc.Block())

        @block.sync
        def _(sp):
            for u in range(2):
                sp.sem_inc(parts_out[u], 16)
            for t in range(2):
                sp.dma_start(xin[:, t], x_dram[t]).then_inc(x_in[t], 16)
            for dst, src in loads:
                sp.dma_start(dst, src).then_inc(consts_in, 16)

            def parts_of(b, half, with_loads):
                t = b * 2 + half
                if with_loads:
                    sp.wait_ge(transposed, t * DC + DC)
                    sp.dma_start(xin[:, half], x_dram[bass.ds(t + 2, 1)].rearrange("a p j d -> (a p) j d"))\
                        .then_inc(x_in[half], 16)
                for u in range(4):
                    sp.wait_ge(low_kept, t * 4 + u + 1)
                    sp.dma_start(split_scr[bass.ds(b * DC + (u // 2 * B * DC + u % 2), 1), :, :, half * TW:(half + 1) * TW]
                                 .rearrange("a p s t -> (a p) s t"),
                                 parts[:, u % 2]).then_inc(parts_out[u % 2], 16)

            with sp.Fori(0, B - 1) as b:
                parts_of(b, 0, True)
                parts_of(b, 1, True)
            parts_of(B - 1, 0, False)
            parts_of(B - 1, 1, False)
            for u in range(2):
                sp.wait_ge(parts_out[u], 16 * 2 * NT + 16)

        @block.gpsimd
        def _(pool):
            nc.gpsimd.memset(mean_w[:], 1.0 / D).then_inc(consts_set, 1)
            nc.gpsimd.memset(eps_col[:], EPS).then_inc(consts_set, 1)

        @block.tensor
        def _(pe):
            pe.sem_inc(var_ready, 1)
            pe.wait_ge(consts_in, CONSTS)
            pe.wait_ge(consts_set, 2)

            def bank_free(t, u):
                if u < 2:
                    pe.wait_ge(rotated, t * 12 + u + 1)
                elif u < 4:
                    pe.wait_ge(v_kept, t * 2 + u - 1)
                elif u < 6:
                    pe.wait_ge(latent_kept, t * 2 + u - 3)
                else:
                    pe.wait_ge(rotated, t * 12 + u - 3)

            def tile(b, half):
                t = b * 2 + half
                pe.wait_ge(x_in[half], b * 16 + 16)
                for c in range(DC):
                    pe.wait_ge(x_kept, t * DC + c + 1)
                    for j in range(TW // P):
                        mm = nc.tensor.transpose(tr_bank[c][:, j * P:(j + 1) * P],
                                                 xin[:, half, j, c * P:(c + 1) * P], ident[:])
                    mm.then_inc(transposed, 1)
                pe.wait_ge(x_kept, t * DC + 2 * DC)
                pe.wait_ge(centred, t * DC + DC)
                for c in range(DC):
                    mm = nc.tensor.matmul(mean_bank[:], mean_w[:], xT[:, c, bass.ds(t * TW, TW)],
                                          start=(c == 0), stop=(c == DC - 1))
                mm.then_inc(mean_ready, 1)
                pe.wait_ge(squared, t * DC + DC)
                pe.wait_ge(rs_step, t * 3 + 1)
                for c in range(DC):
                    mm = nc.tensor.matmul(var_bank[:], mean_w[:], sq[:, c], start=(c == 0), stop=(c == DC - 1))
                mm.then_inc(var_ready, 1)
                pe.wait_ge(normed, t * DC + DC)
                u = 0
                for w in (wdq, wdkv):
                    bank_free(t, u)
                    for c in range(DC):
                        mm = nc.tensor.matmul(proj[u][:], w[:, c], xn[:, c], start=(c == 0), stop=(c == DC - 1))
                    mm.then_inc(proj_ready, 1)
                    u += 1
                for side in range(2):
                    for c in range(DC):
                        cols = slice(c * P, (c + 1) * P)
                        for kind in (1, 2, 0):
                            bank_free(t, u)
                            if u in (2, 8):
                                pe.wait_ge(latent_kept, t * 2 + 2)
                            if side == 0 or kind == 0:
                                w = wq[:, kind, cols] if side == 0 else wkc[:, cols]
                                mm = nc.tensor.matmul(proj[u % 4][:], w, ct[:, side], start=True, stop=True)
                            else:
                                for k in range(DC):
                                    mm = nc.tensor.matmul(proj[u % 4][:], wkr[:, kind - 1, k, cols], xn[:, k],
                                                          start=(k == 0), stop=(k == DC - 1))
                            mm.then_inc(proj_ready, 1)
                            u += 1
                for pair in range(2):
                    bank_free(t, u)
                    for j in range(2):
                        tok = slice((2 * pair + j) * P, (2 * pair + j + 1) * P)
                        mm = nc.tensor.matmul(proj[u % 4][:, j * D:(j + 1) * D], ct[:, 1, tok], wv[:],
                                              start=True, stop=True)
                    mm.then_inc(proj_ready, 1)
                    u += 1

            with pe.Fori(0, B) as b:
                tile(b, 0)
                tile(b, 1)

        @block.scalar
        def _(act):
            nc.scalar.sem_inc(x_kept, DC)
            act.wait_ge(consts_set, 2)
            act.wait_ge(consts_in, CONSTS)

            def tile(b, half):
                t = b * 2 + half
                for c in range(DC):
                    act.wait_ge(transposed, t * DC + c + 1)
                    by_itself(act, act_waited)
                    nc.scalar.activation(xT[:, c, bass.ds(t * TW, TW)], tr_bank[c][:], ACT.Copy).then_inc(x_kept, 1)
                for c in range(DC):
                    act.wait_ge(centred, t * DC + DC + c + 1)
                    act.wait_ge(var_ready, t + 1)
                    nc.scalar.activation(sq[:, c], xc[:, c], ACT.Square).then_inc(squared, 1)
                act.wait_ge(var_ready, t + 2)
                act.wait_ge(rs_step, t * 3 + 1)
                nc.scalar.activation(rs[:, 1], var_bank[:], ACT.Ln, bias=eps_col[:]).then_inc(rs_guess, 1)
                act.wait_ge(rs_guess, t * 2 + 1)
                nc.scalar.activation(rs[:, 0], rs[:, 1], ACT.Exp, scale=-0.5).then_inc(rs_guess, 1)
                for u in range(2):
                    act.wait_ge(proj_ready, t * UNITS + u + 1)
                    nc.scalar.activation(ct[:, u], proj[u][:], ACT.Identity, bias=bcol[:, u:u + 1])\
                        .then_inc(latent_kept, 1)
                for u in range(4):
                    act.wait_ge(summed, t * 4 + u + 1)
                    act.wait_ge(parts_out[u % 2], t * 32 + (u // 2) * 16 + 16)
                    nc.scalar.activation(parts[:, u % 2, 0], full[:, u % 2], ACT.Copy).then_inc(high_kept, 1)
                    act.wait_ge(rest_ready, t * 4 + u + 1)
                    nc.scalar.activation(parts[:, u % 2, 1], rest[:, u % 2], ACT.Copy).then_inc(mid_kept, 1)

            with act.Fori(0, B) as b:
                tile(b, 0)
                tile(b, 1)

        @block.vector
        def _(dve):
            nc.vector.sem_inc(centred, DC)
            nc.vector.sem_inc(rs_step, 1)
            nc.vector.sem_inc(rotated, 2)
            nc.vector.sem_inc(v_kept, 2)
            dve.wait_ge(consts_in, CONSTS)

            def tile(b, half):
                t = b * 2 + half
                for c in range(DC):
                    dve.wait_ge(mean_ready, t + 1)
                    nc.vector.tensor_tensor(xc[:, c], xT[:, c, bass.ds(t * TW, TW)], mean_bank[:], ALU.subtract)\
                        .then_inc(centred, 1)
                dve.wait_ge(rs_guess, t * 2 + 2)
                nc.vector.scalar_tensor_tensor(rs[:, 1], var_bank[:], EPS, rs[:, 0], ALU.add, ALU.mult)\
                    .then_inc(rs_step, 1)
                dve.wait_ge(rs_step, t * 3 + 2)
                nc.vector.scalar_tensor_tensor(rs[:, 2], rs[:, 1], -0.5, rs[:, 0], ALU.mult, ALU.mult)\
                    .then_inc(rs_step, 1)
                dve.wait_ge(rs_step, t * 3 + 3)
                nc.vector.scalar_tensor_tensor(rs[:, 1], rs[:, 2], 1.5, rs[:, 0], ALU.add, ALU.mult)\
                    .then_inc(rs_step, 1)
                dve.wait_ge(rs_step, t * 3 + 4)
                for c in range(DC):
                    nc.vector.tensor_tensor(xn[:, c], xc[:, c], rs[:, 1], ALU.mult).then_inc(normed, 1)
                for u in range(4):
                    side, c = u // 2, u % 2
                    n = t * 12 + 3 * u + 2
                    bias = bcol[:, 2 + 6 * side + 3 * c:5 + 6 * side + 3 * c]
                    banks = [proj[(2 + 3 * u + i) % 4] for i in range(3)]
                    for i, table in enumerate((cosT, sinT)):
                        dve.wait_ge(proj_ready, t * UNITS + 3 + 3 * u + i)
                        nc.vector.scalar_tensor_tensor(rot[:, i], banks[i][:], bias[:, i:i + 1],
                                                       table[:, c, half * TW:(half + 1) * TW], ALU.add, ALU.mult)\
                            .then_inc(rotated, 1)
                    dve.wait_ge(proj_ready, t * UNITS + 5 + 3 * u)
                    dve.wait_ge(rotated, n + 1)
                    nc.vector.scalar_tensor_tensor(rot[:, 2], banks[2][:], bias[:, 2:3], rot[:, 0], ALU.add, ALU.add)\
                        .then_inc(rotated, 1)
                    dve.wait_ge(rotated, n + 3)
                    nc.vector.tensor_tensor(full[:, u % 2], rot[:, 2], rot[:, 1], ALU.add).then_inc(summed, 1)
                    dve.wait_ge(high_kept, t * 4 + u + 1)
                    nc.vector.tensor_tensor(rest[:, u % 2], full[:, u % 2], parts[:, u % 2, 0], ALU.subtract)\
                        .then_inc(rest_ready, 1)
                    dve.wait_ge(mid_kept, t * 4 + u + 1)
                    nc.vector.tensor_tensor(parts[:, u % 2, 2], rest[:, u % 2], parts[:, u % 2, 1], ALU.subtract)\
                        .then_inc(low_kept, 1)
                for pair in range(2):
                    dve.wait_ge(proj_ready, t * UNITS + 15 + pair)
                    for j in range(2):
                        ins = nc.vector.tensor_tensor(vT[:, bass.ds(b * NG, NG), half * 4 + 2 * pair + j, :],
                                                      proj[2 + pair][:, j * D:(j + 1) * D].rearrange("p (g n) -> p g n", g=NG),
                                                      bv[:].rearrange("p (g n) -> p g n", g=NG), ALU.add)
                    ins.then_inc(v_kept, 1)

            with dve.Fori(0, B) as b:
                tile(b, 0)
                tile(b, 1)


def attend(nc, io, vT, split_scr, o_scr):
    NGT = B * NG
    UNITS = G * QT * 2
    HU = UNITS // 2
    LOAD = 16 * 3 * len(Q_PARTS)
    STEPS = 2 * QT
    with ExitStack() as ctx:
        m = Mem(nc, ctx)
        qs = [m.sb(f"qs{i}", [P, 2, G, TW], BF16) for i in range(3)]
        ks = [m.sb(f"ks{i}", [P, G, S], BF16) for i in range(3)]
        vg = [m.sb(f"vg{i}", [P, QT, G, 2 * HD]) for i in range(3)]
        ident = m.sb("ident_a", [P, P])
        probs = m.sb("probs", [P, 2, G, TW])
        mx = m.sb("mx", [P, 2, HU])
        row_max = m.sb("row_max", [P, 2, HU // 2])
        neg_max = m.sb("neg_max", [HU // 2, 2, P])
        neg_rest = m.sb("neg_rest", [HU // 2, 2, P])
        neg_parts = m.sb("neg_parts", [HU // 2, 2, 3, P], BF16)
        o_sb = m.sb("o_sb", [P, 2, TW])
        max_bank = [m.bank(f"max_bank{i}") for i in range(2)]
        score_bank = [m.ctx.enter_context(nc.psum_tensor(f"score_bank{i}", [P, 2, TW], F32)) for i in range(2)]
        o_bank = [m.bank(f"o_bank{i}") for i in range(2)]

        ident_in, ones_set, v_set = m.sem("ident_in"), m.sem("ones_set"), m.sem("v_set")
        stack_in = [m.sem(f"stack_in{i}") for i in range(3)]
        max_ready, reduced, row_max_ready = m.sem("max_ready"), m.sem("reduced"), m.sem("row_max_ready")
        turned, neg_ready, neg_split = m.sem("turned"), m.sem("neg_ready"), m.sem("neg_split")
        max_rows_in = [m.sem(f"max_rows_in{i}") for i in range(2)]
        scores_ready, probs_ready, pv_done = m.sem("scores_ready"), m.sem("probs_ready"), m.sem("pv_done")
        o_kept = m.sem("o_kept")
        o_out = [m.sem(f"o_out{i}") for i in range(2)]

        heads_in = split_scr.rearrange("a (h n) s t -> (a h) n s t", h=2)

        pool_waited = m.sem("pool_waited_attend")
        block = ctx.enter_context(nc.Block())

        def groups(eng, body):
            with eng.Fori(0, (NGT - 1) // 3) as it:
                for r in range(3):
                    body(it * 3 + r, r, it, True)
            body(NGT - 1, (NGT - 1) % 3, (NGT - 1) // 3, False)

        @block.sync
        def _(sp):
            for h in range(2):
                sp.sem_inc(max_rows_in[h], 16)
                sp.sem_inc(o_out[h], 16)

            def load(g, r):
                q_in, k_in = (heads_in[bass.ds(g + side * NGT, 1)].rearrange("a (j i) s t -> (a i) j s t", i=HD)
                              for side in range(2))
                for n in range(len(Q_PARTS)):
                    rows = slice(n * HD, (n + 1) * HD)
                    sp.dma_start(ks[r][rows], k_in[:, :, K_PARTS[n], :]).then_inc(stack_in[r], 16)
                    for h in range(2):
                        sp.dma_start(qs[r][rows, h], q_in[:, :, Q_PARTS[n], h * TW:(h + 1) * TW])\
                            .then_inc(stack_in[r], 16)

            def max_rows(g, r, h):
                sp.wait_ge(neg_split, g * 8 + 4 * h + 12)
                for part in range(3):
                    sp.dma_start(qs[r][SROWS + part:SROWS + part + 1, h], neg_parts[:, h, part, :]).then_inc(max_rows_in[h], 16)

            def o_to_dram(g, h):
                sp.wait_ge(o_kept, g * 2 + h + 3)
                sp.dma_start(o_scr[bass.ds(g, 1), :, h * TW:(h + 1) * TW].rearrange("a p t -> (a p) t"), o_sb[:, h])\
                    .then_inc(o_out[h], 16)

            def body(g, r, with_next=True, with_load=True):
                max_rows(g, r, 1)
                if with_load:
                    sp.wait_ge(scores_ready, g * 2 * STEPS + 1)
                    load(g + 2, (r + 2) % 3)
                if with_next:
                    max_rows(g + 1, (r + 1) % 3, 0)
                o_to_dram(g, 0)
                o_to_dram(g, 1)

            sp.dma_start(ident[:], io["ident"]).then_inc(ident_in, 16)
            load(0, 0)
            load(1, 1)
            max_rows(0, 0, 0)
            with sp.Fori(0, (NGT - 4) // 3) as it:
                for r in range(3):
                    body(it * 3 + r, r)
            for g in range((NGT - 4) // 3 * 3, NGT):
                body(g, g % 3, g < NGT - 1, g < NGT - 2)
            for h in range(2):
                sp.wait_ge(o_out[h], 16 * NGT + 16)

        @block.gpsimd
        def _(pool):
            pool.sem_inc(neg_split, 8)
            for i in range(3):
                nc.gpsimd.memset(ks[i][SROWS:MROWS], 1.0).then_inc(ones_set, 1)
                pool.wait_ge(ones_set, 2 * i + 1)
                nc.gpsimd.memset(vg[i][:, :, :, HD:], 1.0).then_inc(ones_set, 1)
                pool.wait_ge(ones_set, 2 * i + 2)

            def v_of(g, r):
                pool.wait_ge(pv_done, g * STEPS + 2)
                by_itself(pool, pool_waited)
                nc.gpsimd.tensor_copy(vg[r][:, :, :, 0:HD], vT[:, bass.ds(g, 1), :, :]
                                      .rearrange("p a k (j i) -> p (a k) j i", i=HD)).then_inc(v_set, 1)

            def split(g, h):
                n = g * 8 + 4 * h + 8
                pool.wait_ge(neg_ready, g * 2 + h + 1)
                pool.wait_ge(max_rows_in[h], g * 48 + 16)
                by_itself(pool, pool_waited)
                nc.gpsimd.tensor_copy(neg_parts[:, h, 0], neg_max[:, h]).then_inc(neg_split, 1)
                pool.wait_ge(neg_split, n + 1)
                nc.gpsimd.tensor_tensor(neg_rest[:, h], neg_max[:, h], neg_parts[:, h, 0], ALU.subtract)\
                    .then_inc(neg_split, 1)
                pool.wait_ge(neg_split, n + 2)
                by_itself(pool, pool_waited)
                nc.gpsimd.tensor_copy(neg_parts[:, h, 1], neg_rest[:, h]).then_inc(neg_split, 1)
                pool.wait_ge(neg_split, n + 3)
                nc.gpsimd.tensor_tensor(neg_parts[:, h, 2], neg_rest[:, h], neg_parts[:, h, 1], ALU.subtract)\
                    .then_inc(neg_split, 1)

            def body(g, r, it, with_next):
                split(g, 1)
                if with_next:
                    v_of(g + 1, (r + 1) % 3)
                    split(g + 1, 0)

            pool.wait_ge(ones_set, 6)
            v_of(0, 0)
            split(0, 0)
            groups(pool, body)

        @block.tensor
        def _(pe):
            pe.sem_inc(scores_ready, 1)
            pe.sem_inc(pv_done, 3 * STEPS)
            pe.wait_ge(ident_in, 16)
            pe.wait_ge(ones_set, 6)

            def for_max(g, r, a):
                half, j, qt, kh = a // HU, a % HU // 8, a % 8 // 2, a % 2
                pe.wait_ge(reduced, g * UNITS + a + 1)
                nc.tensor.matmul(max_bank[a % 2][:], qs[r][0:SROWS, half, j, qt * P:(qt + 1) * P],
                                 ks[r][0:SROWS, j, kh * TW:(kh + 1) * TW], start=True, stop=True)\
                    .then_inc(max_ready, 1)

            def turn(g, h, a):
                pe.wait_ge(row_max_ready, g * 2 + h + 1)
                nc.tensor.transpose(max_bank[0][0:HU // 2, 0:P], row_max[:, h], ident[:]).then_inc(turned, 1)

            def body(g, r, it, with_next):
                for s in range(STEPS):
                    qh, kt = s // QT, s % QT
                    if kt == 0:
                        pe.wait_ge(max_rows_in[qh], g * 48 + 64)
                    if s == 0 and with_next:
                        pe.wait_ge(stack_in[(r + 1) % 3], it * LOAD + LOAD * (1 + (r + 1) // 3))
                    if s == 2:
                        if with_next:
                            pe.wait_ge(reduced, g * UNITS + UNITS + 4 * s + 1)
                        turn(g, 1, 0)
                    if s == 10 and with_next:
                        pe.wait_ge(reduced, g * UNITS + UNITS + 4 * s + 1)
                        turn(g + 1, 0, 0)
                    for pair in range(2):
                        pe.wait_ge(probs_ready, g * 2 * STEPS + 2 * s + pair + 1)
                        for i in range(2):
                            j = 2 * pair + i
                            mm = nc.tensor.matmul(score_bank[pair][:, i], ks[r][0:MROWS, j, kt * P:(kt + 1) * P],
                                                  qs[r][0:MROWS, qh, j, :], start=True, stop=True)
                        mm.then_inc(scores_ready, 1)
                        if with_next:
                            for i in range(2):
                                if s in (2, 10) and pair == 0 and i == 0:
                                    pe.wait_ge(neg_ready, g * 2 + (2 if s == 2 else 3))
                                for_max(g + 1, (r + 1) % 3, 4 * s + 2 * pair + i)
                    if s > 0:
                        pv(g, r, s - 1)
                pv(g, r, STEPS - 1)

            def pv(g, r, s):
                qh, kt = s // QT, s % QT
                if s == 0:
                    pe.wait_ge(v_set, g + 1)
                if kt == 0:
                    pe.wait_ge(o_kept, g * 2 + qh + 1)
                pe.wait_ge(probs_ready, g * 2 * STEPS + 2 * s + 4)
                for j in range(G):
                    mm = nc.tensor.matmul(o_bank[qh][32 * j:32 * j + 32, :], vg[r][:, kt, j], probs[:, s % 2, j],
                                          start=(kt == 0), stop=(kt == QT - 1))
                mm.then_inc(pv_done, 1)

            pe.wait_ge(stack_in[0], LOAD)
            for a in range(UNITS):
                if a == HU + 8:
                    pe.wait_ge(reduced, a + 1)
                    turn(0, 0, 0)
                    pe.wait_ge(neg_ready, 1)
                for_max(0, 0, a)
            groups(pe, body)

        @block.scalar
        def _(act):
            act.sem_inc(probs_ready, 2)

            def body(g, r, it, with_next):
                for s in range(STEPS):
                    act.wait_ge(pv_done, g * STEPS + (3 * STEPS + s - 1))
                    for pair in range(2):
                        act.wait_ge(scores_ready, g * 2 * STEPS + 2 * s + pair + 2)
                        nc.scalar.activation(probs[:, s % 2, 2 * pair:2 * pair + 2], score_bank[pair][:], ACT.Exp,
                                             scale=SOFTMAX_SCALE).then_inc(probs_ready, 1)

            groups(act, body)

        @block.vector
        def _(dve):
            dve.sem_inc(reduced, 2)
            dve.sem_inc(o_kept, 2)

            def maximum(g, a):
                dve.wait_ge(max_ready, g * UNITS + a + 1)
                nc.vector.tensor_reduce(mx[:, a // HU, a % HU:a % HU + 1], max_bank[a % 2][:], AX_X, ALU.max)\
                    .then_inc(reduced, 1)

            def both_halves(g, h):
                dve.wait_ge(reduced, g * UNITS + (h + 1) * HU + 2)
                nc.vector.tensor_reduce(row_max[:, h], mx[:, h].rearrange("p (u k) -> p u k", k=2), AX_X, ALU.max)\
                    .then_inc(row_max_ready, 1)

            def negate(g, h):
                dve.wait_ge(turned, g * 2 + h + 1)
                dve.wait_ge(neg_split, g * 8 + 4 * h + 4)
                nc.vector.tensor_scalar(neg_max[:, h], max_bank[0][0:HU // 2, 0:P], -1.0, None, ALU.mult)\
                    .then_inc(neg_ready, 1)

            def keep_o(g, qh):
                dve.wait_ge(pv_done, g * STEPS + (3 * STEPS + (qh + 1) * QT))
                dve.wait_ge(o_out[qh], g * 16 + 16)
                nc.vector.tensor_copy(o_sb[:, qh], o_bank[qh][:]).then_inc(o_kept, 1)

            def body(g, r, it, with_next):
                for s in range(STEPS):
                    if s == 2:
                        negate(g, 1)
                    if s == 10 and with_next:
                        negate(g + 1, 0)
                    if with_next:
                        for i in range(4):
                            maximum(g + 1, 4 * s + i)
                    if s == 7 and with_next:
                        both_halves(g + 1, 0)
                    if s == 9:
                        keep_o(g, 0)
                if with_next:
                    both_halves(g + 1, 1)
                keep_o(g, 1)

            for a in range(UNITS):
                if a == HU:
                    both_halves(0, 0)
                if a == HU + 8:
                    negate(0, 0)
                maximum(0, a)
            both_halves(0, 1)
            groups(dve, body)


class Norm:

    def __init__(self, m, xT, xn_at, tag):
        self.xT, self.xn_at = xT, xn_at
        self.mean_w, self.eps_col = m.sb("mean_w" + tag, [P, P]), m.sb("eps_col" + tag, [P, 1])
        self.xc, self.sq = m.sb("xc" + tag, [P, DC, TW]), m.sb("sq" + tag, [P, DC, TW])
        self.rs = m.sb("rs" + tag, [P, 3, TW])
        self.mean_bank, self.var_bank = m.bank("mean_bank" + tag), m.bank("var_bank" + tag)
        self.set, self.mean_ready, self.centred, self.squared, self.var_ready, self.guessed, self.stepped, self.normed = (
            m.sem(n + tag) for n in ("norm_set", "mean_ready", "centred", "squared", "var_ready", "guessed",
                                     "stepped", "normed"))

    def tile(self, c, t):
        return self.xT[:, c, bass.ds(t * TW, TW)]

    def start_pool(self, nc):
        nc.gpsimd.memset(self.mean_w[:], 1.0 / D).then_inc(self.set, 1)
        nc.gpsimd.memset(self.eps_col[:], EPS).then_inc(self.set, 1)

    def start_pe(self, nc, pe):
        pe.sem_inc(self.var_ready, 1)
        pe.wait_ge(self.set, 2)

    def start_dve(self, nc, dve):
        dve.sem_inc(self.centred, DC)
        dve.sem_inc(self.stepped, 1)
        dve.sem_inc(self.normed, DC)

    def start_act(self, nc, act):
        act.wait_ge(self.set, 2)

    def mean(self, nc, pe, t):
        pe.wait_ge(self.centred, t * DC + DC)
        for c in range(DC):
            mm = nc.tensor.matmul(self.mean_bank[:], self.mean_w[:], self.tile(c, t), start=(c == 0), stop=(c == DC - 1))
        mm.then_inc(self.mean_ready, 1)

    def centre(self, nc, dve, t):
        dve.wait_ge(self.mean_ready, t + 1)
        dve.wait_ge(self.normed, t * DC + DC)
        for c in range(DC):
            nc.vector.tensor_tensor(self.xc[:, c], self.tile(c, t), self.mean_bank[:], ALU.subtract)\
                .then_inc(self.centred, 1)

    def square(self, nc, act, t):
        act.wait_ge(self.var_ready, t + 1)
        for c in range(DC):
            act.wait_ge(self.centred, t * DC + DC + c + 1)
            nc.scalar.activation(self.sq[:, c], self.xc[:, c], ACT.Square).then_inc(self.squared, 1)

    def var(self, nc, pe, t):
        pe.wait_ge(self.squared, t * DC + DC)
        pe.wait_ge(self.stepped, t * 3 + 1)
        for c in range(DC):
            mm = nc.tensor.matmul(self.var_bank[:], self.mean_w[:], self.sq[:, c], start=(c == 0), stop=(c == DC - 1))
        mm.then_inc(self.var_ready, 1)

    def guess(self, nc, act, t):
        act.wait_ge(self.var_ready, t + 2)
        act.wait_ge(self.stepped, t * 3 + 1)
        nc.scalar.activation(self.rs[:, 1], self.var_bank[:], ACT.Ln, bias=self.eps_col[:]).then_inc(self.guessed, 1)
        act.wait_ge(self.guessed, t * 2 + 1)
        nc.scalar.activation(self.rs[:, 0], self.rs[:, 1], ACT.Exp, scale=-0.5).then_inc(self.guessed, 1)

    def finish(self, nc, dve, t, xn_at=None):
        rs = self.rs
        dve.wait_ge(self.guessed, t * 2 + 2)
        nc.vector.scalar_tensor_tensor(rs[:, 1], self.var_bank[:], EPS, rs[:, 0], ALU.add, ALU.mult)\
            .then_inc(self.stepped, 1)
        dve.wait_ge(self.stepped, t * 3 + 2)
        nc.vector.scalar_tensor_tensor(rs[:, 2], rs[:, 1], -0.5, rs[:, 0], ALU.mult, ALU.mult)\
            .then_inc(self.stepped, 1)
        dve.wait_ge(self.stepped, t * 3 + 3)
        nc.vector.scalar_tensor_tensor(rs[:, 1], rs[:, 2], 1.5, rs[:, 0], ALU.add, ALU.mult).then_inc(self.stepped, 1)
        dve.wait_ge(self.stepped, t * 3 + 4)
        for c in range(DC):
            nc.vector.tensor_tensor((xn_at or self.xn_at)(c, t), self.xc[:, c], rs[:, 1], ALU.mult).then_inc(self.normed, 1)


def merge_heads(nc, io, xT, o_scr, recip_scr):
    with ExitStack() as ctx:
        m = Mem(nc, ctx)
        wo = m.sb("wo", [P, DC, D])
        bo = m.sb("bo", [P, DC])
        head_of = m.sb("head_of", [H, D])
        sums = m.sb("sums", [P, TW])
        recips = m.sb("recips", [P, TW])
        by_head = m.sb("by_head", [H, B, S])
        o_in = m.sb("o_in", [P, 2, DC, TW])
        o_n = m.sb("o_n", [P, 2, DC, TW])
        recip_bank = [m.bank(f"recip_bank{c}") for c in range(DC)]
        out_bank = [m.bank(f"out_bank{c}") for c in range(DC)]
        consts_in, sums_in, recips_out, by_head_in = (m.sem(n) for n in ("mh_consts", "sums_in", "recips_out", "by_head_in"))
        heads_in = [m.sem(f"heads_in{i}") for i in range(2)]
        recips_ready, spread, divided, out_ready, x_new = (m.sem(n) for n in ("recips_ready", "spread", "divided", "out_ready", "mh_x_new"))
        by_rows = o_scr.rearrange("g (j r) t -> (g j) r t", r=2 * HD)
        pe_waited = m.sem("pe_waited_merge_heads")
        block = ctx.enter_context(nc.Block())

        @block.sync
        def _(sp):
            sp.dma_start(sums[:], by_rows[:, HD, :].rearrange("g (h t) -> g h t", t=TW)).then_inc(sums_in, 16)
            for dst, src in ((wo[:], io["Wo"].rearrange("(c p) n -> p c n", p=P)), (bo[:], io["bo"]), (head_of[:], io["head_of"])):
                sp.dma_start(dst, src).then_inc(consts_in, 16)

            def load(b, half):
                for c in range(DC):
                    sp.dma_start(o_in[:, half, c, :],
                                 by_rows[bass.ds(b * H + c * (H // DC), H // DC), 0:HD, half * TW:(half + 1) * TW])\
                        .then_inc(heads_in[half], 16)

            load(0, 0)
            load(0, 1)
            sp.wait_ge(recips_ready, 1)
            sp.dma_start(recip_scr.rearrange("g (h t) -> (g h) t", t=TW), recips[:]).then_inc(recips_out, 16)
            sp.wait_ge(recips_out, 16)
            sp.dma_start(by_head[:], recip_scr.rearrange("(b h) t -> h b t", h=H)).then_inc(by_head_in, 16)
            with sp.Fori(1, B) as b:
                for half in range(2):
                    sp.wait_ge(divided, b * 2 * DC + half * DC)
                    load(b, half)

        @block.tensor
        def _(pe):
            pe.wait_ge(consts_in, 48)
            pe.wait_ge(by_head_in, 16)

            def tile(b, half):
                t = b * 2 + half
                for c in range(DC):
                    pe.wait_ge(divided, t * DC + c + 1)
                    by_itself(pe, pe_waited)
                    nc.tensor.matmul(recip_bank[c][:], head_of[:, c * P:(c + 1) * P],
                                     by_head[:, bass.ds(b, 1), half * TW:(half + 1) * TW].rearrange("h a t -> h (a t)"),
                                     start=True, stop=True).then_inc(spread, 1)
                pe.wait_ge(divided, t * DC + 2 * DC)
                for c in range(DC):
                    pe.wait_ge(x_new, t * DC + c + 1)
                    for k in range(DC):
                        mm = nc.tensor.matmul(out_bank[c][:], wo[:, k, c * P:(c + 1) * P], o_n[:, half, k],
                                              start=(k == 0), stop=(k == DC - 1))
                    mm.then_inc(out_ready, 1)

            with pe.Fori(0, B) as b:
                tile(b, 0)
                tile(b, 1)

        @block.vector
        def _(dve):
            dve.sem_inc(divided, DC)
            dve.sem_inc(x_new, DC)
            dve.wait_ge(sums_in, 16)
            nc.vector.reciprocal(recips[:], sums[:]).then_inc(recips_ready, 1)

            def tile(b, half):
                t = b * 2 + half
                for c in range(DC):
                    dve.wait_ge(spread, t * DC + c + 1)
                    dve.wait_ge(heads_in[half], b * 32 + 32)
                    nc.vector.tensor_tensor(o_n[:, half, c], o_in[:, half, c], recip_bank[c][:], ALU.mult)\
                        .then_inc(divided, 1)
                for c in range(DC):
                    dve.wait_ge(out_ready, t * DC + c + 1)
                    x = xT[:, c, bass.ds(t * TW, TW)]
                    nc.vector.scalar_tensor_tensor(x, out_bank[c][:], bo[:, c:c + 1], x, ALU.add, ALU.add)\
                        .then_inc(x_new, 1)

            with dve.Fori(0, B) as b:
                tile(b, 0)
                tile(b, 1)


def feed_forward(nc, io, xT, tag):
    BANKS = 4
    with ExitStack() as ctx:
        m = Mem(nc, ctx)
        wfc = m.sb("wfc" + tag, [P, DC, FF])
        wpr = m.sb("wpr" + tag, [P, FC, D])
        xn = m.sb("xn" + tag, [P, DC, T])
        relu = m.sb("relu" + tag, [P, 2, TW])
        hid = m.sb("hid" + tag, [P, FC, TW])
        count = m.sb("count" + tag, [P, DC, TW])
        norm = Norm(m, xT, lambda c, t: xn[:, c, bass.ds(t * TW, TW)], tag)
        hid_bank = [m.bank(f"hid_bank{i}" + tag) for i in range(BANKS)]
        y_bank = [m.bank(f"y_bank{c}" + tag) for c in range(DC)]
        weights_in, hid_ready, relu_ready, hid_kept, y_ready, fired, x_new = (
            m.sem(n + tag) for n in ("weights_in", "hid_ready", "relu_ready", "hid_kept", "y_ready", "fired", "x_new"))
        block = ctx.enter_context(nc.Block())

        @block.sync
        def _(sp):
            sp.dma_start(wfc[:], io["W_fcT"].rearrange("(c p) f -> p c f", p=P)).then_inc(weights_in, 16)
            sp.dma_start(wpr[:], io["W_projT"].rearrange("(f p) d -> p f d", p=P)).then_inc(weights_in, 16)

        @block.gpsimd
        def _(pool):
            norm.start_pool(nc)

        @block.tensor
        def _(pe):
            norm.start_pe(nc, pe)
            norm.mean(nc, pe, 0)
            norm.var(nc, pe, 0)
            pe.wait_ge(weights_in, 32)

            def out(t, f):
                pe.wait_ge(hid_kept, t * FC + f + 1 + BANKS)
                for c in range(DC):
                    if f == 0:
                        pe.wait_ge(x_new, t * DC + c + 1)
                    mm = nc.tensor.matmul(y_bank[c][:], wpr[:, f, c * P:(c + 1) * P], hid[:, f],
                                          start=(f == 0), stop=(f == FC - 1))
                    if f == FC - 1:
                        mm.then_inc(y_ready, 1)

            def tile(t, with_next):
                pe.wait_ge(norm.normed, t * DC + 2 * DC)
                for f in range(FC):
                    pe.wait_ge(hid_kept, t * FC + f + 1)
                    for c in range(DC):
                        mm = nc.tensor.matmul(hid_bank[f % BANKS][:], wfc[:, c, f * P:(f + 1) * P],
                                              xn[:, c, bass.ds(t * TW, TW)], start=(c == 0), stop=(c == DC - 1))
                    mm.then_inc(hid_ready, 1)
                    if f == 2 and with_next:
                        norm.mean(nc, pe, t + 1)
                    if f == 5 and with_next:
                        norm.var(nc, pe, t + 1)
                    if f >= 3:
                        out(t, f - 3)
                for f in range(FC - 3, FC):
                    out(t, f)

            with pe.Fori(0, NT - 1) as t:
                tile(t, True)
            tile(NT - 1, False)

        @block.scalar
        def _(act):
            norm.start_act(nc, act)
            norm.square(nc, act, 0)
            norm.guess(nc, act, 0)

            def tile(t, with_next):
                for f in range(FC):
                    act.wait_ge(hid_ready, t * FC + f + 1)
                    act.wait_ge(hid_kept, t * FC + f + BANKS - 1)
                    nc.scalar.activation(relu[:, f % 2], hid_bank[f % BANKS][:], ACT.Relu).then_inc(relu_ready, 1)
                    if f == 3 and with_next:
                        norm.square(nc, act, t + 1)
                    if f == 6 and with_next:
                        norm.guess(nc, act, t + 1)

            with act.Fori(0, NT - 1) as t:
                tile(t, True)
            tile(NT - 1, False)

        @block.vector
        def _(dve):
            norm.start_dve(nc, dve)
            dve.sem_inc(hid_kept, BANKS)
            dve.sem_inc(x_new, DC)
            norm.centre(nc, dve, 0)
            norm.finish(nc, dve, 0)

            def tile(t, with_next):
                for f in range(FC):
                    dve.wait_ge(relu_ready, t * FC + f + 1)
                    nc.vector.scalar_tensor_tensor(hid[:, f], hid_bank[f % BANKS][:], 0.0, relu[:, f % 2],
                                                   ALU.max, ALU.mult).then_inc(hid_kept, 1)
                    if f == 2 and with_next:
                        norm.centre(nc, dve, t + 1)
                if with_next:
                    norm.finish(nc, dve, t + 1)
                n = t * DC * LIF_STEPS
                for k in range(LIF_STEPS):
                    for c in range(DC):
                        if k == 0:
                            dve.wait_ge(y_ready, t * DC + c + 1)
                            nc.vector.tensor_scalar(count[:, c], y_bank[c][:], THETA[0], None, ALU.is_gt)\
                                .then_inc(fired, 1)
                        else:
                            dve.wait_ge(fired, n + DC * (k - 1) + c + 1)
                            nc.vector.scalar_tensor_tensor(count[:, c], y_bank[c][:], THETA[k], count[:, c],
                                                           ALU.is_gt, ALU.add).then_inc(fired, 1)
                for c in range(DC):
                    dve.wait_ge(fired, n + DC * (LIF_STEPS - 1) + c + 1)
                    x = xT[:, c, bass.ds(t * TW, TW)]
                    nc.vector.scalar_tensor_tensor(x, count[:, c], 1.0 / LIF_STEPS, x, ALU.mult, ALU.add)\
                        .then_inc(x_new, 1)

            with dve.Fori(0, NT - 1) as t:
                tile(t, True)
            tile(NT - 1, False)


def emit(nc, io, xT, out):
    with ExitStack() as ctx:
        m = Mem(nc, ctx)
        ident = m.sb("ident_e", [P, P])
        x_out = m.sb("x_out", [P, 2, TW // P, D])
        bank = [m.bank(f"emit_bank{i}") for i in range(8)]
        stage = m.sb("stage", [P, 2, DC, TW])
        ident_in, turned, kept, staged = m.sem("ident_in_e"), m.sem("turned_e"), m.sem("kept_e"), m.sem("staged")
        sent = [m.sem(f"sent{i}") for i in range(2)]
        out_tiles = out.rearrange("b (i j p) d -> (b i) p j d", j=TW // P, p=P)
        pool_waited = m.sem("pool_waited_emit")
        block = ctx.enter_context(nc.Block())

        @block.sync
        def _(sp):
            for i in range(2):
                sp.sem_inc(sent[i], 16)
            sp.dma_start(ident[:], io["ident"]).then_inc(ident_in, 16)
            with sp.Fori(0, B) as b:
                for half in range(2):
                    sp.wait_ge(kept, b * 8 + half * 4 + 4 + 8)
                    sp.dma_start(out_tiles[bass.ds(b * 2 + half, 1)].rearrange("a p j d -> (a p) j d"), x_out[:, half])\
                        .then_inc(sent[half], 16)
            for i in range(2):
                sp.wait_ge(sent[i], 16 * B + 16)

        @block.tensor
        def _(pe):
            pe.wait_ge(ident_in, 16)
            with pe.Fori(0, B) as b:
                for half in range(2):
                    for j in range(TW // P):
                        pe.wait_ge(kept, b * 8 + half * 4 + j + 1)
                        if j == 0:
                            pe.wait_ge(staged, b * 2 + half + 1 + 2)
                        for c in range(DC):
                            mm = nc.tensor.transpose(bank[half * 4 + j][:, c * P:(c + 1) * P],
                                                     stage[:, half, c, j * P:(j + 1) * P], ident[:])
                        mm.then_inc(turned, 1)

        @block.gpsimd
        def _(pool):
            pool.sem_inc(staged, 2)
            with pool.Fori(0, B) as b:
                for half in range(2):
                    pool.wait_ge(kept, b * 8 + half * 4 + 4)
                    by_itself(pool, pool_waited)
                    nc.gpsimd.tensor_copy(stage[:, half], xT[:, :, bass.ds(b * S + half * TW, TW)]).then_inc(staged, 1)

        @block.scalar
        def _(act):
            act.sem_inc(kept, 8)
            with act.Fori(0, B) as b:
                for half in range(2):
                    act.wait_ge(sent[half], b * 16 + 16)
                    for j in range(TW // P):
                        act.wait_ge(turned, b * 8 + half * 4 + j + 1)
                        nc.scalar.activation(x_out[:, half, j], bank[half * 4 + j][:, 0:D], ACT.Copy).then_inc(kept, 1)


def scan(nc, io, xT, bc_scr):
    NU = NS * DC
    BANKED = 14
    BC = 4
    WR = 4
    AR = 2
    with ExitStack() as ctx:
        m = Mem(nc, ctx)
        wx, wz, wout = m.sb("wx", [P, DC, D]), m.sb("wz", [P, DC, D]), m.sb("wout", [P, DC, D])
        wpar = m.sb("wpar", [P, DC, R + 2 * NS])
        wdt = m.sb("wdt", [R, D])
        conv_w, b_dt, d_par = m.sb("conv_w", [P, DC, TAPS]), m.sb("b_dt", [P, DC]), m.sb("d_par", [P, DC])
        ident = m.sb("ident_s", [P, P])
        ones = m.sb("ones_s", [P, P])
        decay = m.sb("decay", [P, 6, DC, NS])
        neg_a, a_col, is_small, not_small, a_den, a_rec = (decay[:, i] for i in range(6))
        small_any = m.sb("small_any", [P, 1])
        small_int = m.sb("small_int", [1, 1], I32)
        xn = m.sb("xn_s", [P, DC, S])
        par = m.sb("par", [R + 2 * NS, 2, TW])
        log_part, exp_part = m.sb("log_part", [P, TW]), m.sb("exp_part", [P, TW])
        xr = m.sb("xr", [P, DC, TAPS - 1 + S])
        cv = m.sb("cv", [P, S])
        dt, u, sz = (m.sb(n, [P, 2, DC, S]) for n in ("dt", "u", "sz"))
        bc = m.sb("bc", [P, BC, 2, S])
        a_t = m.sb("a_t", [P, AR, S])
        w_in = m.sb("w_in", [P, WR, S])
        h_out = m.sb("h_out", [P, WR, S])
        norm = Norm(m, xT, None, "_s")
        work = [m.bank(f"work{i}") for i in range(2)]
        y_bank = [m.bank(f"ys_bank{i}") for i in range(2 * DC)]

        (consts_in, exp_a, decay_set, small_summed, zeros_set, prep_made, prep_used, par_out, soft_act, soft_dve,
         conv_step, silu_u, decays, inputs, scaled, scanned, weighted, summed, gated, out_made, x_new) = (
            m.sem(n + "_s") for n in (
                "consts_in", "exp_a", "decay_set", "small_summed", "zeros_set", "prep_made", "prep_used", "par_out",
                "soft_act", "soft_dve", "conv_step", "silu_u", "decays", "inputs", "scaled", "scanned", "weighted",
                "summed", "gated", "out_made", "x_new"))
        bc_in = [m.sem(f"bc_in{i}") for i in range(BC)]
        loads = [(w[:], io[n].rearrange("(c p) n -> p c n", p=P)) for w, n in
                 ((wx, "W_xT"), (wz, "W_zT"), (wout, "W_outT"), (wpar, "W_paramsT"), (conv_w, "conv"), (neg_a, "A_log"))]
        loads += [(wdt[:], io["W_dtT"]), (b_dt[:], io["b_dt"]), (d_par[:], io["D_param"]), (ident[:], io["ident"])]
        CONSTS = 16 * len(loads)
        pool_waited = m.sem("pool_waited_scan")
        act_waited = m.sem("act_waited_scan")
        dve_waited = m.sem("dve_waited_scan")
        block = ctx.enter_context(nc.Block())

        DT, XR, Z = 2, 6, 10
        norm_slot = (0, 5)
        made_slot = [6, 11, 13, 15, 17, 19] + list(range(20, 28))
        pieces = []
        for h in range(2):
            s = norm_slot[h]
            pieces += [(s, "pe", "mean", h), (s + 1, "dve", "centre", h), (s + 2, "act", "square", h),
                       (s + 3, "pe", "var", h), (s + 4, "act", "guess", h), (s + 5, "dve", "finish", h)]
        for i in range(BANKED):
            pieces += [(made_slot[i], "pe", "make", i), (made_slot[i] + 1, "act", "use", i)]
            if DT <= i < XR:
                pieces.append((made_slot[i] + 2, "dve", "soft", i - DT))
        pieces += [(23, "dve", "conv", 0), (25, "act", "silu", 0), (26, "dve", "conv", 1), (28, "act", "silu", 1)]
        pieces.sort(key=lambda piece: piece[0])

        def prepare(engine, run, b, slot=None):
            for s, e, name, arg in pieces:
                if e == engine and (slot is None or s == slot):
                    run[name](b, arg)

        def batches(eng, body):
            with eng.Fori(0, B - 1) as b:
                body(b, True)
            body(B - 1, False)

        def turn(b):
            return bass.ds(b % 2, 1)

        @block.sync
        def _(sp):
            sp.sem_inc(par_out, 16)
            for dst, src in loads:
                sp.dma_start(dst, src).then_inc(consts_in, 16)

            def bc_out(b):
                sp.wait_ge(prep_used, b * BANKED + 4)
                sp.dma_start(bc_scr[bass.ds(b, 1)].rearrange("a n t -> (a n) t"),
                             par[R:R + 2 * NS].rearrange("p h t -> p (h t)")).then_inc(par_out, 16)

            def body(b, with_next):
                sp.wait_ge(par_out, b * 16 + 32)
                for n in range(NS):
                    sp.wait_ge(weighted, b * NU + 2 * n + 2)
                    src = bc_scr[bass.ds(b, 1)].rearrange("a (g n) t -> a n g t", n=NS)[:, n]
                    sp.dma_start(bc[:, n % BC], src.rearrange("a g t -> (a g) t").partition_broadcast(P))\
                        .then_inc(bc_in[n % BC], 16)
                    if n == 9 and with_next:
                        bc_out(b + 1)

            bc_out(0)
            batches(sp, body)

        @block.gpsimd
        def _(pool):
            norm.start_pool(nc)
            nc.gpsimd.memset(xr[:, :, 0:TAPS - 1], 0.0).then_inc(zeros_set, 1)
            nc.gpsimd.memset(ones[:], 1.0).then_inc(zeros_set, 1)

            def body(b, with_next):
                for k in range(NU):
                    n, f = k // DC, k % DC
                    pool.wait_ge(bc_in[n % BC], b * (NS // BC * 16) + (n // BC * 16 + 16))
                    if k < DC:
                        pool.wait_ge(silu_u, b * DC + k + 2)
                    pool.wait_ge(scanned, b * NU + k + 1)
                    by_itself(pool, pool_waited)
                    nc.gpsimd.tensor_tensor(w_in[:, k % WR], u[:, turn(b), f].rearrange("p a t -> p (a t)"),
                                            bc[:, n % BC, 0], ALU.mult).then_inc(inputs, 1)

            batches(pool, body)

        @block.tensor
        def _(pe):
            norm.start_pe(nc, pe)
            pe.sem_inc(prep_made, 1)
            pe.sem_inc(summed, WR)
            pe.wait_ge(consts_in, CONSTS)
            pe.wait_ge(zeros_set, 2)
            pe.wait_ge(decay_set, 8)
            nc.tensor.matmul(work[0][0:1, 0:1], small_any[:], ones[:, 0:1], start=True, stop=True)\
                .then_inc(small_summed, 1)

            def make(b, i):
                pe.wait_ge(prep_used, b * BANKED + i + 1)
                if i < 2:
                    pe.wait_ge(x_new, b * 4 + 4)
                    pe.wait_ge(norm.normed, b * 2 * DC + (i + 2) * DC)
                if DT <= i < XR:
                    f, h = (i - DT) // 2, (i - DT) % 2
                    pe.wait_ge(prep_used, b * BANKED + 4)
                    mm = nc.tensor.matmul(work[i % 2][:], wdt[:, f * P:(f + 1) * P], par[0:R, h], start=True, stop=True)
                else:
                    if i < DT:
                        h, out, w = i, work[i % 2][0:R + 2 * NS], wpar[:]
                    else:
                        f, h = (i - XR) % 4 // 2, (i - XR) % 2
                        out, w = work[i % 2][:], (wx if i < Z else wz)[:, :, f * P:(f + 1) * P]
                    for c in range(DC):
                        mm = nc.tensor.matmul(out, w[:, c], xn[:, c, h * TW:(h + 1) * TW],
                                              start=(c == 0), stop=(c == DC - 1))
                mm.then_inc(prep_made, 1)

            run = {"mean": lambda b, h: norm.mean(nc, pe, b * 2 + h), "var": lambda b, h: norm.var(nc, pe, b * 2 + h),
                   "make": make}

            def unit(b, k):
                f = k % DC
                if k < DC:
                    pe.wait_ge(gated, b * 8 + 4)
                pe.wait_ge(weighted, b * NU + k + 9)
                for h in range(2):
                    mm = nc.tensor.matmul(y_bank[2 * f + h][:], ident[:], h_out[:, k % WR, h * TW:(h + 1) * TW],
                                          start=(k < DC), stop=(k >= NU - DC))
                mm.then_inc(summed, 1)

            def body(b, with_next):
                for k in range(NU):
                    if k:
                        unit(b, k - 1)
                    if with_next:
                        prepare("pe", run, b + 1, k)
                unit(b, NU - 1)
                pe.wait_ge(gated, b * 8 + 16)
                for q in range(4):
                    c, h = q // 2, q % 2
                    pe.wait_ge(prep_used, (b * BANKED + 2 * BANKED + 2) if with_next else B * BANKED + 2)
                    pe.wait_ge(x_new, b * 4 + q + 7)
                    for f in range(DC):
                        mm = nc.tensor.matmul(work[q % 2][:], wout[:, f, c * P:(c + 1) * P],
                                              u[:, turn(b), f, h * TW:(h + 1) * TW].rearrange("p a t -> p (a t)"),
                                              start=(f == 0), stop=(f == DC - 1))
                    mm.then_inc(out_made, 1)

            prepare("pe", run, 0)
            batches(pe, body)

        @block.scalar
        def _(act):
            act.sem_inc(silu_u, 1)
            norm.start_act(nc, act)
            act.wait_ge(consts_in, CONSTS)
            nc.scalar.activation(a_den, neg_a, ACT.Exp).then_inc(exp_a, 1)
            act.wait_ge(decay_set, 9)
            act.sem_inc(prep_used, 2)

            def use(b, i):
                act.wait_ge(prep_made, b * BANKED + i + 2)
                bank = work[i % 2]
                if i < DT:
                    act.wait_ge(par_out, b * 16 + 16)
                    nc.scalar.activation(par[:, i], bank[0:R + 2 * NS], ACT.Copy).then_inc(prep_used, 1)
                elif i < XR:
                    f, h = (i - DT) // 2, (i - DT) % 2
                    out = dt[:, turn(b), f, h * TW:(h + 1) * TW].rearrange("p a t -> p (a t)")
                    n = b * 12 + 3 * (i - DT)
                    act.wait_ge(soft_dve, b * 16 + 4 * (i - DT) + 1)
                    by_itself(act, act_waited)
                    nc.scalar.activation(exp_part[:], bank[:], ACT.Abs, bias=b_dt[:, f:f + 1]).then_inc(soft_act, 1)
                    nc.scalar.activation(out, bank[:], ACT.Relu, bias=b_dt[:, f:f + 1]).then_inc(prep_used, 1)
                    act.wait_ge(soft_act, n + 1)
                    nc.scalar.activation(exp_part[:], exp_part[:], ACT.Exp, scale=-1.0).then_inc(soft_act, 1)
                    act.wait_ge(soft_act, n + 2)
                    nc.scalar.activation(log_part[:], exp_part[:], ACT.Ln, bias=ones[:, 0:1]).then_inc(soft_act, 1)
                elif i < Z:
                    f, h = (i - XR) // 2, (i - XR) % 2
                    act.wait_ge(conv_step, b * 8 + 1)
                    nc.scalar.activation(xr[:, f, TAPS - 1 + h * TW:TAPS - 1 + (h + 1) * TW], bank[:], ACT.Copy)\
                        .then_inc(prep_used, 1)
                else:
                    f, h = (i - Z) // 2, (i - Z) % 2
                    by_itself(act, act_waited)
                    nc.scalar.activation(sz[:, turn(b), f, h * TW:(h + 1) * TW].rearrange("p a t -> p (a t)"), bank[:],
                                         ACT.Silu).then_inc(prep_used, 1)

            def silu(b, f):
                act.wait_ge(conv_step, b * 8 + 4 * f + 5)
                by_itself(act, act_waited)
                nc.scalar.activation(u[:, turn(b), f].rearrange("p a t -> p (a t)"), cv[:], ACT.Silu).then_inc(silu_u, 1)

            run = {"square": lambda b, h: norm.square(nc, act, b * 2 + h),
                   "guess": lambda b, h: norm.guess(nc, act, b * 2 + h), "use": use, "silu": silu}

            def body(b, with_next):
                for k in range(NU):
                    n, f = k // DC, k % DC
                    if k == 0:
                        act.wait_ge(soft_dve, b * 16 + 17)
                    act.wait_ge(scanned, b * NU + k - AR + 1 + WR)
                    by_itself(act, act_waited)
                    nc.scalar.activation(a_t[:, k % AR], dt[:, turn(b), f].rearrange("p a t -> p (a t)"), ACT.Exp,
                                         scale=a_col[:, f, n:n + 1]).then_inc(decays, 1)
                    if with_next:
                        prepare("act", run, b + 1, k)

            act.wait_ge(zeros_set, 2)
            prepare("act", run, 0)
            batches(act, body)

        @block.vector
        def _(dve):
            norm.start_dve(nc, dve)
            dve.sem_inc(soft_dve, 1)
            dve.sem_inc(conv_step, 1)
            dve.sem_inc(scanned, WR)
            dve.sem_inc(weighted, 8)
            dve.sem_inc(gated, 8)
            dve.sem_inc(x_new, 8)
            dve.wait_ge(consts_in, CONSTS)
            dve.wait_ge(exp_a, 1)
            steps = [
                lambda: nc.vector.tensor_scalar(a_col, a_den, -1.0, None, ALU.mult),
                lambda: nc.vector.tensor_scalar(is_small, a_den, 1e-8, None, ALU.is_lt),
                lambda: nc.vector.tensor_scalar(not_small, is_small, -1.0, 1.0, ALU.mult, ALU.add),
                lambda: nc.vector.scalar_tensor_tensor(a_den, a_col, 1e-10, not_small, ALU.add, ALU.mult),
                lambda: nc.vector.tensor_tensor(a_den, a_den, is_small, ALU.add),
                lambda: nc.vector.reciprocal(a_rec, a_den),
                lambda: nc.vector.tensor_copy(neg_a, is_small),
                lambda: nc.vector.tensor_reduce(small_any[:], neg_a.rearrange("p c n -> p (c n)"), AX_X, ALU.add)]
            for n, step in enumerate(steps):
                if n:
                    dve.wait_ge(decay_set, n)
                step().then_inc(decay_set, 1)
            dve.wait_ge(small_summed, 1)
            nc.vector.tensor_copy(small_int[:], work[0][0:1, 0:1]).then_inc(decay_set, 1)
            dve.wait_ge(decay_set, len(steps) + 1)
            small = dve.value_load(small_int[:])

            def soft(b, i):
                f, h = i // 2, i % 2
                out = dt[:, turn(b), f, h * TW:(h + 1) * TW].rearrange("p a t -> p (a t)")
                n = b * 16 + 4 * i + 1
                dve.wait_ge(soft_act, b * 12 + 3 * i + 3)
                dve.wait_ge(prep_used, b * BANKED + DT + i + 3)
                nc.vector.tensor_tensor(out, out, log_part[:], ALU.add).then_inc(soft_dve, 1)
                dve.wait_ge(soft_dve, n + 1)
                nc.vector.tensor_scalar(log_part[:], exp_part[:], 1.0, 1.0, ALU.add, ALU.subtract).then_inc(soft_dve, 1)
                dve.wait_ge(soft_dve, n + 2)
                nc.vector.tensor_tensor(exp_part[:], exp_part[:], log_part[:], ALU.subtract).then_inc(soft_dve, 1)
                dve.wait_ge(soft_dve, n + 3)
                nc.vector.tensor_tensor(out, out, exp_part[:], ALU.add).then_inc(soft_dve, 1)

            def conv(b, f):
                dve.wait_ge(prep_used, b * BANKED + XR + 2 * f + 4)
                dve.wait_ge(silu_u, b * DC + f + 1)
                if f == 0:
                    dve.wait_ge(zeros_set, 2)
                for tap in range(TAPS):
                    w = conv_w[:, f, tap:tap + 1]
                    if tap == 0:
                        nc.vector.tensor_scalar(cv[:], xr[:, f, 0:S], w, None, ALU.mult).then_inc(conv_step, 1)
                        continue
                    dve.wait_ge(conv_step, b * 8 + 4 * f + tap + 1)
                    nc.vector.scalar_tensor_tensor(cv[:], xr[:, f, tap:tap + S], w, cv[:], ALU.mult, ALU.add)\
                        .then_inc(conv_step, 1)

            run = {"centre": lambda b, h: norm.centre(nc, dve, b * 2 + h), "soft": soft, "conv": conv}

            def finish(b, h):
                dve.wait_ge(prep_made, b * BANKED + 1)
                norm.finish(nc, dve, b * 2 + h, lambda c, t: xn[:, c, h * TW:(h + 1) * TW])

            run["finish"] = finish

            def weigh(b, k):
                n, f = k // DC, k % DC
                dve.wait_ge(scanned, b * NU + k + 1 + WR)
                nc.vector.scalar_tensor_tensor(h_out[:, k % WR], h_out[:, k % WR], a_rec[:, f, n:n + 1], bc[:, n % BC, 1],
                                               ALU.mult, ALU.mult).then_inc(weighted, 1)

            def body(b, with_next):
                for k in range(NU):
                    n, f = k // DC, k % DC
                    dve.wait_ge(decays, b * NU + k + 1)
                    dve.wait_ge(inputs, b * NU + k + 1)
                    dve.wait_ge(summed, b * NU + k + 1)
                    by_itself(dve, dve_waited)
                    with dve.If(small != 0):
                        nc.vector.scalar_tensor_tensor(h_out[:, k % WR], dt[:, turn(b), f].rearrange("p a t -> p (a t)"),
                                                       is_small[:, f, n:n + 1], w_in[:, k % WR], ALU.mult, ALU.mult)
                        dve.drain()
                        nc.vector.scalar_tensor_tensor(w_in[:, k % WR], a_t[:, k % AR], 1.0, w_in[:, k % WR],
                                                       ALU.subtract, ALU.mult)
                        dve.drain()
                        nc.vector.tensor_tensor(w_in[:, k % WR], w_in[:, k % WR], h_out[:, k % WR], ALU.add)\
                            .then_inc(scaled, 1)
                    with dve.Else():
                        nc.vector.scalar_tensor_tensor(w_in[:, k % WR], a_t[:, k % AR], 1.0, w_in[:, k % WR],
                                                       ALU.subtract, ALU.mult).then_inc(scaled, 1)
                    if k:
                        weigh(b, k - 1)
                    dve.wait_ge(scaled, b * NU + k + 1)
                    nc.vector.tensor_tensor_scan(h_out[:, k % WR], a_t[:, k % AR], w_in[:, k % WR], 0.0,
                                                 ALU.mult, ALU.add).then_inc(scanned, 1)
                    if with_next:
                        prepare("dve", run, b + 1, k)
                weigh(b, NU - 1)
                dve.wait_ge(summed, b * NU + NU + WR)
                parts = [(f, h) for f in range(DC) for h in range(2)]
                for f, h in parts:
                    y = u[:, turn(b), f, h * TW:(h + 1) * TW].rearrange("p a t -> p (a t)")
                    nc.vector.scalar_tensor_tensor(y, y, d_par[:, f:f + 1], y_bank[2 * f + h][:], ALU.mult, ALU.add)\
                        .then_inc(gated, 1)
                for i, (f, h) in enumerate(parts):
                    y = u[:, turn(b), f, h * TW:(h + 1) * TW].rearrange("p a t -> p (a t)")
                    z = sz[:, turn(b), f, h * TW:(h + 1) * TW].rearrange("p a t -> p (a t)")
                    dve.wait_ge(gated, b * 8 + i + 9)
                    nc.vector.tensor_tensor(y, y, z, ALU.mult).then_inc(gated, 1)
                for q in range(4):
                    c, h = q // 2, q % 2
                    dve.wait_ge(out_made, b * 4 + q + 1)
                    x = xT[:, c, bass.ds(b * S + h * TW, TW)]
                    nc.vector.tensor_tensor(x, work[q % 2][:], x, ALU.add).then_inc(x_new, 1)

            prepare("dve", run, 0)
            batches(dve, body)


def lay_out(v):
    a = {k: np.asarray(x) for k, x in v.items()}

    def pairs_swapped(w):
        return w.reshape(*w.shape[:-1], D // 2, 2)[..., ::-1].reshape(w.shape)

    def cols(w):
        return w.reshape(DC, P).T

    at, mb = (lambda n: a["L0_attn_a_" + n]), (lambda n: a["L0_attn_b_" + n])
    q = [cols(x) for x in (at("Wq_r_b"), pairs_swapped(at("Wq_r_b")), at("Wu_q_b"))]
    k = [cols(x) for x in (at("Wk_r_b"), pairs_swapped(at("Wk_r_b")), at("Wu_k_b"))]
    bcol = np.stack([at("Wd_q_b"), at("Wd_kv_b")] + [x[:, c] for side in (q, k) for c in range(DC) for x in side], 1)
    theta = np.float32(10000.0) ** (np.float32(-2.0) * np.arange(D // 2, dtype=np.float32)) / np.float32(D // 2)
    angle = np.arange(S, dtype=np.float32)[:, None] * theta.astype(np.float32)[None, :]
    cos, sin = np.cos(angle), np.sin(angle)
    out = {
        "x": at("x"), "ident": np.eye(P, dtype=np.float32),
        "cos": np.repeat(cos.T, 2, axis=0), "sin": np.stack([-sin.T, sin.T], 1).reshape(D, S),
        "Wd_q": at("Wd_q_w"), "Wd_kv": at("Wd_kv_w"), "Wu_q": at("Wu_q_w"), "Wq_r": at("Wq_r_w"),
        "Wq_r_swap": pairs_swapped(at("Wq_r_w")), "Wu_k": at("Wu_k_w"), "Wk_r": at("Wk_r_w"),
        "Wk_r_swap": pairs_swapped(at("Wk_r_w")), "Wu_v": at("Wu_v_w"),
        "bv": np.broadcast_to(at("Wu_v_b"), (P, D)), "bcol_attn": bcol,
        "Wo": at("Wo_w"), "bo": cols(at("Wo_b")),
        "head_of": np.repeat(np.eye(H, dtype=np.float32), HD, axis=1),
        "W_fcT": a["L0_ffn_W_fc"].T, "W_projT": a["L0_ffn_W_proj"].T,
        "W_xT": mb("W_x").T, "W_zT": mb("W_z").T, "W_paramsT": mb("W_params").T, "W_dtT": mb("W_dt").T,
        "W_outT": mb("W_out").T, "conv": mb("conv_w").reshape(D, TAPS), "b_dt": cols(mb("b_dt")),
        "D_param": cols(mb("D_param")), "A_log": mb("A_log"),
    }
    return {k: np.ascontiguousarray(x) for k, x in out.items()}


def program(nc, io, out):
    qk_parts = nc.dram_tensor("qk_parts", (B * 2 * DC, P, 3, S), BF16, kind="Internal").ap()
    o_scr = nc.dram_tensor("o_scr", (B * NG, P, S), F32, kind="Internal").ap()
    recip_scr = nc.dram_tensor("recip_scr", (B * H, S), F32, kind="Internal").ap()
    bc_scr = nc.dram_tensor("bc_scr", (B, 2 * NS, S), F32, kind="Internal").ap()
    with ExitStack() as ctx:
        xT = ctx.enter_context(nc.sbuf_tensor("xT", [P, DC, T], F32))
        with nc.sbuf_tensor("vT", [P, B * NG, QT, G * HD], F32) as vT:
            project(nc, io, xT, vT, qk_parts)
            attend(nc, io, vT, qk_parts, o_scr)
        merge_heads(nc, io, xT, o_scr, recip_scr)
        feed_forward(nc, io, xT, "_f1")
        scan(nc, io, xT, bc_scr)
        feed_forward(nc, io, xT, "_f2")
        emit(nc, io, xT, out)


def kernel(**inputs):
    import concourse.bacc as bacc
    from concourse.bass_utils import run_bass_kernel_spmd as run

    nc = bacc.Bacc("TRN2", target_bir_lowering=False, num_devices=1)
    arrays = {f"in_{name}_dram": a for name, a in lay_out(inputs).items()}
    io = {name[3:-5]: nc.dram_tensor(name, a.shape, mybir.dt.from_np(a.dtype), kind="ExternalInput").ap()
          for name, a in arrays.items()}
    out = nc.dram_tensor("out_0_dram", (B, S, D), F32, kind="ExternalOutput").ap()
    program(nc, io, out)
    return run(nc, [arrays], core_ids=[0]).results[0]["out_0_dram"]
```

```python
import numpy as np
from contextlib import ExitStack

import concourse.bass as bass
from concourse import mybir

F32 = mybir.dt.float32
BF16 = mybir.dt.bfloat16
I32 = mybir.dt.int32
ALU = mybir.AluOpType
ACT = mybir.ActivationFunctionType
AX_X = mybir.AxisListType.X

P = 128
B, S, D = 4, 1024, 256
T = B * S
TW = 512
NT = T // TW
TPB = S // TW
DC = D // P
H = 16
HD = D // H
LAT = 128
G = 4
NG = H // G
QT = S // P
FF = 4 * D
FC = FF // P
R = 64
NS = 16
TAPS = 4
EPS = 1e-5
SOFTMAX_SCALE = 1.0 / float(np.sqrt(np.float32(H + LAT + LAT)))
Q_PARTS = (0, 0, 1, 1, 0, 2)
K_PARTS = (0, 1, 0, 1, 2, 0)
SROWS = len(Q_PARTS) * HD
MROWS = SROWS + 3
LIF_STEPS, BETA, THRESHOLD = 5, 0.9, 1.0


def spike_thresholds():
    f = np.float32

    def spikes(y):
        mem, count = f(0), 0
        for _ in range(LIF_STEPS):
            reset = f(mem - f(THRESHOLD) > 0)
            mem = f(f(f(f(BETA) * mem) + y) - f(reset * f(THRESHOLD)))
            count += int(mem - f(THRESHOLD) > 0)
        return count

    found = []
    for k in range(1, LIF_STEPS + 1):
        low, high = (int(np.array(v, f).view(np.int32)) for v in (0.0, 64.0))
        while high - low > 1:
            mid = (low + high) // 2
            if spikes(np.array(mid, np.int32).view(f)[()]) >= k:
                high = mid
            else:
                low = mid
        found.append(float(np.array(low, np.int32).view(f)))
    return found


THETA = spike_thresholds()


def by_itself(eng, waited):
    eng.sem_inc(waited, 1)


class Mem:

    def __init__(self, nc, ctx):
        self.nc, self.ctx = nc, ctx

    def sb(self, name, shape, dt=F32):
        return self.ctx.enter_context(self.nc.sbuf_tensor(name, shape, dt))

    def bank(self, name):
        return self.ctx.enter_context(self.nc.psum_tensor(name, [P, TW], F32))

    def sem(self, name):
        return self.ctx.enter_context(self.nc.semaphore(name))


def project(nc, io, xT, vT, split_scr):
    CHUNKS = 2 * DC
    with ExitStack() as ctx:
        m = Mem(nc, ctx)
        ident = m.sb("ident", [P, P])
        mean_w = m.sb("mean_w", [P, P])
        eps_col = m.sb("eps_col", [P, 1])
        cosT = m.sb("cosT", [P, DC, S])
        sinT = m.sb("sinT", [P, DC, S])
        wdq = m.sb("wdq", [P, DC, LAT])
        wdkv = m.sb("wdkv", [P, DC, LAT])
        wq = m.sb("wq", [P, 3, D])
        wkc = m.sb("wkc", [P, D])
        wkr = m.sb("wkr", [P, 2, DC, D])
        wv = m.sb("wv", [P, D])
        bv = m.sb("bv", [P, D])
        bcol = m.sb("bcol", [P, 14])
        xin = m.sb("xin", [P, 2, TW // P, D])
        xc = m.sb("xc", [P, DC, TW])
        sq = m.sb("sq", [P, DC, TW])
        rs = m.sb("rs", [P, 3, TW])
        xn = m.sb("xn", [P, 2, DC, TW])
        ct = m.sb("ct", [P, 2, TW])
        rot = m.sb("rot", [P, 2, 3, TW])
        full = m.sb("full", [P, CHUNKS, TW])
        rest = m.sb("rest", [P, CHUNKS, TW])
        parts = m.sb("parts", [P, CHUNKS, 3, TW], BF16)
        tr_bank = [m.bank(f"tr_bank{c}") for c in range(DC)]
        mean_bank, var_bank = m.bank("mean_bank"), m.bank("var_bank")
        proj = [m.bank(f"proj{i}") for i in range(4)]

        consts_in = m.sem("consts_in")
        x_in = [m.sem("x_in0"), m.sem("x_in1")]
        consts_set = m.sem("consts_set")
        transposed, x_kept = m.sem("transposed"), m.sem("x_kept")
        mean_ready, centred, squared = m.sem("mean_ready"), m.sem("centred"), m.sem("squared")
        var_ready, rs_guess, rs_step, normed = m.sem("var_ready"), m.sem("rs_guess"), m.sem("rs_step"), m.sem("normed")
        proj_ready, latent_kept, rotated = m.sem("proj_ready"), m.sem("latent_kept"), m.sem("rotated")
        summed, high_kept, mid_kept = m.sem("summed"), m.sem("high_kept"), m.sem("mid_kept")
        rest_ready, low_kept, v_kept = m.sem("rest_ready"), m.sem("low_kept"), m.sem("v_kept")
        parts_out = [m.sem(f"parts_out{u}") for u in range(CHUNKS)]

        loads = [(ident[:], io["ident"]), (cosT[:], io["cos"].rearrange("(c p) t -> p c t", p=P)),
                 (sinT[:], io["sin"].rearrange("(c p) t -> p c t", p=P)),
                 (wdq[:], io["Wd_q"].rearrange("(c p) n -> p c n", p=P)),
                 (wdkv[:], io["Wd_kv"].rearrange("(c p) n -> p c n", p=P)),
                 (wq[:, 0, :], io["Wu_q"]), (wq[:, 1, :], io["Wq_r"]), (wq[:, 2, :], io["Wq_r_swap"]),
                 (wkc[:], io["Wu_k"]), (wkr[:, 0], io["Wk_r"].rearrange("(c p) n -> p c n", p=P)),
                 (wkr[:, 1], io["Wk_r_swap"].rearrange("(c p) n -> p c n", p=P)),
                 (wv[:], io["Wu_v"]), (bv[:], io["bv"]), (bcol[:], io["bcol_attn"])]
        CONSTS = 16 * len(loads)
        x_dram = io["x"].rearrange("b (i j p) d -> (b i) p j d", j=TW // P, p=P)
        UNITS = 16

        act_waited = m.sem("act_waited_project")
        block = ctx.enter_context(nc.Block())

        @block.sync
        def _(sp):
            for u in range(CHUNKS):
                sp.sem_inc(parts_out[u], 16)
            for t in range(2):
                sp.dma_start(xin[:, t], x_dram[t]).then_inc(x_in[t], 16)
            for dst, src in loads:
                sp.dma_start(dst, src).then_inc(consts_in, 16)

            def parts_of(b, half, with_loads):
                t = b * 2 + half
                if with_loads:
                    sp.wait_ge(transposed, t * DC + DC)
                    sp.dma_start(xin[:, half], x_dram[bass.ds(t + 2, 1)].rearrange("a p j d -> (a p) j d"))\
                        .then_inc(x_in[half], 16)
                for u in range(CHUNKS):
                    sp.wait_ge(low_kept, t * CHUNKS + u + 1 + CHUNKS)
                    side, c = 1 - u // DC, u % DC
                    sp.dma_start(split_scr[bass.ds(b * DC + (side * B * DC + c), 1), :, :, half * TW:(half + 1) * TW]
                                 .rearrange("a p s t -> (a p) s t"),
                                 parts[:, u]).then_inc(parts_out[u], 16)

            with sp.Fori(0, B - 1) as b:
                parts_of(b, 0, True)
                parts_of(b, 1, True)
            parts_of(B - 1, 0, False)
            parts_of(B - 1, 1, False)
            for u in range(CHUNKS):
                sp.wait_ge(parts_out[u], 16 * NT + 16)

        @block.gpsimd
        def _(pool):
            nc.gpsimd.memset(mean_w[:], 1.0 / D).then_inc(consts_set, 1)
            nc.gpsimd.memset(eps_col[:], EPS).then_inc(consts_set, 1)

        def tiles(eng, body):
            with eng.Fori(0, B - 1) as b:
                body(b, 0, True)
                body(b, 1, True)
            body(B - 1, 0, True)
            body(B - 1, 1, False)

        def following(b, half):
            return (b, 1) if half == 0 else (b + 1, 0)

        @block.tensor
        def _(pe):
            pe.sem_inc(var_ready, 1)
            pe.wait_ge(consts_in, CONSTS)
            pe.wait_ge(consts_set, 2)

            def turn(b, half):
                t = b * 2 + half
                pe.wait_ge(x_in[half], b * 16 + 16)
                for c in range(DC):
                    pe.wait_ge(x_kept, t * DC + c + 1)
                    for j in range(TW // P):
                        mm = nc.tensor.transpose(tr_bank[c][:, j * P:(j + 1) * P],
                                                 xin[:, half, j, c * P:(c + 1) * P], ident[:])
                    mm.then_inc(transposed, 1)

            def mean(b, half):
                t = b * 2 + half
                pe.wait_ge(x_kept, t * DC + 2 * DC)
                pe.wait_ge(centred, t * DC + DC)
                for c in range(DC):
                    mm = nc.tensor.matmul(mean_bank[:], mean_w[:], xT[:, c, bass.ds(t * TW, TW)],
                                          start=(c == 0), stop=(c == DC - 1))
                mm.then_inc(mean_ready, 1)

            def var(b, half):
                t = b * 2 + half
                pe.wait_ge(squared, t * DC + DC)
                pe.wait_ge(rs_step, t * 3 + 1)
                for c in range(DC):
                    mm = nc.tensor.matmul(var_bank[:], mean_w[:], sq[:, c], start=(c == 0), stop=(c == DC - 1))
                mm.then_inc(var_ready, 1)

            def project_unit(t, half, u):
                if u < 2:
                    pe.wait_ge(rotated, t * 12 + u + 1)
                elif u < 4:
                    pe.wait_ge(v_kept, t * 2 + u - 1)
                elif u < 6:
                    pe.wait_ge(latent_kept, t * 2 + u - 3)
                else:
                    pe.wait_ge(rotated, t * 12 + u - 3)
                side, c, kind = 1 - (u - 2) // 6, (u - 2) % 6 // 3, (1, 2, 0)[(u - 2) % 3]
                if u in (4, 8):
                    pe.wait_ge(latent_kept, t * 2 + 2)
                bank = proj[u % 4]
                if u < 2:
                    products = [(bank[:], (wdq, wdkv)[u][:, k], xn[:, half, k]) for k in range(DC)]
                elif u >= 14:
                    for j in range(2):
                        tok = slice((2 * (u - 14) + j) * P, (2 * (u - 14) + j + 1) * P)
                        mm = nc.tensor.matmul(bank[:, j * D:(j + 1) * D], ct[:, 1, tok], wv[:], start=True, stop=True)
                    mm.then_inc(proj_ready, 1)
                    return
                else:
                    cols = slice(c * P, (c + 1) * P)
                    if side == 0:
                        products = [(bank[:], wq[:, kind, cols], ct[:, 0])]
                    elif kind == 0:
                        products = [(bank[:], wkc[:, cols], ct[:, 1])]
                    else:
                        products = [(bank[:], wkr[:, kind - 1, k, cols], xn[:, half, k]) for k in range(DC)]
                for k, (to, w, x) in enumerate(products):
                    mm = nc.tensor.matmul(to, w, x, start=(k == 0), stop=(k == len(products) - 1))
                mm.then_inc(proj_ready, 1)

            def tile(b, half, with_next):
                t = b * 2 + half
                pe.wait_ge(normed, t * DC + DC)
                for u in range(UNITS):
                    project_unit(t, half, u)
                    if with_next and u == 1:
                        turn(*following(b, half))
                    if with_next and u == 3:
                        mean(*following(b, half))
                    if with_next and u == 6:
                        var(*following(b, half))

            turn(0, 0)
            mean(0, 0)
            var(0, 0)
            tiles(pe, tile)

        @block.scalar
        def _(act):
            nc.scalar.sem_inc(x_kept, DC)
            act.wait_ge(consts_set, 2)
            act.wait_ge(consts_in, CONSTS)

            def keep_x(b, half):
                t = b * 2 + half
                for c in range(DC):
                    act.wait_ge(transposed, t * DC + c + 1)
                    by_itself(act, act_waited)
                    nc.scalar.activation(xT[:, c, bass.ds(t * TW, TW)], tr_bank[c][:], ACT.Copy).then_inc(x_kept, 1)

            def square(b, half):
                t = b * 2 + half
                for c in range(DC):
                    act.wait_ge(centred, t * DC + DC + c + 1)
                    act.wait_ge(var_ready, t + 1)
                    nc.scalar.activation(sq[:, c], xc[:, c], ACT.Square).then_inc(squared, 1)

            def guess(b, half):
                t = b * 2 + half
                act.wait_ge(var_ready, t + 2)
                act.wait_ge(rs_step, t * 3 + 1)
                nc.scalar.activation(rs[:, 1], var_bank[:], ACT.Ln, bias=eps_col[:]).then_inc(rs_guess, 1)
                act.wait_ge(rs_guess, t * 2 + 1)
                nc.scalar.activation(rs[:, 0], rs[:, 1], ACT.Exp, scale=-0.5).then_inc(rs_guess, 1)

            def high(t, u):
                act.wait_ge(summed, t * CHUNKS + u + 3)
                act.wait_ge(parts_out[u], t * 16 + 16)
                nc.scalar.activation(parts[:, u, 0], full[:, u], ACT.Copy).then_inc(high_kept, 1)

            def middle(t, u):
                act.wait_ge(rest_ready, t * CHUNKS + u + 1)
                nc.scalar.activation(parts[:, u, 1], rest[:, u], ACT.Copy).then_inc(mid_kept, 1)

            def tile(b, half, with_next):
                t = b * 2 + half
                for u in range(2):
                    act.wait_ge(proj_ready, t * UNITS + u + 1)
                    nc.scalar.activation(ct[:, u], proj[u][:], ACT.Identity, bias=bcol[:, u:u + 1])\
                        .then_inc(latent_kept, 1)
                if with_next:
                    keep_x(*following(b, half))
                    square(*following(b, half))
                high(t, 0)
                if with_next:
                    guess(*following(b, half))
                high(t, 1)
                middle(t, 0)
                high(t, 2)
                middle(t, 1)
                high(t, 3)
                middle(t, 2)
                middle(t, 3)

            keep_x(0, 0)
            square(0, 0)
            guess(0, 0)
            tiles(act, tile)

        @block.vector
        def _(dve):
            nc.vector.sem_inc(centred, DC)
            nc.vector.sem_inc(rs_step, 1)
            nc.vector.sem_inc(rotated, 2)
            nc.vector.sem_inc(v_kept, 2)
            nc.vector.sem_inc(summed, 2)
            nc.vector.sem_inc(low_kept, CHUNKS)
            dve.wait_ge(consts_in, CONSTS)

            def centre(b, half):
                t = b * 2 + half
                dve.wait_ge(mean_ready, t + 1)
                for c in range(DC):
                    nc.vector.tensor_tensor(xc[:, c], xT[:, c, bass.ds(t * TW, TW)], mean_bank[:], ALU.subtract)\
                        .then_inc(centred, 1)

            def finish(b, half):
                t = b * 2 + half
                dve.wait_ge(rs_guess, t * 2 + 2)
                nc.vector.scalar_tensor_tensor(rs[:, 1], var_bank[:], EPS, rs[:, 0], ALU.add, ALU.mult)\
                    .then_inc(rs_step, 1)
                dve.wait_ge(rs_step, t * 3 + 2)
                nc.vector.scalar_tensor_tensor(rs[:, 2], rs[:, 1], -0.5, rs[:, 0], ALU.mult, ALU.mult)\
                    .then_inc(rs_step, 1)
                dve.wait_ge(rs_step, t * 3 + 3)
                nc.vector.scalar_tensor_tensor(rs[:, 1], rs[:, 2], 1.5, rs[:, 0], ALU.add, ALU.mult)\
                    .then_inc(rs_step, 1)
                dve.wait_ge(rs_step, t * 3 + 4)
                for c in range(DC):
                    nc.vector.tensor_tensor(xn[:, half, c], xc[:, c], rs[:, 1], ALU.mult).then_inc(normed, 1)

            def rotate(t, half, u):
                side, c = 1 - u // DC, u % DC
                n = t * 12 + 3 * u + 2
                bias = bcol[:, 2 + 6 * side + 3 * c:5 + 6 * side + 3 * c]
                banks = [proj[(2 + 3 * u + i) % 4] for i in range(3)]
                r = rot[:, u % 2]
                dve.wait_ge(summed, t * CHUNKS + u + 1)
                for i, table in enumerate((cosT, sinT)):
                    dve.wait_ge(proj_ready, t * UNITS + 3 + 3 * u + i)
                    nc.vector.scalar_tensor_tensor(r[:, i], banks[i][:], bias[:, i:i + 1],
                                                   table[:, c, half * TW:(half + 1) * TW], ALU.add, ALU.mult)\
                        .then_inc(rotated, 1)
                dve.wait_ge(proj_ready, t * UNITS + 5 + 3 * u)
                dve.wait_ge(rotated, n + 1)
                nc.vector.scalar_tensor_tensor(r[:, 2], banks[2][:], bias[:, 2:3], r[:, 0], ALU.add, ALU.add)\
                    .then_inc(rotated, 1)
                dve.wait_ge(rotated, n + 3)
                nc.vector.tensor_tensor(full[:, u], r[:, 2], r[:, 1], ALU.add).then_inc(summed, 1)

            def leave_rest(t, u):
                dve.wait_ge(high_kept, t * CHUNKS + u + 1)
                dve.wait_ge(low_kept, t * CHUNKS + u + 1)
                nc.vector.tensor_tensor(rest[:, u], full[:, u], parts[:, u, 0], ALU.subtract).then_inc(rest_ready, 1)

            def low(t, u):
                dve.wait_ge(mid_kept, t * CHUNKS + u + 1)
                nc.vector.tensor_tensor(parts[:, u, 2], rest[:, u], parts[:, u, 1], ALU.subtract).then_inc(low_kept, 1)

            def keep_v(b, half, t, pair):
                dve.wait_ge(proj_ready, t * UNITS + 15 + pair)
                for j in range(2):
                    ins = nc.vector.tensor_tensor(vT[:, bass.ds(b * NG, NG), half * 4 + 2 * pair + j, :],
                                                  proj[2 + pair][:, j * D:(j + 1) * D].rearrange("p (g n) -> p g n", g=NG),
                                                  bv[:].rearrange("p (g n) -> p g n", g=NG), ALU.add)
                ins.then_inc(v_kept, 1)

            def tile(b, half, with_next):
                t = b * 2 + half
                if with_next:
                    centre(*following(b, half))
                rotate(t, half, 0)
                rotate(t, half, 1)
                leave_rest(t, 0)
                if with_next:
                    finish(*following(b, half))
                rotate(t, half, 2)
                leave_rest(t, 1)
                low(t, 0)
                rotate(t, half, 3)
                leave_rest(t, 2)
                low(t, 1)
                keep_v(b, half, t, 0)
                keep_v(b, half, t, 1)
                leave_rest(t, 3)
                low(t, 2)
                low(t, 3)

            centre(0, 0)
            finish(0, 0)
            tiles(dve, tile)


def attend(nc, io, vT, split_scr, o_scr):
    NGT = B * NG
    UNITS = G * QT * 2
    HU = UNITS // 2
    LOAD = 16 * 3 * len(Q_PARTS)
    STEPS = 2 * QT
    MB = 3
    TURN_NOW, TURN_NEXT = 2, 10
    with ExitStack() as ctx:
        m = Mem(nc, ctx)
        qs = [m.sb(f"qs{i}", [P, 2, G, TW], BF16) for i in range(3)]
        ks = [m.sb(f"ks{i}", [P, G, S], BF16) for i in range(3)]
        vg = [m.sb(f"vg{i}", [P, QT, G, 2 * HD]) for i in range(3)]
        ident = m.sb("ident_a", [P, P])
        probs = m.sb("probs", [P, 2, G, TW])
        mx = m.sb("mx", [P, 2, HU])
        row_max = m.sb("row_max", [P, 2, HU // 2])
        neg_max = m.sb("neg_max", [HU // 2, 2, P])
        neg_rest = m.sb("neg_rest", [HU // 2, 2, P])
        neg_parts = m.sb("neg_parts", [HU // 2, 2, 3, P], BF16)
        o_sb = m.sb("o_sb", [P, 2, TW])
        max_bank = [m.bank(f"max_bank{i}") for i in range(MB)]
        score_bank = [m.ctx.enter_context(nc.psum_tensor(f"score_bank{i}", [P, 2, TW], F32)) for i in range(2)]
        o_bank = m.bank("o_bank")

        ident_in, ones_set, v_set = m.sem("ident_in"), m.sem("ones_set"), m.sem("v_set")
        stack_in = [m.sem(f"stack_in{i}") for i in range(3)]
        max_ready, reduced, row_max_ready = m.sem("max_ready"), m.sem("reduced"), m.sem("row_max_ready")
        turned, neg_ready, neg_split = m.sem("turned"), m.sem("neg_ready"), m.sem("neg_split")
        max_rows_in = [m.sem(f"max_rows_in{i}") for i in range(2)]
        scores_ready, probs_ready, pv_done = m.sem("scores_ready"), m.sem("probs_ready"), m.sem("pv_done")
        o_kept = m.sem("o_kept")
        o_out = [m.sem(f"o_out{i}") for i in range(2)]

        heads_in = split_scr.rearrange("a (h n) s t -> (a h) n s t", h=2)

        pool_waited = m.sem("pool_waited_attend")
        block = ctx.enter_context(nc.Block())

        def turn_bank(r, s):
            return max_bank[(r + 1 + 4 * (s + 1)) % MB]

        def groups(eng, body):
            with eng.Fori(0, (NGT - 1) // 3) as it:
                for r in range(3):
                    body(it * 3 + r, r, it, True)
            body(NGT - 1, (NGT - 1) % 3, (NGT - 1) // 3, False)

        @block.sync
        def _(sp):
            for h in range(2):
                sp.sem_inc(max_rows_in[h], 16)
                sp.sem_inc(o_out[h], 16)

            def load(g, r):
                q_in, k_in = (heads_in[bass.ds(g + side * NGT, 1)].rearrange("a (j i) s t -> (a i) j s t", i=HD)
                              for side in range(2))
                for n in range(len(Q_PARTS)):
                    rows = slice(n * HD, (n + 1) * HD)
                    sp.dma_start(ks[r][rows], k_in[:, :, K_PARTS[n], :]).then_inc(stack_in[r], 16)
                    for h in range(2):
                        sp.dma_start(qs[r][rows, h], q_in[:, :, Q_PARTS[n], h * TW:(h + 1) * TW])\
                            .then_inc(stack_in[r], 16)

            def max_rows(g, r, h):
                sp.wait_ge(neg_split, g * 8 + 4 * h + 12)
                for part in range(3):
                    sp.dma_start(qs[r][SROWS + part:SROWS + part + 1, h], neg_parts[:, h, part, :]).then_inc(max_rows_in[h], 16)

            def o_to_dram(g, h):
                sp.wait_ge(o_kept, g * 2 + h + 3)
                sp.dma_start(o_scr[bass.ds(g, 1), :, h * TW:(h + 1) * TW].rearrange("a p t -> (a p) t"), o_sb[:, h])\
                    .then_inc(o_out[h], 16)

            def body(g, r, with_next=True, with_load=True):
                max_rows(g, r, 1)
                if with_load:
                    sp.wait_ge(scores_ready, g * 2 * STEPS + 1)
                    load(g + 2, (r + 2) % 3)
                if with_next:
                    max_rows(g + 1, (r + 1) % 3, 0)
                o_to_dram(g, 0)
                o_to_dram(g, 1)

            sp.dma_start(ident[:], io["ident"]).then_inc(ident_in, 16)
            load(0, 0)
            load(1, 1)
            max_rows(0, 0, 0)
            with sp.Fori(0, (NGT - 4) // 3) as it:
                for r in range(3):
                    body(it * 3 + r, r)
            for g in range((NGT - 4) // 3 * 3, NGT):
                body(g, g % 3, g < NGT - 1, g < NGT - 2)
            for h in range(2):
                sp.wait_ge(o_out[h], 16 * NGT + 16)

        @block.gpsimd
        def _(pool):
            pool.sem_inc(neg_split, 8)
            for i in range(3):
                nc.gpsimd.memset(ks[i][SROWS:MROWS], 1.0).then_inc(ones_set, 1)
                pool.wait_ge(ones_set, 2 * i + 1)
                nc.gpsimd.memset(vg[i][:, :, :, HD:], 1.0).then_inc(ones_set, 1)
                pool.wait_ge(ones_set, 2 * i + 2)

            def v_of(g, r):
                pool.wait_ge(pv_done, g * STEPS + STEPS)
                by_itself(pool, pool_waited)
                nc.gpsimd.tensor_copy(vg[r][:, :, :, 0:HD], vT[:, bass.ds(g, 1), :, :]
                                      .rearrange("p a k (j i) -> p (a k) j i", i=HD)).then_inc(v_set, 1)

            def split(g, h):
                n = g * 8 + 4 * h + 8
                pool.wait_ge(neg_ready, g * 2 + h + 1)
                pool.wait_ge(max_rows_in[h], g * 48 + 16)
                by_itself(pool, pool_waited)
                nc.gpsimd.tensor_copy(neg_parts[:, h, 0], neg_max[:, h]).then_inc(neg_split, 1)
                pool.wait_ge(neg_split, n + 1)
                nc.gpsimd.tensor_tensor(neg_rest[:, h], neg_max[:, h], neg_parts[:, h, 0], ALU.subtract)\
                    .then_inc(neg_split, 1)
                pool.wait_ge(neg_split, n + 2)
                by_itself(pool, pool_waited)
                nc.gpsimd.tensor_copy(neg_parts[:, h, 1], neg_rest[:, h]).then_inc(neg_split, 1)
                pool.wait_ge(neg_split, n + 3)
                nc.gpsimd.tensor_tensor(neg_parts[:, h, 2], neg_rest[:, h], neg_parts[:, h, 1], ALU.subtract)\
                    .then_inc(neg_split, 1)

            def body(g, r, it, with_next):
                split(g, 1)
                if with_next:
                    v_of(g + 1, (r + 1) % 3)
                    split(g + 1, 0)

            pool.wait_ge(ones_set, 6)
            v_of(0, 0)
            split(0, 0)
            groups(pool, body)

        @block.tensor
        def _(pe):
            pe.sem_inc(scores_ready, 1)
            pe.sem_inc(pv_done, 3 * STEPS)
            pe.wait_ge(ident_in, 16)
            pe.wait_ge(ones_set, 6)

            def for_max(g, r, a):
                half, j, qt, kh = a // HU, a % HU // 8, a % 8 // 2, a % 2
                pe.wait_ge(reduced, g * UNITS + a + 1)
                nc.tensor.matmul(max_bank[(r + a) % MB][:], qs[r][0:SROWS, half, j, qt * P:(qt + 1) * P],
                                 ks[r][0:SROWS, j, kh * TW:(kh + 1) * TW], start=True, stop=True)\
                    .then_inc(max_ready, 1)

            def turn(g, h, bank):
                pe.wait_ge(row_max_ready, g * 2 + h + 1)
                nc.tensor.transpose(bank[0:HU // 2, 0:P], row_max[:, h], ident[:]).then_inc(turned, 1)

            def scores(g, r, s, pair):
                pe.wait_ge(probs_ready, g * 2 * STEPS + 2 * s + pair + 1)
                qh, kt = s // QT, s % QT
                for j in (2 * pair, 2 * pair + 1):
                    mm = nc.tensor.matmul(score_bank[pair][:, j % 2], ks[r][0:MROWS, j, kt * P:(kt + 1) * P],
                                          qs[r][0:MROWS, qh, j, :], start=True, stop=True)
                mm.then_inc(scores_ready, 1)

            def body(g, r, it, with_next):
                for s in range(STEPS):
                    if s % QT == 0:
                        pe.wait_ge(max_rows_in[s // QT], g * 48 + 64)
                    if s == 0 and with_next:
                        pe.wait_ge(stack_in[(r + 1) % 3], it * LOAD + LOAD * (1 + (r + 1) // 3))
                    for pair in range(2):
                        scores(g, r, s, pair)
                        if with_next:
                            if s in (TURN_NOW + 1, TURN_NEXT + 1) and pair == 0:
                                pe.wait_ge(neg_ready, g * 2 + (2 if s == TURN_NOW + 1 else 3))
                            for_max(g + 1, (r + 1) % 3, 4 * s + pair)
                    if with_next:
                        for_max(g + 1, (r + 1) % 3, 4 * s + 2)
                    if s > 0:
                        pv(g, r, s - 1)
                    elif r > 0:
                        pv(g - 1, r - 1, STEPS - 1)
                    if s == TURN_NOW or s == TURN_NEXT and with_next:
                        if with_next:
                            pe.wait_ge(reduced, g * UNITS + UNITS + 4 * s + 2 + MB)
                        turn(g if s == TURN_NOW else g + 1, 1 if s == TURN_NOW else 0, turn_bank(r, s))
                    if with_next:
                        for_max(g + 1, (r + 1) % 3, 4 * s + 3)
                if r == 2 or not with_next:
                    pv(g, r, STEPS - 1)

            def pv(g, r, s):
                qh, kt = s // QT, s % QT
                if s == 0:
                    pe.wait_ge(v_set, g + 1)
                if kt == 0:
                    pe.wait_ge(o_kept, g * 2 + qh + 2)
                pe.wait_ge(probs_ready, g * 2 * STEPS + 2 * s + 4)
                for j in range(G):
                    mm = nc.tensor.matmul(o_bank[32 * j:32 * j + 32, :], vg[r][:, kt, j], probs[:, s % 2, j],
                                          start=(kt == 0), stop=(kt == QT - 1))
                mm.then_inc(pv_done, 1)

            pe.wait_ge(stack_in[0], LOAD)
            for n in range(HU):
                half, j, qt = n // (HU // 2), n % (HU // 2) // 4, n % 4
                if n > 1:
                    pe.wait_ge(reduced, 2 * (n - 1) + MB)
                for kh in range(2):
                    mm = nc.tensor.matmul(score_bank[n % 2][:, kh], qs[0][0:SROWS, half, j, qt * P:(qt + 1) * P],
                                          ks[0][0:SROWS, j, kh * TW:(kh + 1) * TW], start=True, stop=True)
                mm.then_inc(max_ready, 2)
                if n == HU // 2 + 2:
                    turn(0, 0, max_bank[0])
            pe.wait_ge(neg_ready, 1)
            pe.wait_ge(reduced, UNITS + MB)
            groups(pe, body)

        @block.scalar
        def _(act):
            act.sem_inc(probs_ready, 2)

            def body(g, r, it, with_next):
                for s in range(STEPS):
                    act.wait_ge(pv_done, g * STEPS + (3 * STEPS + s - 1))
                    for pair in range(2):
                        act.wait_ge(scores_ready, g * 2 * STEPS + 2 * s + pair + 2)
                        nc.scalar.activation(probs[:, s % 2, 2 * pair:2 * pair + 2], score_bank[pair][:], ACT.Exp,
                                             scale=SOFTMAX_SCALE).then_inc(probs_ready, 1)

            groups(act, body)

        @block.vector
        def _(dve):
            dve.sem_inc(reduced, MB)
            dve.sem_inc(o_kept, 2)

            def maximum(g, r, a):
                dve.wait_ge(max_ready, g * UNITS + a + 1)
                nc.vector.tensor_reduce(mx[:, a // HU, a % HU:a % HU + 1], max_bank[(r + a) % MB][:], AX_X, ALU.max)\
                    .then_inc(reduced, 1)

            def both_halves(g, h):
                dve.wait_ge(reduced, g * UNITS + (h + 1) * HU + MB)
                nc.vector.tensor_reduce(row_max[:, h], mx[:, h].rearrange("p (u k) -> p u k", k=2), AX_X, ALU.max)\
                    .then_inc(row_max_ready, 1)

            def negate(g, h, bank):
                dve.wait_ge(turned, g * 2 + h + 1)
                dve.wait_ge(neg_split, g * 8 + 4 * h + 4)
                nc.vector.tensor_scalar(neg_max[:, h], bank[0:HU // 2, 0:P], -1.0, None, ALU.mult)\
                    .then_inc(neg_ready, 1)

            def keep_o(g, qh):
                dve.wait_ge(pv_done, g * STEPS + (3 * STEPS + (qh + 1) * QT))
                dve.wait_ge(o_out[qh], g * 16 + 16)
                nc.vector.tensor_copy(o_sb[:, qh], o_bank[:]).then_inc(o_kept, 1)

            def body(g, r, it, with_next):
                for s in range(STEPS):
                    for i in range(4):
                        if i == 3 and s == TURN_NOW:
                            negate(g, 1, turn_bank(r, s))
                        if i == 3 and s == TURN_NEXT and with_next:
                            negate(g + 1, 0, turn_bank(r, s))
                        if i == 3 and s == 0 and r > 0:
                            keep_o(g - 1, 1)
                        if i == 3 and s == QT:
                            keep_o(g, 0)
                        if with_next:
                            maximum(g + 1, (r + 1) % 3, 4 * s + i)
                    if s == QT - 1 and with_next:
                        both_halves(g + 1, 0)
                if with_next:
                    both_halves(g + 1, 1)
                if r == 2 or not with_next:
                    keep_o(g, 1)

            for n in range(HU):
                half, i = n // (HU // 2), n % (HU // 2)
                dve.wait_ge(max_ready, 2 * n + 2)
                nc.vector.tensor_reduce(row_max[:, half, i:i + 1], score_bank[n % 2][:].rearrange("p a t -> p (a t)"),
                                        AX_X, ALU.max).then_inc(reduced, 2)
                if i == HU // 2 - 1:
                    dve.wait_ge(reduced, 2 * n + 2 + MB)
                    nc.vector.sem_inc(row_max_ready, 1)
                if n == HU // 2 + 3:
                    negate(0, 0, max_bank[0])
            groups(dve, body)


class Norm:

    def __init__(self, m, xT, xn_at, tag):
        self.xT, self.xn_at = xT, xn_at
        self.mean_w, self.eps_col = m.sb("mean_w" + tag, [P, P]), m.sb("eps_col" + tag, [P, 1])
        self.xc, self.sq = m.sb("xc" + tag, [P, DC, TW]), m.sb("sq" + tag, [P, DC, TW])
        self.rs = m.sb("rs" + tag, [P, 3, TW])
        self.mean_bank, self.var_bank = m.bank("mean_bank" + tag), m.bank("var_bank" + tag)
        self.set, self.mean_ready, self.centred, self.squared, self.var_ready, self.guessed, self.stepped, self.normed = (
            m.sem(n + tag) for n in ("norm_set", "mean_ready", "centred", "squared", "var_ready", "guessed",
                                     "stepped", "normed"))

    def tile(self, c, t):
        return self.xT[:, c, bass.ds(t * TW, TW)]

    def start_pool(self, nc):
        nc.gpsimd.memset(self.mean_w[:], 1.0 / D).then_inc(self.set, 1)
        nc.gpsimd.memset(self.eps_col[:], EPS).then_inc(self.set, 1)

    def start_pe(self, nc, pe):
        pe.sem_inc(self.var_ready, 1)
        pe.wait_ge(self.set, 2)

    def start_dve(self, nc, dve):
        dve.sem_inc(self.centred, DC)
        dve.sem_inc(self.stepped, 1)
        dve.sem_inc(self.normed, DC)

    def start_act(self, nc, act):
        act.wait_ge(self.set, 2)

    def mean(self, nc, pe, t):
        pe.wait_ge(self.centred, t * DC + DC)
        for c in range(DC):
            mm = nc.tensor.matmul(self.mean_bank[:], self.mean_w[:], self.tile(c, t), start=(c == 0), stop=(c == DC - 1))
        mm.then_inc(self.mean_ready, 1)

    def centre(self, nc, dve, t):
        dve.wait_ge(self.mean_ready, t + 1)
        dve.wait_ge(self.normed, t * DC + DC)
        for c in range(DC):
            nc.vector.tensor_tensor(self.xc[:, c], self.tile(c, t), self.mean_bank[:], ALU.subtract)\
                .then_inc(self.centred, 1)

    def square(self, nc, act, t):
        act.wait_ge(self.var_ready, t + 1)
        for c in range(DC):
            act.wait_ge(self.centred, t * DC + DC + c + 1)
            nc.scalar.activation(self.sq[:, c], self.xc[:, c], ACT.Square).then_inc(self.squared, 1)

    def var(self, nc, pe, t):
        pe.wait_ge(self.squared, t * DC + DC)
        pe.wait_ge(self.stepped, t * 3 + 1)
        for c in range(DC):
            mm = nc.tensor.matmul(self.var_bank[:], self.mean_w[:], self.sq[:, c], start=(c == 0), stop=(c == DC - 1))
        mm.then_inc(self.var_ready, 1)

    def guess(self, nc, act, t):
        act.wait_ge(self.var_ready, t + 2)
        act.wait_ge(self.stepped, t * 3 + 1)
        nc.scalar.activation(self.rs[:, 1], self.var_bank[:], ACT.Ln, bias=self.eps_col[:]).then_inc(self.guessed, 1)
        act.wait_ge(self.guessed, t * 2 + 1)
        nc.scalar.activation(self.rs[:, 0], self.rs[:, 1], ACT.Exp, scale=-0.5).then_inc(self.guessed, 1)

    def finish(self, nc, dve, t, xn_at=None):
        rs = self.rs
        dve.wait_ge(self.guessed, t * 2 + 2)
        nc.vector.scalar_tensor_tensor(rs[:, 1], self.var_bank[:], EPS, rs[:, 0], ALU.add, ALU.mult)\
            .then_inc(self.stepped, 1)
        dve.wait_ge(self.stepped, t * 3 + 2)
        nc.vector.scalar_tensor_tensor(rs[:, 2], rs[:, 1], -0.5, rs[:, 0], ALU.mult, ALU.mult)\
            .then_inc(self.stepped, 1)
        dve.wait_ge(self.stepped, t * 3 + 3)
        nc.vector.scalar_tensor_tensor(rs[:, 1], rs[:, 2], 1.5, rs[:, 0], ALU.add, ALU.mult).then_inc(self.stepped, 1)
        dve.wait_ge(self.stepped, t * 3 + 4)
        for c in range(DC):
            nc.vector.tensor_tensor((xn_at or self.xn_at)(c, t), self.xc[:, c], rs[:, 1], ALU.mult).then_inc(self.normed, 1)


def merge_heads(nc, io, xT, o_scr, recip_scr):
    with ExitStack() as ctx:
        m = Mem(nc, ctx)
        wo = m.sb("wo", [P, DC, D])
        bo = m.sb("bo", [P, DC])
        head_of = m.sb("head_of", [H, D])
        sums = m.sb("sums", [P, TW])
        recips = m.sb("recips", [P, TW])
        by_head = m.sb("by_head", [H, B, S])
        o_in = m.sb("o_in", [P, 2, DC, TW])
        o_n = m.sb("o_n", [P, 2, DC, TW])
        recip_bank = [m.bank(f"recip_bank{c}") for c in range(DC)]
        out_bank = [m.bank(f"out_bank{c}") for c in range(DC)]
        consts_in, sums_in, recips_out, by_head_in = (m.sem(n) for n in ("mh_consts", "sums_in", "recips_out", "by_head_in"))
        heads_in = [m.sem(f"heads_in{i}") for i in range(2)]
        recips_ready, spread, divided, out_ready, x_new = (m.sem(n) for n in ("recips_ready", "spread", "divided", "out_ready", "mh_x_new"))
        by_rows = o_scr.rearrange("g (j r) t -> (g j) r t", r=2 * HD)
        pe_waited = m.sem("pe_waited_merge_heads")
        block = ctx.enter_context(nc.Block())

        @block.sync
        def _(sp):
            sp.dma_start(sums[:], by_rows[:, HD, :].rearrange("g (h t) -> g h t", t=TW)).then_inc(sums_in, 16)
            for dst, src in ((wo[:], io["Wo"].rearrange("(c p) n -> p c n", p=P)), (bo[:], io["bo"]), (head_of[:], io["head_of"])):
                sp.dma_start(dst, src).then_inc(consts_in, 16)

            def load(b, half):
                for c in range(DC):
                    sp.dma_start(o_in[:, half, c, :],
                                 by_rows[bass.ds(b * H + c * (H // DC), H // DC), 0:HD, half * TW:(half + 1) * TW])\
                        .then_inc(heads_in[half], 16)

            load(0, 0)
            load(0, 1)
            sp.wait_ge(recips_ready, 1)
            sp.dma_start(recip_scr.rearrange("g (h t) -> (g h) t", t=TW), recips[:]).then_inc(recips_out, 16)
            sp.wait_ge(recips_out, 16)
            sp.dma_start(by_head[:], recip_scr.rearrange("(b h) t -> h b t", h=H)).then_inc(by_head_in, 16)
            with sp.Fori(1, B) as b:
                for half in range(2):
                    sp.wait_ge(divided, b * 2 * DC + half * DC)
                    load(b, half)

        @block.tensor
        def _(pe):
            pe.wait_ge(consts_in, 48)
            pe.wait_ge(by_head_in, 16)

            def tile(b, half):
                t = b * 2 + half
                for c in range(DC):
                    pe.wait_ge(divided, t * DC + c + 1)
                    by_itself(pe, pe_waited)
                    nc.tensor.matmul(recip_bank[c][:], head_of[:, c * P:(c + 1) * P],
                                     by_head[:, bass.ds(b, 1), half * TW:(half + 1) * TW].rearrange("h a t -> h (a t)"),
                                     start=True, stop=True).then_inc(spread, 1)
                pe.wait_ge(divided, t * DC + 2 * DC)
                for c in range(DC):
                    pe.wait_ge(x_new, t * DC + c + 1)
                    for k in range(DC):
                        mm = nc.tensor.matmul(out_bank[c][:], wo[:, k, c * P:(c + 1) * P], o_n[:, half, k],
                                              start=(k == 0), stop=(k == DC - 1))
                    mm.then_inc(out_ready, 1)

            with pe.Fori(0, B) as b:
                tile(b, 0)
                tile(b, 1)

        @block.vector
        def _(dve):
            dve.sem_inc(divided, DC)
            dve.sem_inc(x_new, DC)
            dve.wait_ge(sums_in, 16)
            nc.vector.reciprocal(recips[:], sums[:]).then_inc(recips_ready, 1)

            def tile(b, half):
                t = b * 2 + half
                for c in range(DC):
                    dve.wait_ge(spread, t * DC + c + 1)
                    dve.wait_ge(heads_in[half], b * 32 + 32)
                    nc.vector.tensor_tensor(o_n[:, half, c], o_in[:, half, c], recip_bank[c][:], ALU.mult)\
                        .then_inc(divided, 1)
                for c in range(DC):
                    dve.wait_ge(out_ready, t * DC + c + 1)
                    x = xT[:, c, bass.ds(t * TW, TW)]
                    nc.vector.scalar_tensor_tensor(x, out_bank[c][:], bo[:, c:c + 1], x, ALU.add, ALU.add)\
                        .then_inc(x_new, 1)

            with dve.Fori(0, B) as b:
                tile(b, 0)
                tile(b, 1)


def feed_forward(nc, io, xT, tag):
    BANKS = 4
    with ExitStack() as ctx:
        m = Mem(nc, ctx)
        wfc = m.sb("wfc" + tag, [P, DC, FF])
        wpr = m.sb("wpr" + tag, [P, FC, D])
        xn = m.sb("xn" + tag, [P, DC, T])
        relu = m.sb("relu" + tag, [P, 2, TW])
        hid = m.sb("hid" + tag, [P, FC, TW])
        count = m.sb("count" + tag, [P, DC, TW])
        norm = Norm(m, xT, lambda c, t: xn[:, c, bass.ds(t * TW, TW)], tag)
        hid_bank = [m.bank(f"hid_bank{i}" + tag) for i in range(BANKS)]
        y_bank = [m.bank(f"y_bank{c}" + tag) for c in range(DC)]
        weights_in, hid_ready, relu_ready, hid_kept, y_ready, fired, x_new = (
            m.sem(n + tag) for n in ("weights_in", "hid_ready", "relu_ready", "hid_kept", "y_ready", "fired", "x_new"))
        block = ctx.enter_context(nc.Block())

        @block.sync
        def _(sp):
            sp.dma_start(wfc[:], io["W_fcT"].rearrange("(c p) f -> p c f", p=P)).then_inc(weights_in, 16)
            sp.dma_start(wpr[:], io["W_projT"].rearrange("(f p) d -> p f d", p=P)).then_inc(weights_in, 16)

        @block.gpsimd
        def _(pool):
            norm.start_pool(nc)

        @block.tensor
        def _(pe):
            norm.start_pe(nc, pe)
            norm.mean(nc, pe, 0)
            norm.var(nc, pe, 0)
            pe.wait_ge(weights_in, 32)

            def out(t, f):
                pe.wait_ge(hid_kept, t * FC + f + 1 + BANKS)
                for c in range(DC):
                    if f == 0:
                        pe.wait_ge(x_new, t * DC + c + 1)
                    mm = nc.tensor.matmul(y_bank[c][:], wpr[:, f, c * P:(c + 1) * P], hid[:, f],
                                          start=(f == 0), stop=(f == FC - 1))
                    if f == FC - 1:
                        mm.then_inc(y_ready, 1)

            def tile(t, with_next):
                pe.wait_ge(norm.normed, t * DC + 2 * DC)
                for f in range(FC):
                    pe.wait_ge(hid_kept, t * FC + f + 1)
                    for c in range(DC):
                        mm = nc.tensor.matmul(hid_bank[f % BANKS][:], wfc[:, c, f * P:(f + 1) * P],
                                              xn[:, c, bass.ds(t * TW, TW)], start=(c == 0), stop=(c == DC - 1))
                    mm.then_inc(hid_ready, 1)
                    if f == 2 and with_next:
                        norm.mean(nc, pe, t + 1)
                    if f == 5 and with_next:
                        norm.var(nc, pe, t + 1)
                    if f >= 3:
                        out(t, f - 3)
                for f in range(FC - 3, FC):
                    out(t, f)

            with pe.Fori(0, NT - 1) as t:
                tile(t, True)
            tile(NT - 1, False)

        @block.scalar
        def _(act):
            norm.start_act(nc, act)
            norm.square(nc, act, 0)
            norm.guess(nc, act, 0)

            def tile(t, with_next):
                for f in range(FC):
                    act.wait_ge(hid_ready, t * FC + f + 1)
                    act.wait_ge(hid_kept, t * FC + f + BANKS - 1)
                    nc.scalar.activation(relu[:, f % 2], hid_bank[f % BANKS][:], ACT.Relu).then_inc(relu_ready, 1)
                    if f == 3 and with_next:
                        norm.square(nc, act, t + 1)
                    if f == 6 and with_next:
                        norm.guess(nc, act, t + 1)

            with act.Fori(0, NT - 1) as t:
                tile(t, True)
            tile(NT - 1, False)

        @block.vector
        def _(dve):
            norm.start_dve(nc, dve)
            dve.sem_inc(hid_kept, BANKS)
            dve.sem_inc(x_new, DC)
            norm.centre(nc, dve, 0)
            norm.finish(nc, dve, 0)

            def tile(t, with_next):
                for f in range(FC):
                    dve.wait_ge(relu_ready, t * FC + f + 1)
                    nc.vector.scalar_tensor_tensor(hid[:, f], hid_bank[f % BANKS][:], 0.0, relu[:, f % 2],
                                                   ALU.max, ALU.mult).then_inc(hid_kept, 1)
                    if f == 2 and with_next:
                        norm.centre(nc, dve, t + 1)
                if with_next:
                    norm.finish(nc, dve, t + 1)
                n = t * DC * LIF_STEPS
                for k in range(LIF_STEPS):
                    for c in range(DC):
                        if k == 0:
                            dve.wait_ge(y_ready, t * DC + c + 1)
                            nc.vector.tensor_scalar(count[:, c], y_bank[c][:], THETA[0], None, ALU.is_gt)\
                                .then_inc(fired, 1)
                        else:
                            dve.wait_ge(fired, n + DC * (k - 1) + c + 1)
                            nc.vector.scalar_tensor_tensor(count[:, c], y_bank[c][:], THETA[k], count[:, c],
                                                           ALU.is_gt, ALU.add).then_inc(fired, 1)
                for c in range(DC):
                    dve.wait_ge(fired, n + DC * (LIF_STEPS - 1) + c + 1)
                    x = xT[:, c, bass.ds(t * TW, TW)]
                    nc.vector.scalar_tensor_tensor(x, count[:, c], 1.0 / LIF_STEPS, x, ALU.mult, ALU.add)\
                        .then_inc(x_new, 1)

            with dve.Fori(0, NT - 1) as t:
                tile(t, True)
            tile(NT - 1, False)


def emit(nc, io, xT, out):
    with ExitStack() as ctx:
        m = Mem(nc, ctx)
        ident = m.sb("ident_e", [P, P])
        x_out = m.sb("x_out", [P, 2, TW // P, D])
        bank = [m.bank(f"emit_bank{i}") for i in range(8)]
        stage = m.sb("stage", [P, 2, DC, TW])
        ident_in, turned, kept, staged = m.sem("ident_in_e"), m.sem("turned_e"), m.sem("kept_e"), m.sem("staged")
        sent = [m.sem(f"sent{i}") for i in range(2)]
        out_tiles = out.rearrange("b (i j p) d -> (b i) p j d", j=TW // P, p=P)
        pool_waited = m.sem("pool_waited_emit")
        block = ctx.enter_context(nc.Block())

        @block.sync
        def _(sp):
            for i in range(2):
                sp.sem_inc(sent[i], 16)
            sp.dma_start(ident[:], io["ident"]).then_inc(ident_in, 16)
            with sp.Fori(0, B) as b:
                for half in range(2):
                    sp.wait_ge(kept, b * 8 + half * 4 + 4 + 8)
                    sp.dma_start(out_tiles[bass.ds(b * 2 + half, 1)].rearrange("a p j d -> (a p) j d"), x_out[:, half])\
                        .then_inc(sent[half], 16)
            for i in range(2):
                sp.wait_ge(sent[i], 16 * B + 16)

        @block.tensor
        def _(pe):
            pe.wait_ge(ident_in, 16)
            with pe.Fori(0, B) as b:
                for half in range(2):
                    for j in range(TW // P):
                        pe.wait_ge(kept, b * 8 + half * 4 + j + 1)
                        if j == 0:
                            pe.wait_ge(staged, b * 2 + half + 1 + 2)
                        for c in range(DC):
                            mm = nc.tensor.transpose(bank[half * 4 + j][:, c * P:(c + 1) * P],
                                                     stage[:, half, c, j * P:(j + 1) * P], ident[:])
                        mm.then_inc(turned, 1)

        @block.gpsimd
        def _(pool):
            pool.sem_inc(staged, 2)
            with pool.Fori(0, B) as b:
                for half in range(2):
                    pool.wait_ge(kept, b * 8 + half * 4 + 4)
                    by_itself(pool, pool_waited)
                    nc.gpsimd.tensor_copy(stage[:, half], xT[:, :, bass.ds(b * S + half * TW, TW)]).then_inc(staged, 1)

        @block.scalar
        def _(act):
            act.sem_inc(kept, 8)
            with act.Fori(0, B) as b:
                for half in range(2):
                    act.wait_ge(sent[half], b * 16 + 16)
                    for j in range(TW // P):
                        act.wait_ge(turned, b * 8 + half * 4 + j + 1)
                        nc.scalar.activation(x_out[:, half, j], bank[half * 4 + j][:, 0:D], ACT.Copy).then_inc(kept, 1)


def scan(nc, io, xT, bc_scr):
    NU = NS * DC
    BANKED = 14
    BC = 4
    WR = 4
    AR = 2
    with ExitStack() as ctx:
        m = Mem(nc, ctx)
        wx, wz, wout = m.sb("wx", [P, DC, D]), m.sb("wz", [P, DC, D]), m.sb("wout", [P, DC, D])
        wpar = m.sb("wpar", [P, DC, R + 2 * NS])
        wdt = m.sb("wdt", [R, D])
        conv_w, b_dt, d_par = m.sb("conv_w", [P, DC, TAPS]), m.sb("b_dt", [P, DC]), m.sb("d_par", [P, DC])
        ident = m.sb("ident_s", [P, P])
        ones = m.sb("ones_s", [P, P])
        decay = m.sb("decay", [P, 6, DC, NS])
        neg_a, a_col, is_small, not_small, a_den, a_rec = (decay[:, i] for i in range(6))
        small_any = m.sb("small_any", [P, 1])
        small_int = m.sb("small_int", [1, 1], I32)
        xn = m.sb("xn_s", [P, DC, S])
        par = m.sb("par", [R + 2 * NS, 2, TW])
        log_part, exp_part = m.sb("log_part", [P, TW]), m.sb("exp_part", [P, TW])
        xr = m.sb("xr", [P, DC, TAPS - 1 + S])
        cv = m.sb("cv", [P, S])
        dt, u, sz = (m.sb(n, [P, 2, DC, S]) for n in ("dt", "u", "sz"))
        bc = m.sb("bc", [P, BC, 2, S])
        a_t = m.sb("a_t", [P, AR, S])
        w_in = m.sb("w_in", [P, WR, S])
        h_out = m.sb("h_out", [P, WR, S])
        norm = Norm(m, xT, None, "_s")
        work = [m.bank(f"work{i}") for i in range(2)]
        y_bank = [m.bank(f"ys_bank{i}") for i in range(2 * DC)]

        (consts_in, exp_a, decay_set, small_summed, zeros_set, prep_made, prep_used, par_out, soft_act, soft_dve,
         conv_step, silu_u, decays, inputs, scaled, scanned, weighted, summed, gated, out_made, x_new) = (
            m.sem(n + "_s") for n in (
                "consts_in", "exp_a", "decay_set", "small_summed", "zeros_set", "prep_made", "prep_used", "par_out",
                "soft_act", "soft_dve", "conv_step", "silu_u", "decays", "inputs", "scaled", "scanned", "weighted",
                "summed", "gated", "out_made", "x_new"))
        bc_in = [m.sem(f"bc_in{i}") for i in range(BC)]
        loads = [(w[:], io[n].rearrange("(c p) n -> p c n", p=P)) for w, n in
                 ((wx, "W_xT"), (wz, "W_zT"), (wout, "W_outT"), (wpar, "W_paramsT"), (conv_w, "conv"), (neg_a, "A_log"))]
        loads += [(wdt[:], io["W_dtT"]), (b_dt[:], io["b_dt"]), (d_par[:], io["D_param"]), (ident[:], io["ident"])]
        CONSTS = 16 * len(loads)
        pool_waited = m.sem("pool_waited_scan")
        act_waited = m.sem("act_waited_scan")
        dve_waited = m.sem("dve_waited_scan")
        block = ctx.enter_context(nc.Block())

        DT, XR, Z = 2, 6, 10
        norm_slot = (0, 5)
        made_slot = [6, 11, 13, 15, 17, 19] + list(range(20, 28))
        pieces = []
        for h in range(2):
            s = norm_slot[h]
            pieces += [(s, "pe", "mean", h), (s + 1, "dve", "centre", h), (s + 2, "act", "square", h),
                       (s + 3, "pe", "var", h), (s + 4, "act", "guess", h), (s + 5, "dve", "finish", h)]
        for i in range(BANKED):
            pieces += [(made_slot[i], "pe", "make", i), (made_slot[i] + 1, "act", "use", i)]
            if DT <= i < XR:
                pieces.append((made_slot[i] + 2, "dve", "soft", i - DT))
        pieces += [(23, "dve", "conv", 0), (25, "act", "silu", 0), (26, "dve", "conv", 1), (28, "act", "silu", 1)]
        pieces.sort(key=lambda piece: piece[0])

        def prepare(engine, run, b, slot=None):
            for s, e, name, arg in pieces:
                if e == engine and (slot is None or s == slot):
                    run[name](b, arg)

        def batches(eng, body):
            with eng.Fori(0, B - 1) as b:
                body(b, True)
            body(B - 1, False)

        def turn(b):
            return bass.ds(b % 2, 1)

        @block.sync
        def _(sp):
            sp.sem_inc(par_out, 16)
            for dst, src in loads:
                sp.dma_start(dst, src).then_inc(consts_in, 16)

            def bc_out(b):
                sp.wait_ge(prep_used, b * BANKED + 4)
                sp.dma_start(bc_scr[bass.ds(b, 1)].rearrange("a n t -> (a n) t"),
                             par[R:R + 2 * NS].rearrange("p h t -> p (h t)")).then_inc(par_out, 16)

            def body(b, with_next):
                sp.wait_ge(par_out, b * 16 + 32)
                for n in range(NS):
                    sp.wait_ge(weighted, b * NU + 2 * n + 2)
                    src = bc_scr[bass.ds(b, 1)].rearrange("a (g n) t -> a n g t", n=NS)[:, n]
                    sp.dma_start(bc[:, n % BC], src.rearrange("a g t -> (a g) t").partition_broadcast(P))\
                        .then_inc(bc_in[n % BC], 16)
                    if n == 9 and with_next:
                        bc_out(b + 1)

            bc_out(0)
            batches(sp, body)

        @block.gpsimd
        def _(pool):
            norm.start_pool(nc)
            nc.gpsimd.memset(xr[:, :, 0:TAPS - 1], 0.0).then_inc(zeros_set, 1)
            nc.gpsimd.memset(ones[:], 1.0).then_inc(zeros_set, 1)

            def body(b, with_next):
                for k in range(NU):
                    n, f = k // DC, k % DC
                    pool.wait_ge(bc_in[n % BC], b * (NS // BC * 16) + (n // BC * 16 + 16))
                    if k < DC:
                        pool.wait_ge(silu_u, b * DC + k + 2)
                    pool.wait_ge(scanned, b * NU + k + 1)
                    by_itself(pool, pool_waited)
                    nc.gpsimd.tensor_tensor(w_in[:, k % WR], u[:, turn(b), f].rearrange("p a t -> p (a t)"),
                                            bc[:, n % BC, 0], ALU.mult).then_inc(inputs, 1)

            batches(pool, body)

        @block.tensor
        def _(pe):
            norm.start_pe(nc, pe)
            pe.sem_inc(prep_made, 1)
            pe.sem_inc(summed, WR)
            pe.wait_ge(consts_in, CONSTS)
            pe.wait_ge(zeros_set, 2)
            pe.wait_ge(decay_set, 8)
            nc.tensor.matmul(work[0][0:1, 0:1], small_any[:], ones[:, 0:1], start=True, stop=True)\
                .then_inc(small_summed, 1)

            def make(b, i):
                pe.wait_ge(prep_used, b * BANKED + i + 1)
                if i < 2:
                    pe.wait_ge(x_new, b * 4 + 4)
                    pe.wait_ge(norm.normed, b * 2 * DC + (i + 2) * DC)
                if DT <= i < XR:
                    f, h = (i - DT) // 2, (i - DT) % 2
                    pe.wait_ge(prep_used, b * BANKED + 4)
                    mm = nc.tensor.matmul(work[i % 2][:], wdt[:, f * P:(f + 1) * P], par[0:R, h], start=True, stop=True)
                else:
                    if i < DT:
                        h, out, w = i, work[i % 2][0:R + 2 * NS], wpar[:]
                    else:
                        f, h = (i - XR) % 4 // 2, (i - XR) % 2
                        out, w = work[i % 2][:], (wx if i < Z else wz)[:, :, f * P:(f + 1) * P]
                    for c in range(DC):
                        mm = nc.tensor.matmul(out, w[:, c], xn[:, c, h * TW:(h + 1) * TW],
                                              start=(c == 0), stop=(c == DC - 1))
                mm.then_inc(prep_made, 1)

            run = {"mean": lambda b, h: norm.mean(nc, pe, b * 2 + h), "var": lambda b, h: norm.var(nc, pe, b * 2 + h),
                   "make": make}

            def unit(b, k):
                f = k % DC
                if k < DC:
                    pe.wait_ge(gated, b * 8 + 4)
                pe.wait_ge(weighted, b * NU + k + 9)
                for h in range(2):
                    mm = nc.tensor.matmul(y_bank[2 * f + h][:], ident[:], h_out[:, k % WR, h * TW:(h + 1) * TW],
                                          start=(k < DC), stop=(k >= NU - DC))
                mm.then_inc(summed, 1)

            def body(b, with_next):
                for k in range(NU):
                    if k:
                        unit(b, k - 1)
                    if with_next:
                        prepare("pe", run, b + 1, k)
                unit(b, NU - 1)
                pe.wait_ge(gated, b * 8 + 16)
                for q in range(4):
                    c, h = q // 2, q % 2
                    pe.wait_ge(prep_used, (b * BANKED + 2 * BANKED + 2) if with_next else B * BANKED + 2)
                    pe.wait_ge(x_new, b * 4 + q + 7)
                    for f in range(DC):
                        mm = nc.tensor.matmul(work[q % 2][:], wout[:, f, c * P:(c + 1) * P],
                                              u[:, turn(b), f, h * TW:(h + 1) * TW].rearrange("p a t -> p (a t)"),
                                              start=(f == 0), stop=(f == DC - 1))
                    mm.then_inc(out_made, 1)

            prepare("pe", run, 0)
            batches(pe, body)

        @block.scalar
        def _(act):
            act.sem_inc(silu_u, 1)
            norm.start_act(nc, act)
            act.wait_ge(consts_in, CONSTS)
            nc.scalar.activation(a_den, neg_a, ACT.Exp).then_inc(exp_a, 1)
            act.wait_ge(decay_set, 9)
            act.sem_inc(prep_used, 2)

            def use(b, i):
                act.wait_ge(prep_made, b * BANKED + i + 2)
                bank = work[i % 2]
                if i < DT:
                    act.wait_ge(par_out, b * 16 + 16)
                    nc.scalar.activation(par[:, i], bank[0:R + 2 * NS], ACT.Copy).then_inc(prep_used, 1)
                elif i < XR:
                    f, h = (i - DT) // 2, (i - DT) % 2
                    out = dt[:, turn(b), f, h * TW:(h + 1) * TW].rearrange("p a t -> p (a t)")
                    n = b * 12 + 3 * (i - DT)
                    act.wait_ge(soft_dve, b * 16 + 4 * (i - DT) + 1)
                    by_itself(act, act_waited)
                    nc.scalar.activation(exp_part[:], bank[:], ACT.Abs, bias=b_dt[:, f:f + 1]).then_inc(soft_act, 1)
                    nc.scalar.activation(out, bank[:], ACT.Relu, bias=b_dt[:, f:f + 1]).then_inc(prep_used, 1)
                    act.wait_ge(soft_act, n + 1)
                    nc.scalar.activation(exp_part[:], exp_part[:], ACT.Exp, scale=-1.0).then_inc(soft_act, 1)
                    act.wait_ge(soft_act, n + 2)
                    nc.scalar.activation(log_part[:], exp_part[:], ACT.Ln, bias=ones[:, 0:1]).then_inc(soft_act, 1)
                elif i < Z:
                    f, h = (i - XR) // 2, (i - XR) % 2
                    act.wait_ge(conv_step, b * 8 + 1)
                    nc.scalar.activation(xr[:, f, TAPS - 1 + h * TW:TAPS - 1 + (h + 1) * TW], bank[:], ACT.Copy)\
                        .then_inc(prep_used, 1)
                else:
                    f, h = (i - Z) // 2, (i - Z) % 2
                    by_itself(act, act_waited)
                    nc.scalar.activation(sz[:, turn(b), f, h * TW:(h + 1) * TW].rearrange("p a t -> p (a t)"), bank[:],
                                         ACT.Silu).then_inc(prep_used, 1)

            def silu(b, f):
                act.wait_ge(conv_step, b * 8 + 4 * f + 5)
                by_itself(act, act_waited)
                nc.scalar.activation(u[:, turn(b), f].rearrange("p a t -> p (a t)"), cv[:], ACT.Silu).then_inc(silu_u, 1)

            run = {"square": lambda b, h: norm.square(nc, act, b * 2 + h),
                   "guess": lambda b, h: norm.guess(nc, act, b * 2 + h), "use": use, "silu": silu}

            def body(b, with_next):
                for k in range(NU):
                    n, f = k // DC, k % DC
                    if k == 0:
                        act.wait_ge(soft_dve, b * 16 + 17)
                    act.wait_ge(scanned, b * NU + k - AR + 1 + WR)
                    by_itself(act, act_waited)
                    nc.scalar.activation(a_t[:, k % AR], dt[:, turn(b), f].rearrange("p a t -> p (a t)"), ACT.Exp,
                                         scale=a_col[:, f, n:n + 1]).then_inc(decays, 1)
                    if with_next:
                        prepare("act", run, b + 1, k)

            act.wait_ge(zeros_set, 2)
            prepare("act", run, 0)
            batches(act, body)

        @block.vector
        def _(dve):
            norm.start_dve(nc, dve)
            dve.sem_inc(soft_dve, 1)
            dve.sem_inc(conv_step, 1)
            dve.sem_inc(scanned, WR)
            dve.sem_inc(weighted, 8)
            dve.sem_inc(gated, 8)
            dve.sem_inc(x_new, 8)
            dve.wait_ge(consts_in, CONSTS)
            dve.wait_ge(exp_a, 1)
            steps = [
                lambda: nc.vector.tensor_scalar(a_col, a_den, -1.0, None, ALU.mult),
                lambda: nc.vector.tensor_scalar(is_small, a_den, 1e-8, None, ALU.is_lt),
                lambda: nc.vector.tensor_scalar(not_small, is_small, -1.0, 1.0, ALU.mult, ALU.add),
                lambda: nc.vector.scalar_tensor_tensor(a_den, a_col, 1e-10, not_small, ALU.add, ALU.mult),
                lambda: nc.vector.tensor_tensor(a_den, a_den, is_small, ALU.add),
                lambda: nc.vector.reciprocal(a_rec, a_den),
                lambda: nc.vector.tensor_copy(neg_a, is_small),
                lambda: nc.vector.tensor_reduce(small_any[:], neg_a.rearrange("p c n -> p (c n)"), AX_X, ALU.add)]
            for n, step in enumerate(steps):
                if n:
                    dve.wait_ge(decay_set, n)
                step().then_inc(decay_set, 1)
            dve.wait_ge(small_summed, 1)
            nc.vector.tensor_copy(small_int[:], work[0][0:1, 0:1]).then_inc(decay_set, 1)
            dve.wait_ge(decay_set, len(steps) + 1)
            small = dve.value_load(small_int[:])

            def soft(b, i):
                f, h = i // 2, i % 2
                out = dt[:, turn(b), f, h * TW:(h + 1) * TW].rearrange("p a t -> p (a t)")
                n = b * 16 + 4 * i + 1
                dve.wait_ge(soft_act, b * 12 + 3 * i + 3)
                dve.wait_ge(prep_used, b * BANKED + DT + i + 3)
                nc.vector.tensor_tensor(out, out, log_part[:], ALU.add).then_inc(soft_dve, 1)
                dve.wait_ge(soft_dve, n + 1)
                nc.vector.tensor_scalar(log_part[:], exp_part[:], 1.0, 1.0, ALU.add, ALU.subtract).then_inc(soft_dve, 1)
                dve.wait_ge(soft_dve, n + 2)
                nc.vector.tensor_tensor(exp_part[:], exp_part[:], log_part[:], ALU.subtract).then_inc(soft_dve, 1)
                dve.wait_ge(soft_dve, n + 3)
                nc.vector.tensor_tensor(out, out, exp_part[:], ALU.add).then_inc(soft_dve, 1)

            def conv(b, f):
                dve.wait_ge(prep_used, b * BANKED + XR + 2 * f + 4)
                dve.wait_ge(silu_u, b * DC + f + 1)
                if f == 0:
                    dve.wait_ge(zeros_set, 2)
                for tap in range(TAPS):
                    w = conv_w[:, f, tap:tap + 1]
                    if tap == 0:
                        nc.vector.tensor_scalar(cv[:], xr[:, f, 0:S], w, None, ALU.mult).then_inc(conv_step, 1)
                        continue
                    dve.wait_ge(conv_step, b * 8 + 4 * f + tap + 1)
                    nc.vector.scalar_tensor_tensor(cv[:], xr[:, f, tap:tap + S], w, cv[:], ALU.mult, ALU.add)\
                        .then_inc(conv_step, 1)

            run = {"centre": lambda b, h: norm.centre(nc, dve, b * 2 + h), "soft": soft, "conv": conv}

            def finish(b, h):
                dve.wait_ge(prep_made, b * BANKED + 1)
                norm.finish(nc, dve, b * 2 + h, lambda c, t: xn[:, c, h * TW:(h + 1) * TW])

            run["finish"] = finish

            def weigh(b, k):
                n, f = k // DC, k % DC
                dve.wait_ge(scanned, b * NU + k + 1 + WR)
                nc.vector.scalar_tensor_tensor(h_out[:, k % WR], h_out[:, k % WR], a_rec[:, f, n:n + 1], bc[:, n % BC, 1],
                                               ALU.mult, ALU.mult).then_inc(weighted, 1)

            def body(b, with_next):
                for k in range(NU):
                    n, f = k // DC, k % DC
                    dve.wait_ge(decays, b * NU + k + 1)
                    dve.wait_ge(inputs, b * NU + k + 1)
                    dve.wait_ge(summed, b * NU + k + 1)
                    by_itself(dve, dve_waited)
                    with dve.If(small != 0):
                        nc.vector.scalar_tensor_tensor(h_out[:, k % WR], dt[:, turn(b), f].rearrange("p a t -> p (a t)"),
                                                       is_small[:, f, n:n + 1], w_in[:, k % WR], ALU.mult, ALU.mult)
                        dve.drain()
                        nc.vector.scalar_tensor_tensor(w_in[:, k % WR], a_t[:, k % AR], 1.0, w_in[:, k % WR],
                                                       ALU.subtract, ALU.mult)
                        dve.drain()
                        nc.vector.tensor_tensor(w_in[:, k % WR], w_in[:, k % WR], h_out[:, k % WR], ALU.add)\
                            .then_inc(scaled, 1)
                    with dve.Else():
                        nc.vector.scalar_tensor_tensor(w_in[:, k % WR], a_t[:, k % AR], 1.0, w_in[:, k % WR],
                                                       ALU.subtract, ALU.mult).then_inc(scaled, 1)
                    if k:
                        weigh(b, k - 1)
                    dve.wait_ge(scaled, b * NU + k + 1)
                    nc.vector.tensor_tensor_scan(h_out[:, k % WR], a_t[:, k % AR], w_in[:, k % WR], 0.0,
                                                 ALU.mult, ALU.add).then_inc(scanned, 1)
                    if with_next:
                        prepare("dve", run, b + 1, k)
                weigh(b, NU - 1)
                dve.wait_ge(summed, b * NU + NU + WR)
                parts = [(f, h) for f in range(DC) for h in range(2)]
                for f, h in parts:
                    y = u[:, turn(b), f, h * TW:(h + 1) * TW].rearrange("p a t -> p (a t)")
                    nc.vector.scalar_tensor_tensor(y, y, d_par[:, f:f + 1], y_bank[2 * f + h][:], ALU.mult, ALU.add)\
                        .then_inc(gated, 1)
                for i, (f, h) in enumerate(parts):
                    y = u[:, turn(b), f, h * TW:(h + 1) * TW].rearrange("p a t -> p (a t)")
                    z = sz[:, turn(b), f, h * TW:(h + 1) * TW].rearrange("p a t -> p (a t)")
                    dve.wait_ge(gated, b * 8 + i + 9)
                    nc.vector.tensor_tensor(y, y, z, ALU.mult).then_inc(gated, 1)
                for q in range(4):
                    c, h = q // 2, q % 2
                    dve.wait_ge(out_made, b * 4 + q + 1)
                    x = xT[:, c, bass.ds(b * S + h * TW, TW)]
                    nc.vector.tensor_tensor(x, work[q % 2][:], x, ALU.add).then_inc(x_new, 1)

            prepare("dve", run, 0)
            batches(dve, body)


def lay_out(v):
    a = {k: np.asarray(x) for k, x in v.items()}

    def pairs_swapped(w):
        return w.reshape(*w.shape[:-1], D // 2, 2)[..., ::-1].reshape(w.shape)

    def cols(w):
        return w.reshape(DC, P).T

    at, mb = (lambda n: a["L0_attn_a_" + n]), (lambda n: a["L0_attn_b_" + n])
    q = [cols(x) for x in (at("Wq_r_b"), pairs_swapped(at("Wq_r_b")), at("Wu_q_b"))]
    k = [cols(x) for x in (at("Wk_r_b"), pairs_swapped(at("Wk_r_b")), at("Wu_k_b"))]
    bcol = np.stack([at("Wd_q_b"), at("Wd_kv_b")] + [x[:, c] for side in (q, k) for c in range(DC) for x in side], 1)
    theta = np.float32(10000.0) ** (np.float32(-2.0) * np.arange(D // 2, dtype=np.float32)) / np.float32(D // 2)
    angle = np.arange(S, dtype=np.float32)[:, None] * theta.astype(np.float32)[None, :]
    cos, sin = np.cos(angle), np.sin(angle)
    out = {
        "x": at("x"), "ident": np.eye(P, dtype=np.float32),
        "cos": np.repeat(cos.T, 2, axis=0), "sin": np.stack([-sin.T, sin.T], 1).reshape(D, S),
        "Wd_q": at("Wd_q_w"), "Wd_kv": at("Wd_kv_w"), "Wu_q": at("Wu_q_w"), "Wq_r": at("Wq_r_w"),
        "Wq_r_swap": pairs_swapped(at("Wq_r_w")), "Wu_k": at("Wu_k_w"), "Wk_r": at("Wk_r_w"),
        "Wk_r_swap": pairs_swapped(at("Wk_r_w")), "Wu_v": at("Wu_v_w"),
        "bv": np.broadcast_to(at("Wu_v_b"), (P, D)), "bcol_attn": bcol,
        "Wo": at("Wo_w"), "bo": cols(at("Wo_b")),
        "head_of": np.repeat(np.eye(H, dtype=np.float32), HD, axis=1),
        "W_fcT": a["L0_ffn_W_fc"].T, "W_projT": a["L0_ffn_W_proj"].T,
        "W_xT": mb("W_x").T, "W_zT": mb("W_z").T, "W_paramsT": mb("W_params").T, "W_dtT": mb("W_dt").T,
        "W_outT": mb("W_out").T, "conv": mb("conv_w").reshape(D, TAPS), "b_dt": cols(mb("b_dt")),
        "D_param": cols(mb("D_param")), "A_log": mb("A_log"),
    }
    return {k: np.ascontiguousarray(x) for k, x in out.items()}


def program(nc, io, out):
    qk_parts = nc.dram_tensor("qk_parts", (B * 2 * DC, P, 3, S), BF16, kind="Internal").ap()
    o_scr = nc.dram_tensor("o_scr", (B * NG, P, S), F32, kind="Internal").ap()
    recip_scr = nc.dram_tensor("recip_scr", (B * H, S), F32, kind="Internal").ap()
    bc_scr = nc.dram_tensor("bc_scr", (B, 2 * NS, S), F32, kind="Internal").ap()
    with ExitStack() as ctx:
        xT = ctx.enter_context(nc.sbuf_tensor("xT", [P, DC, T], F32))
        with nc.sbuf_tensor("vT", [P, B * NG, QT, G * HD], F32) as vT:
            project(nc, io, xT, vT, qk_parts)
            attend(nc, io, vT, qk_parts, o_scr)
        merge_heads(nc, io, xT, o_scr, recip_scr)
        feed_forward(nc, io, xT, "_f1")
        scan(nc, io, xT, bc_scr)
        feed_forward(nc, io, xT, "_f2")
        emit(nc, io, xT, out)


def kernel(**inputs):
    import concourse.bacc as bacc
    from concourse.bass_utils import run_bass_kernel_spmd as run

    nc = bacc.Bacc("TRN2", target_bir_lowering=False, num_devices=1)
    arrays = {f"in_{name}_dram": a for name, a in lay_out(inputs).items()}
    io = {name[3:-5]: nc.dram_tensor(name, a.shape, mybir.dt.from_np(a.dtype), kind="ExternalInput").ap()
          for name, a in arrays.items()}
    out = nc.dram_tensor("out_0_dram", (B, S, D), F32, kind="ExternalOutput").ap()
    program(nc, io, out)
    return run(nc, [arrays], core_ids=[0]).results[0]["out_0_dram"]
```

```python
import numpy as np
from contextlib import ExitStack

import concourse.bass as bass
from concourse import mybir

F32 = mybir.dt.float32
BF16 = mybir.dt.bfloat16
I32 = mybir.dt.int32
ALU = mybir.AluOpType
ACT = mybir.ActivationFunctionType
AX_X = mybir.AxisListType.X

P = 128
B, S, D = 4, 1024, 256
T = B * S
TW = 512
NT = T // TW
TPB = S // TW
DC = D // P
H = 16
HD = D // H
LAT = 128
G = 4
NG = H // G
QT = S // P
FF = 4 * D
FC = FF // P
R = 64
NS = 16
TAPS = 4
EPS = 1e-5
SOFTMAX_SCALE = 1.0 / float(np.sqrt(np.float32(H + LAT + LAT)))
Q_PARTS = (0, 0, 1, 1, 0, 2)
K_PARTS = (0, 1, 0, 1, 2, 0)
SROWS = len(Q_PARTS) * HD
MROWS = SROWS + 3
STACK_LOAD = 16 * 3 * len(Q_PARTS)
LIF_STEPS, BETA, THRESHOLD = 5, 0.9, 1.0


def spike_thresholds():
    f = np.float32

    def spikes(y):
        mem, count = f(0), 0
        for _ in range(LIF_STEPS):
            reset = f(mem - f(THRESHOLD) > 0)
            mem = f(f(f(f(BETA) * mem) + y) - f(reset * f(THRESHOLD)))
            count += int(mem - f(THRESHOLD) > 0)
        return count

    found = []
    for k in range(1, LIF_STEPS + 1):
        low, high = (int(np.array(v, f).view(np.int32)) for v in (0.0, 64.0))
        while high - low > 1:
            mid = (low + high) // 2
            if spikes(np.array(mid, np.int32).view(f)[()]) >= k:
                high = mid
            else:
                low = mid
        found.append(float(np.array(low, np.int32).view(f)))
    return found


THETA = spike_thresholds()


def by_itself(eng, waited):
    eng.sem_inc(waited, 1)


class Mem:

    def __init__(self, nc, ctx):
        self.nc, self.ctx = nc, ctx

    def sb(self, name, shape, dt=F32):
        return self.ctx.enter_context(self.nc.sbuf_tensor(name, shape, dt))

    def bank(self, name):
        return self.ctx.enter_context(self.nc.psum_tensor(name, [P, TW], F32))

    def sem(self, name):
        return self.ctx.enter_context(self.nc.semaphore(name))


def project(nc, io, xT, vT, split_scr, q_stack, k_stack):
    CHUNKS = 2 * DC
    with ExitStack() as ctx:
        m = Mem(nc, ctx)
        ident = m.sb("ident", [P, P])
        mean_w = m.sb("mean_w", [P, P])
        eps_col = m.sb("eps_col", [P, 1])
        cosT = m.sb("cosT", [P, DC, S])
        sinT = m.sb("sinT", [P, DC, S])
        wdq = m.sb("wdq", [P, DC, LAT])
        wdkv = m.sb("wdkv", [P, DC, LAT])
        wq = m.sb("wq", [P, 3, D])
        wkc = m.sb("wkc", [P, D])
        wkr = m.sb("wkr", [P, 2, DC, D])
        wv = m.sb("wv", [P, D])
        bv = m.sb("bv", [P, D])
        bcol = m.sb("bcol", [P, 14])
        xin = m.sb("xin", [P, 2, TW // P, D])
        xc = m.sb("xc", [P, DC, TW])
        sq = m.sb("sq", [P, DC, TW])
        rs = m.sb("rs", [P, 3, TW])
        xn = m.sb("xn", [P, 2, DC, TW])
        ct = m.sb("ct", [P, 2, TW])
        rot = m.sb("rot", [P, 2, 3, TW])
        full = m.sb("full", [P, CHUNKS, TW])
        rest = m.sb("rest", [P, CHUNKS, TW])
        parts = m.sb("parts", [P, CHUNKS, 3, TW], BF16)
        tr_bank = [m.bank(f"tr_bank{c}") for c in range(DC)]
        mean_bank, var_bank = m.bank("mean_bank"), m.bank("var_bank")
        proj = [m.bank(f"proj{i}") for i in range(4)]

        ident_in, consts_in = m.sem("ident_in"), m.sem("consts_in")
        x_in = [m.sem("x_in0"), m.sem("x_in1")]
        consts_set = m.sem("consts_set")
        transposed, x_kept = m.sem("transposed"), m.sem("x_kept")
        mean_ready, centred, squared = m.sem("mean_ready"), m.sem("centred"), m.sem("squared")
        var_ready, rs_guess, rs_step, normed = m.sem("var_ready"), m.sem("rs_guess"), m.sem("rs_step"), m.sem("normed")
        proj_ready, latent_kept, rotated = m.sem("proj_ready"), m.sem("latent_kept"), m.sem("rotated")
        summed, high_kept, mid_kept = m.sem("summed"), m.sem("high_kept"), m.sem("mid_kept")
        rest_ready, low_kept, v_kept = m.sem("rest_ready"), m.sem("low_kept"), m.sem("v_kept")
        stack_in = m.sem("first_stack_in")
        parts_out = [m.sem(f"parts_out{u}") for u in range(CHUNKS)]

        loads = [(cosT[:], io["cos"].rearrange("(c p) t -> p c t", p=P)),
                 (sinT[:], io["sin"].rearrange("(c p) t -> p c t", p=P)),
                 (wdq[:], io["Wd_q"].rearrange("(c p) n -> p c n", p=P)),
                 (wdkv[:], io["Wd_kv"].rearrange("(c p) n -> p c n", p=P)),
                 (wq[:, 0, :], io["Wu_q"]), (wq[:, 1, :], io["Wq_r"]), (wq[:, 2, :], io["Wq_r_swap"]),
                 (wkc[:], io["Wu_k"]), (wkr[:, 0], io["Wk_r"].rearrange("(c p) n -> p c n", p=P)),
                 (wkr[:, 1], io["Wk_r_swap"].rearrange("(c p) n -> p c n", p=P)),
                 (wv[:], io["Wu_v"]), (bv[:], io["bv"]), (bcol[:], io["bcol_attn"])]
        CONSTS = 16 * len(loads)
        x_dram = io["x"].rearrange("b (i j p) d -> (b i) p j d", j=TW // P, p=P)
        UNITS = 16

        act_waited = m.sem("act_waited_project")
        block = ctx.enter_context(nc.Block())

        @block.sync
        def _(sp):
            for u in range(CHUNKS):
                sp.sem_inc(parts_out[u], 16)
            sp.dma_start(xin[:, 0], x_dram[0]).then_inc(x_in[0], 16)
            sp.dma_start(ident[:], io["ident"]).then_inc(ident_in, 16)
            sp.dma_start(xin[:, 1], x_dram[1]).then_inc(x_in[1], 16)
            for dst, src in loads:
                sp.dma_start(dst, src).then_inc(consts_in, 16)

            def parts_of(b, half, with_loads):
                t = b * 2 + half
                if with_loads:
                    sp.wait_ge(transposed, t * DC + DC)
                    sp.dma_start(xin[:, half], x_dram[bass.ds(t + 2, 1)].rearrange("a p j d -> (a p) j d"))\
                        .then_inc(x_in[half], 16)
                for u in range(CHUNKS):
                    sp.wait_ge(low_kept, t * CHUNKS + u + 1 + CHUNKS)
                    side, c = 1 - u % 2, u // 2
                    sp.dma_start(split_scr[bass.ds(b * DC + (side * B * DC + c), 1), :, :, half * TW:(half + 1) * TW]
                                 .rearrange("a p s t -> (a p) s t"),
                                 parts[:, u]).then_inc(parts_out[u], 16)

            with sp.Fori(0, B - 1) as b:
                parts_of(b, 0, True)
                parts_of(b, 1, True)
            for u in range(CHUNKS):
                sp.wait_ge(parts_out[u], 16 * 2 * (B - 1) + 16)
            load_stack(sp, split_scr, q_stack, k_stack, 0, stack_in)
            parts_of(B - 1, 0, False)
            parts_of(B - 1, 1, False)
            sp.wait_ge(stack_in, STACK_LOAD)
            for u in range(CHUNKS):
                sp.wait_ge(parts_out[u], 16 * NT + 16)

        @block.gpsimd
        def _(pool):
            nc.gpsimd.memset(mean_w[:], 1.0 / D).then_inc(consts_set, 1)
            nc.gpsimd.memset(eps_col[:], EPS).then_inc(consts_set, 1)

        def tiles(eng, body):
            with eng.Fori(0, B - 1) as b:
                body(b, 0, True)
                body(b, 1, True)
            body(B - 1, 0, True)
            body(B - 1, 1, False)

        def following(b, half):
            return (b, 1) if half == 0 else (b + 1, 0)

        @block.tensor
        def _(pe):
            pe.sem_inc(var_ready, 1)
            pe.wait_ge(ident_in, 16)
            pe.wait_ge(consts_set, 2)

            def turn(b, half):
                t = b * 2 + half
                pe.wait_ge(x_in[half], b * 16 + 16)
                for c in range(DC):
                    pe.wait_ge(x_kept, t * DC + c + 1)
                    for j in range(TW // P):
                        mm = nc.tensor.transpose(tr_bank[c][:, j * P:(j + 1) * P],
                                                 xin[:, half, j, c * P:(c + 1) * P], ident[:])
                    mm.then_inc(transposed, 1)

            def mean(b, half):
                t = b * 2 + half
                pe.wait_ge(x_kept, t * DC + 2 * DC)
                pe.wait_ge(centred, t * DC + DC)
                for c in range(DC):
                    mm = nc.tensor.matmul(mean_bank[:], mean_w[:], xT[:, c, bass.ds(t * TW, TW)],
                                          start=(c == 0), stop=(c == DC - 1))
                mm.then_inc(mean_ready, 1)

            def var(b, half):
                t = b * 2 + half
                pe.wait_ge(squared, t * DC + DC)
                pe.wait_ge(rs_step, t * 3 + 1)
                for c in range(DC):
                    mm = nc.tensor.matmul(var_bank[:], mean_w[:], sq[:, c], start=(c == 0), stop=(c == DC - 1))
                mm.then_inc(var_ready, 1)

            def project_unit(t, half, u):
                if u < 2:
                    pe.wait_ge(rotated, t * 12 + u + 1)
                elif u < 4:
                    pe.wait_ge(v_kept, t * 2 + u - 1)
                elif u < 6:
                    pe.wait_ge(latent_kept, t * 2 + u - 3)
                else:
                    pe.wait_ge(rotated, t * 12 + u - 3)
                side, c, kind = 1 - (u - 2) // 3 % 2, (u - 2) // 6, (1, 2, 0)[(u - 2) % 3]
                if u == 4:
                    pe.wait_ge(latent_kept, t * 2 + 2)
                bank = proj[u % 4]
                if u < 2:
                    products = [(bank[:], (wdq, wdkv)[u][:, k], xn[:, half, k]) for k in range(DC)]
                elif u >= 14:
                    for j in range(2):
                        tok = slice((2 * (u - 14) + j) * P, (2 * (u - 14) + j + 1) * P)
                        mm = nc.tensor.matmul(bank[:, j * D:(j + 1) * D], ct[:, 1, tok], wv[:], start=True, stop=True)
                    mm.then_inc(proj_ready, 1)
                    return
                else:
                    cols = slice(c * P, (c + 1) * P)
                    if side == 0:
                        products = [(bank[:], wq[:, kind, cols], ct[:, 0])]
                    elif kind == 0:
                        products = [(bank[:], wkc[:, cols], ct[:, 1])]
                    else:
                        products = [(bank[:], wkr[:, kind - 1, k, cols], xn[:, half, k]) for k in range(DC)]
                for k, (to, w, x) in enumerate(products):
                    mm = nc.tensor.matmul(to, w, x, start=(k == 0), stop=(k == len(products) - 1))
                mm.then_inc(proj_ready, 1)

            def tile(b, half, with_next):
                t = b * 2 + half
                pe.wait_ge(normed, t * DC + DC)
                for u in range(UNITS):
                    project_unit(t, half, u)
                    if with_next and u == 1:
                        turn(*following(b, half))
                    if with_next and u == 2:
                        mean(*following(b, half))
                    if with_next and u == 5:
                        var(*following(b, half))

            turn(0, 0)
            mean(0, 0)
            var(0, 0)
            pe.wait_ge(consts_in, CONSTS)
            tiles(pe, tile)

        @block.scalar
        def _(act):
            nc.scalar.sem_inc(x_kept, DC)
            act.wait_ge(consts_set, 2)

            def keep_x(b, half):
                t = b * 2 + half
                for c in range(DC):
                    act.wait_ge(transposed, t * DC + c + 1)
                    by_itself(act, act_waited)
                    nc.scalar.activation(xT[:, c, bass.ds(t * TW, TW)], tr_bank[c][:], ACT.Copy).then_inc(x_kept, 1)

            def square(b, half):
                t = b * 2 + half
                for c in range(DC):
                    act.wait_ge(centred, t * DC + DC + c + 1)
                    act.wait_ge(var_ready, t + 1)
                    nc.scalar.activation(sq[:, c], xc[:, c], ACT.Square).then_inc(squared, 1)

            def guess(b, half):
                t = b * 2 + half
                act.wait_ge(var_ready, t + 2)
                act.wait_ge(rs_step, t * 3 + 1)
                nc.scalar.activation(rs[:, 1], var_bank[:], ACT.Ln, bias=eps_col[:]).then_inc(rs_guess, 1)
                act.wait_ge(rs_guess, t * 2 + 1)
                nc.scalar.activation(rs[:, 0], rs[:, 1], ACT.Exp, scale=-0.5).then_inc(rs_guess, 1)

            def high(t, u):
                act.wait_ge(summed, t * CHUNKS + u + 3)
                act.wait_ge(parts_out[u], t * 16 + 16)
                nc.scalar.activation(parts[:, u, 0], full[:, u], ACT.Copy).then_inc(high_kept, 1)

            def middle(t, u):
                act.wait_ge(rest_ready, t * CHUNKS + u + 1)
                nc.scalar.activation(parts[:, u, 1], rest[:, u], ACT.Copy).then_inc(mid_kept, 1)

            def tile(b, half, with_next):
                t = b * 2 + half
                for u in range(2):
                    act.wait_ge(proj_ready, t * UNITS + u + 1)
                    nc.scalar.activation(ct[:, u], proj[u][:], ACT.Identity, bias=bcol[:, u:u + 1])\
                        .then_inc(latent_kept, 1)
                if with_next:
                    keep_x(*following(b, half))
                    square(*following(b, half))
                high(t, 0)
                if with_next:
                    guess(*following(b, half))
                high(t, 1)
                middle(t, 0)
                high(t, 2)
                middle(t, 1)
                high(t, 3)
                middle(t, 2)
                middle(t, 3)

            keep_x(0, 0)
            square(0, 0)
            guess(0, 0)
            act.wait_ge(consts_in, CONSTS)
            tiles(act, tile)

        @block.vector
        def _(dve):
            nc.vector.sem_inc(centred, DC)
            nc.vector.sem_inc(rs_step, 1)
            nc.vector.sem_inc(rotated, 2)
            nc.vector.sem_inc(v_kept, 2)
            nc.vector.sem_inc(summed, 2)
            nc.vector.sem_inc(low_kept, CHUNKS)

            def centre(b, half):
                t = b * 2 + half
                dve.wait_ge(mean_ready, t + 1)
                for c in range(DC):
                    nc.vector.tensor_tensor(xc[:, c], xT[:, c, bass.ds(t * TW, TW)], mean_bank[:], ALU.subtract)\
                        .then_inc(centred, 1)

            def finish(b, half):
                t = b * 2 + half
                dve.wait_ge(rs_guess, t * 2 + 2)
                nc.vector.scalar_tensor_tensor(rs[:, 1], var_bank[:], EPS, rs[:, 0], ALU.add, ALU.mult)\
                    .then_inc(rs_step, 1)
                dve.wait_ge(rs_step, t * 3 + 2)
                nc.vector.scalar_tensor_tensor(rs[:, 2], rs[:, 1], -0.5, rs[:, 0], ALU.mult, ALU.mult)\
                    .then_inc(rs_step, 1)
                dve.wait_ge(rs_step, t * 3 + 3)
                nc.vector.scalar_tensor_tensor(rs[:, 1], rs[:, 2], 1.5, rs[:, 0], ALU.add, ALU.mult)\
                    .then_inc(rs_step, 1)
                dve.wait_ge(rs_step, t * 3 + 4)
                for c in range(DC):
                    nc.vector.tensor_tensor(xn[:, half, c], xc[:, c], rs[:, 1], ALU.mult).then_inc(normed, 1)

            def rotate(t, half, u):
                side, c = 1 - u % 2, u // 2
                n = t * 12 + 3 * u + 2
                bias = bcol[:, 2 + 6 * side + 3 * c:5 + 6 * side + 3 * c]
                banks = [proj[(2 + 3 * u + i) % 4] for i in range(3)]
                r = rot[:, u % 2]
                dve.wait_ge(summed, t * CHUNKS + u + 1)
                for i, table in enumerate((cosT, sinT)):
                    dve.wait_ge(proj_ready, t * UNITS + 3 + 3 * u + i)
                    nc.vector.scalar_tensor_tensor(r[:, i], banks[i][:], bias[:, i:i + 1],
                                                   table[:, c, half * TW:(half + 1) * TW], ALU.add, ALU.mult)\
                        .then_inc(rotated, 1)
                dve.wait_ge(proj_ready, t * UNITS + 5 + 3 * u)
                dve.wait_ge(rotated, n + 1)
                nc.vector.scalar_tensor_tensor(r[:, 2], banks[2][:], bias[:, 2:3], r[:, 0], ALU.add, ALU.add)\
                    .then_inc(rotated, 1)
                dve.wait_ge(rotated, n + 3)
                nc.vector.tensor_tensor(full[:, u], r[:, 2], r[:, 1], ALU.add).then_inc(summed, 1)

            def leave_rest(t, u):
                dve.wait_ge(high_kept, t * CHUNKS + u + 1)
                dve.wait_ge(low_kept, t * CHUNKS + u + 1)
                nc.vector.tensor_tensor(rest[:, u], full[:, u], parts[:, u, 0], ALU.subtract).then_inc(rest_ready, 1)

            def low(t, u):
                dve.wait_ge(mid_kept, t * CHUNKS + u + 1)
                nc.vector.tensor_tensor(parts[:, u, 2], rest[:, u], parts[:, u, 1], ALU.subtract).then_inc(low_kept, 1)

            def keep_v(b, half, t, pair):
                dve.wait_ge(proj_ready, t * UNITS + 15 + pair)
                for j in range(2):
                    ins = nc.vector.tensor_tensor(vT[:, bass.ds(b * NG, NG), half * 4 + 2 * pair + j, :],
                                                  proj[2 + pair][:, j * D:(j + 1) * D].rearrange("p (g n) -> p g n", g=NG),
                                                  bv[:].rearrange("p (g n) -> p g n", g=NG), ALU.add)
                ins.then_inc(v_kept, 1)

            def tile(b, half, with_next):
                t = b * 2 + half
                if with_next:
                    centre(*following(b, half))
                rotate(t, half, 0)
                rotate(t, half, 1)
                leave_rest(t, 0)
                if with_next:
                    finish(*following(b, half))
                rotate(t, half, 2)
                leave_rest(t, 1)
                low(t, 0)
                rotate(t, half, 3)
                leave_rest(t, 2)
                low(t, 1)
                keep_v(b, half, t, 0)
                keep_v(b, half, t, 1)
                leave_rest(t, 3)
                low(t, 2)
                low(t, 3)

            centre(0, 0)
            finish(0, 0)
            dve.wait_ge(consts_in, CONSTS)
            tiles(dve, tile)


def load_stack(eng, split_scr, q, k, g, done):
    heads = split_scr.rearrange("a (h n) s t -> (a h) n s t", h=2)
    q_in, k_in = (heads[bass.ds(g + side * B * NG, 1)].rearrange("a (j i) s t -> (a i) j s t", i=HD) for side in range(2))
    for n in range(len(Q_PARTS)):
        rows = slice(n * HD, (n + 1) * HD)
        eng.dma_start(k[rows], k_in[:, :, K_PARTS[n], :]).then_inc(done, 16)
        for h in range(2):
            eng.dma_start(q[rows, h], q_in[:, :, Q_PARTS[n], h * TW:(h + 1) * TW]).then_inc(done, 16)


def attend(nc, io, vT, split_scr, q_stack, k_stack, o_scr):
    NGT = B * NG
    UNITS = G * QT * 2
    HU = UNITS // 2
    STEPS = 2 * QT
    MB = 3
    TURN_NOW, TURN_NEXT = 2, 10
    with ExitStack() as ctx:
        m = Mem(nc, ctx)
        qs = [q_stack] + [m.sb(f"qs{i}", [P, 2, G, TW], BF16) for i in (1, 2)]
        ks = [k_stack] + [m.sb(f"ks{i}", [P, G, S], BF16) for i in (1, 2)]
        vg = [m.sb(f"vg{i}", [P, QT, G, 2 * HD]) for i in range(3)]
        ident = m.sb("ident_a", [P, P])
        probs = m.sb("probs", [P, 2, G, TW])
        mx = m.sb("mx", [P, 2, HU])
        row_max = m.sb("row_max", [P, 2, HU // 2])
        neg_max = m.sb("neg_max", [HU // 2, 2, P])
        neg_rest = m.sb("neg_rest", [HU // 2, 2, P])
        neg_parts = m.sb("neg_parts", [HU // 2, 2, 3, P], BF16)
        o_sb = m.sb("o_sb", [P, 2, TW])
        max_bank = [m.bank(f"max_bank{i}") for i in range(MB)]
        score_bank = [m.ctx.enter_context(nc.psum_tensor(f"score_bank{i}", [P, 2, TW], F32)) for i in range(2)]
        o_bank = m.bank("o_bank")

        ident_in, ones_set, v_set = m.sem("ident_in"), m.sem("ones_set"), m.sem("v_set")
        stack_in = [m.sem(f"stack_in{i}") for i in range(3)]
        max_ready, reduced, row_max_ready = m.sem("max_ready"), m.sem("reduced"), m.sem("row_max_ready")
        turned, neg_ready, neg_split = m.sem("turned"), m.sem("neg_ready"), m.sem("neg_split")
        max_rows_in = [m.sem(f"max_rows_in{i}") for i in range(2)]
        scores_ready, probs_ready, pv_done = m.sem("scores_ready"), m.sem("probs_ready"), m.sem("pv_done")
        o_kept = m.sem("o_kept")
        o_out = [m.sem(f"o_out{i}") for i in range(2)]

        pool_waited = m.sem("pool_waited_attend")
        block = ctx.enter_context(nc.Block())

        def turn_bank(r, s):
            return max_bank[(r + 1 + 4 * (s + 1)) % MB]

        def groups(eng, body):
            with eng.Fori(0, (NGT - 1) // 3) as it:
                for r in range(3):
                    body(it * 3 + r, r, it, True)
            body(NGT - 1, (NGT - 1) % 3, (NGT - 1) // 3, False)

        @block.sync
        def _(sp):
            for h in range(2):
                sp.sem_inc(max_rows_in[h], 16)
                sp.sem_inc(o_out[h], 16)

            def load(g, r):
                load_stack(sp, split_scr, qs[r], ks[r], g, stack_in[r])

            def max_rows(g, r, h):
                sp.wait_ge(neg_split, g * 8 + 4 * h + 12)
                for part in range(3):
                    sp.dma_start(qs[r][SROWS + part:SROWS + part + 1, h], neg_parts[:, h, part, :]).then_inc(max_rows_in[h], 16)

            def o_to_dram(g, h):
                sp.wait_ge(o_kept, g * 2 + h + 3)
                sp.dma_start(o_scr[bass.ds(g, 1), :, h * TW:(h + 1) * TW].rearrange("a p t -> (a p) t"), o_sb[:, h])\
                    .then_inc(o_out[h], 16)

            def body(g, r, with_next=True, with_load=True):
                max_rows(g, r, 1)
                if with_load:
                    sp.wait_ge(scores_ready, g * 2 * STEPS + 1)
                    load(g + 2, (r + 2) % 3)
                if with_next:
                    max_rows(g + 1, (r + 1) % 3, 0)
                o_to_dram(g, 0)
                o_to_dram(g, 1)

            sp.dma_start(ident[:], io["ident"]).then_inc(ident_in, 16)
            sp.sem_inc(stack_in[0], STACK_LOAD)
            load(1, 1)
            max_rows(0, 0, 0)
            with sp.Fori(0, (NGT - 4) // 3) as it:
                for r in range(3):
                    body(it * 3 + r, r)
            for g in range((NGT - 4) // 3 * 3, NGT):
                body(g, g % 3, g < NGT - 1, g < NGT - 2)
            for h in range(2):
                sp.wait_ge(o_out[h], 16 * NGT + 16)

        @block.gpsimd
        def _(pool):
            pool.sem_inc(neg_split, 8)
            for i in range(3):
                nc.gpsimd.memset(ks[i][SROWS:MROWS], 1.0).then_inc(ones_set, 1)
                pool.wait_ge(ones_set, 2 * i + 1)
                nc.gpsimd.memset(vg[i][:, :, :, HD:], 1.0).then_inc(ones_set, 1)
                pool.wait_ge(ones_set, 2 * i + 2)

            def v_of(g, r):
                pool.wait_ge(pv_done, g * STEPS + STEPS)
                by_itself(pool, pool_waited)
                nc.gpsimd.tensor_copy(vg[r][:, :, :, 0:HD], vT[:, bass.ds(g, 1), :, :]
                                      .rearrange("p a k (j i) -> p (a k) j i", i=HD)).then_inc(v_set, 1)

            def split(g, h):
                n = g * 8 + 4 * h + 8
                pool.wait_ge(neg_ready, g * 2 + h + 1)
                pool.wait_ge(max_rows_in[h], g * 48 + 16)
                by_itself(pool, pool_waited)
                nc.gpsimd.tensor_copy(neg_parts[:, h, 0], neg_max[:, h]).then_inc(neg_split, 1)
                pool.wait_ge(neg_split, n + 1)
                nc.gpsimd.tensor_tensor(neg_rest[:, h], neg_max[:, h], neg_parts[:, h, 0], ALU.subtract)\
                    .then_inc(neg_split, 1)
                pool.wait_ge(neg_split, n + 2)
                by_itself(pool, pool_waited)
                nc.gpsimd.tensor_copy(neg_parts[:, h, 1], neg_rest[:, h]).then_inc(neg_split, 1)
                pool.wait_ge(neg_split, n + 3)
                nc.gpsimd.tensor_tensor(neg_parts[:, h, 2], neg_rest[:, h], neg_parts[:, h, 1], ALU.subtract)\
                    .then_inc(neg_split, 1)

            def body(g, r, it, with_next):
                split(g, 1)
                if with_next:
                    v_of(g + 1, (r + 1) % 3)
                    split(g + 1, 0)

            pool.wait_ge(ones_set, 6)
            v_of(0, 0)
            split(0, 0)
            groups(pool, body)

        @block.tensor
        def _(pe):
            pe.sem_inc(scores_ready, 1)
            pe.sem_inc(pv_done, 3 * STEPS)

            def for_max(g, r, a):
                half, j, qt, kh = a // HU, a % HU // 8, a % 8 // 2, a % 2
                pe.wait_ge(reduced, g * UNITS + a + 1)
                nc.tensor.matmul(max_bank[(r + a) % MB][:], qs[r][0:SROWS, half, j, qt * P:(qt + 1) * P],
                                 ks[r][0:SROWS, j, kh * TW:(kh + 1) * TW], start=True, stop=True)\
                    .then_inc(max_ready, 1)

            def turn(g, h, bank):
                pe.wait_ge(row_max_ready, g * 2 + h + 1)
                nc.tensor.transpose(bank[0:HU // 2, 0:P], row_max[:, h], ident[:]).then_inc(turned, 1)

            def scores(g, r, s, pair):
                pe.wait_ge(probs_ready, g * 2 * STEPS + 2 * s + pair + 1)
                qh, kt = s // QT, s % QT
                for j in (2 * pair, 2 * pair + 1):
                    mm = nc.tensor.matmul(score_bank[pair][:, j % 2], ks[r][0:MROWS, j, kt * P:(kt + 1) * P],
                                          qs[r][0:MROWS, qh, j, :], start=True, stop=True)
                mm.then_inc(scores_ready, 1)

            def body(g, r, it, with_next):
                for s in range(STEPS):
                    if s % QT == 0:
                        pe.wait_ge(max_rows_in[s // QT], g * 48 + 64)
                    if s == 0 and with_next:
                        pe.wait_ge(stack_in[(r + 1) % 3], it * STACK_LOAD + STACK_LOAD * (1 + (r + 1) // 3))
                    for pair in range(2):
                        scores(g, r, s, pair)
                        if with_next:
                            if s in (TURN_NOW + 1, TURN_NEXT + 1) and pair == 0:
                                pe.wait_ge(neg_ready, g * 2 + (2 if s == TURN_NOW + 1 else 3))
                            for_max(g + 1, (r + 1) % 3, 4 * s + pair)
                    if with_next:
                        for_max(g + 1, (r + 1) % 3, 4 * s + 2)
                    if s > 0:
                        pv(g, r, s - 1)
                    elif r > 0:
                        pv(g - 1, r - 1, STEPS - 1)
                    if s == TURN_NOW or s == TURN_NEXT and with_next:
                        if with_next:
                            pe.wait_ge(reduced, g * UNITS + UNITS + 4 * s + 2 + MB)
                        turn(g if s == TURN_NOW else g + 1, 1 if s == TURN_NOW else 0, turn_bank(r, s))
                    if with_next:
                        for_max(g + 1, (r + 1) % 3, 4 * s + 3)
                if r == 2 or not with_next:
                    pv(g, r, STEPS - 1)

            def pv(g, r, s):
                qh, kt = s // QT, s % QT
                if s == 0:
                    pe.wait_ge(v_set, g + 1)
                if kt == 0:
                    pe.wait_ge(o_kept, g * 2 + qh + 2)
                pe.wait_ge(probs_ready, g * 2 * STEPS + 2 * s + 4)
                for j in range(G):
                    mm = nc.tensor.matmul(o_bank[32 * j:32 * j + 32, :], vg[r][:, kt, j], probs[:, s % 2, j],
                                          start=(kt == 0), stop=(kt == QT - 1))
                mm.then_inc(pv_done, 1)

            pe.wait_ge(stack_in[0], STACK_LOAD)
            for n in range(HU):
                half, j, qt = n // (HU // 2), n % (HU // 2) // 4, n % 4
                if n > 1:
                    pe.wait_ge(reduced, 2 * (n - 1) + MB)
                for kh in range(2):
                    mm = nc.tensor.matmul(score_bank[n % 2][:, kh], qs[0][0:SROWS, half, j, qt * P:(qt + 1) * P],
                                          ks[0][0:SROWS, j, kh * TW:(kh + 1) * TW], start=True, stop=True)
                mm.then_inc(max_ready, 2)
                if n == HU // 2 + 2:
                    pe.wait_ge(ident_in, 16)
                    turn(0, 0, max_bank[0])
            pe.wait_ge(neg_ready, 1)
            pe.wait_ge(reduced, UNITS + MB)
            pe.wait_ge(ones_set, 6)
            groups(pe, body)

        @block.scalar
        def _(act):
            act.sem_inc(probs_ready, 2)

            def body(g, r, it, with_next):
                for s in range(STEPS):
                    act.wait_ge(pv_done, g * STEPS + (3 * STEPS + s - 1))
                    for pair in range(2):
                        act.wait_ge(scores_ready, g * 2 * STEPS + 2 * s + pair + 2)
                        nc.scalar.activation(probs[:, s % 2, 2 * pair:2 * pair + 2], score_bank[pair][:], ACT.Exp,
                                             scale=SOFTMAX_SCALE).then_inc(probs_ready, 1)

            groups(act, body)

        @block.vector
        def _(dve):
            dve.sem_inc(reduced, MB)
            dve.sem_inc(o_kept, 2)

            def maximum(g, r, a):
                dve.wait_ge(max_ready, g * UNITS + a + 1)
                nc.vector.tensor_reduce(mx[:, a // HU, a % HU:a % HU + 1], max_bank[(r + a) % MB][:], AX_X, ALU.max)\
                    .then_inc(reduced, 1)

            def both_halves(g, h):
                dve.wait_ge(reduced, g * UNITS + (h + 1) * HU + MB)
                nc.vector.tensor_reduce(row_max[:, h], mx[:, h].rearrange("p (u k) -> p u k", k=2), AX_X, ALU.max)\
                    .then_inc(row_max_ready, 1)

            def negate(g, h, bank):
                dve.wait_ge(turned, g * 2 + h + 1)
                dve.wait_ge(neg_split, g * 8 + 4 * h + 4)
                nc.vector.tensor_scalar(neg_max[:, h], bank[0:HU // 2, 0:P], -1.0, None, ALU.mult)\
                    .then_inc(neg_ready, 1)

            def keep_o(g, qh):
                dve.wait_ge(pv_done, g * STEPS + (3 * STEPS + (qh + 1) * QT))
                dve.wait_ge(o_out[qh], g * 16 + 16)
                nc.vector.tensor_copy(o_sb[:, qh], o_bank[:]).then_inc(o_kept, 1)

            def body(g, r, it, with_next):
                for s in range(STEPS):
                    for i in range(4):
                        if i == 3 and s == TURN_NOW:
                            negate(g, 1, turn_bank(r, s))
                        if i == 3 and s == TURN_NEXT and with_next:
                            negate(g + 1, 0, turn_bank(r, s))
                        if i == 3 and s == 0 and r > 0:
                            keep_o(g - 1, 1)
                        if i == 3 and s == QT:
                            keep_o(g, 0)
                        if with_next:
                            maximum(g + 1, (r + 1) % 3, 4 * s + i)
                    if s == QT - 1 and with_next:
                        both_halves(g + 1, 0)
                if with_next:
                    both_halves(g + 1, 1)
                if r == 2 or not with_next:
                    keep_o(g, 1)

            for n in range(HU):
                half, i = n // (HU // 2), n % (HU // 2)
                dve.wait_ge(max_ready, 2 * n + 2)
                nc.vector.tensor_reduce(row_max[:, half, i:i + 1], score_bank[n % 2][:].rearrange("p a t -> p (a t)"),
                                        AX_X, ALU.max).then_inc(reduced, 2)
                if i == HU // 2 - 1:
                    dve.wait_ge(reduced, 2 * n + 2 + MB)
                    nc.vector.sem_inc(row_max_ready, 1)
                if n == HU // 2 + 3:
                    negate(0, 0, max_bank[0])
            groups(dve, body)


class Norm:

    def __init__(self, m, xT, xn_at, tag, done=0):
        self.xT, self.xn_at, self.done = xT, xn_at, done
        self.mean_w, self.eps_col = m.sb("mean_w" + tag, [P, P]), m.sb("eps_col" + tag, [P, 1])
        self.xc, self.sq = m.sb("xc" + tag, [P, DC, TW]), m.sb("sq" + tag, [P, DC, TW])
        self.rs = self.sq
        self.mean_bank, self.var_bank = m.bank("mean_bank" + tag), m.bank("var_bank" + tag)
        self.set, self.mean_ready, self.centred, self.squared, self.var_ready, self.guessed, self.stepped, self.normed = (
            m.sem(n + tag) for n in ("norm_set", "mean_ready", "centred", "squared", "var_ready", "guessed",
                                     "stepped", "normed"))

    def tile(self, c, t, at):
        return self.xT[:, c, bass.ds((t if at is None else at) * TW, TW)]

    def start_pool(self, nc):
        nc.gpsimd.memset(self.mean_w[:], 1.0 / D).then_inc(self.set, 1)
        nc.gpsimd.memset(self.eps_col[:], EPS).then_inc(self.set, 1)

    def start_pe(self, nc, pe):
        pe.sem_inc(self.var_ready, 1 + self.done)
        if self.done:
            pe.sem_inc(self.mean_ready, self.done)
        pe.wait_ge(self.set, 2)

    def start_dve(self, nc, dve):
        dve.sem_inc(self.centred, DC + self.done * DC)
        dve.sem_inc(self.stepped, 1 + self.done * 3)
        dve.sem_inc(self.normed, DC + self.done * DC)

    def start_act(self, nc, act):
        if self.done:
            act.sem_inc(self.squared, self.done * DC)
            act.sem_inc(self.guessed, self.done * 2)
        act.wait_ge(self.set, 2)

    def mean(self, nc, pe, t, at=None):
        pe.wait_ge(self.centred, t * DC + DC)
        for c in range(DC):
            mm = nc.tensor.matmul(self.mean_bank[:], self.mean_w[:], self.tile(c, t, at), start=(c == 0), stop=(c == DC - 1))
        mm.then_inc(self.mean_ready, 1)

    def centre(self, nc, dve, t, at=None):
        dve.wait_ge(self.mean_ready, t + 1)
        dve.wait_ge(self.normed, t * DC + DC)
        for c in range(DC):
            nc.vector.tensor_tensor(self.xc[:, c], self.tile(c, t, at), self.mean_bank[:], ALU.subtract)\
                .then_inc(self.centred, 1)

    def square(self, nc, act, t):
        act.wait_ge(self.var_ready, t + 1)
        for c in range(DC):
            act.wait_ge(self.centred, t * DC + DC + c + 1)
            nc.scalar.activation(self.sq[:, c], self.xc[:, c], ACT.Square).then_inc(self.squared, 1)

    def var(self, nc, pe, t):
        pe.wait_ge(self.squared, t * DC + DC)
        pe.wait_ge(self.stepped, t * 3 + 1)
        for c in range(DC):
            mm = nc.tensor.matmul(self.var_bank[:], self.mean_w[:], self.sq[:, c], start=(c == 0), stop=(c == DC - 1))
        mm.then_inc(self.var_ready, 1)

    def guess(self, nc, act, t):
        act.wait_ge(self.var_ready, t + 2)
        act.wait_ge(self.stepped, t * 3 + 1)
        nc.scalar.activation(self.rs[:, 1], self.var_bank[:], ACT.Ln, bias=self.eps_col[:]).then_inc(self.guessed, 1)
        act.wait_ge(self.guessed, t * 2 + 1)
        nc.scalar.activation(self.rs[:, 0], self.rs[:, 1], ACT.Exp, scale=-0.5).then_inc(self.guessed, 1)

    def finish(self, nc, dve, t, xn_at=None):
        rs = self.rs
        dve.wait_ge(self.guessed, t * 2 + 2)
        nc.vector.scalar_tensor_tensor(rs[:, 1], self.var_bank[:], EPS, rs[:, 0], ALU.add, ALU.mult)\
            .then_inc(self.stepped, 1)
        dve.wait_ge(self.stepped, t * 3 + 2)
        nc.vector.scalar_tensor_tensor(rs[:, 1], rs[:, 1], -0.5, rs[:, 0], ALU.mult, ALU.mult)\
            .then_inc(self.stepped, 1)
        dve.wait_ge(self.stepped, t * 3 + 3)
        nc.vector.scalar_tensor_tensor(rs[:, 1], rs[:, 1], 1.5, rs[:, 0], ALU.add, ALU.mult).then_inc(self.stepped, 1)
        dve.wait_ge(self.stepped, t * 3 + 4)
        for c in range(DC):
            nc.vector.tensor_tensor((xn_at or self.xn_at)(c, t), self.xc[:, c], rs[:, 1], ALU.mult).then_inc(self.normed, 1)


def merge_heads(nc, io, xT, o_scr, recip_scr, xn, more_loads):
    with ExitStack() as ctx:
        m = Mem(nc, ctx)
        wo = m.sb("wo", [P, DC, D])
        bo = m.sb("bo", [P, DC])
        head_of = m.sb("head_of", [H, D])
        sums = m.sb("sums", [P, TW])
        recips = m.sb("recips", [P, TW])
        by_head = m.sb("by_head", [H, B, S])
        o_in = m.sb("o_in", [P, 2, DC, TW])
        o_n = m.sb("o_n", [P, 2, DC, TW])
        recip_bank = [m.bank(f"recip_bank{c}") for c in range(DC)]
        out_bank = [m.bank(f"out_bank{c}") for c in range(DC)]
        norm = Norm(m, xT, lambda c, t: xn[:, c, 0:TW], "_mh")
        more_in = m.sem("more_in_mh")
        consts_in, sums_in, recips_out, by_head_in = (m.sem(n) for n in ("mh_consts", "sums_in", "recips_out", "by_head_in"))
        heads_in = [m.sem(f"heads_in{i}") for i in range(2)]
        recips_ready, spread, divided, out_ready, x_new = (m.sem(n) for n in ("recips_ready", "spread", "divided", "out_ready", "mh_x_new"))
        by_rows = o_scr.rearrange("g (j r) t -> (g j) r t", r=2 * HD)
        pe_waited = m.sem("pe_waited_merge_heads")
        block = ctx.enter_context(nc.Block())

        @block.sync
        def _(sp):
            sp.dma_start(sums[:], by_rows[:, HD, :].rearrange("g (h t) -> g h t", t=TW)).then_inc(sums_in, 16)
            for dst, src in ((wo[:], io["Wo"].rearrange("(c p) n -> p c n", p=P)), (bo[:], io["bo"]), (head_of[:], io["head_of"])):
                sp.dma_start(dst, src).then_inc(consts_in, 16)

            def load(b, half):
                for c in range(DC):
                    sp.dma_start(o_in[:, half, c, :],
                                 by_rows[bass.ds(b * H + c * (H // DC), H // DC), 0:HD, half * TW:(half + 1) * TW])\
                        .then_inc(heads_in[half], 16)

            load(0, 0)
            load(0, 1)
            sp.wait_ge(recips_ready, 1)
            sp.dma_start(recip_scr.rearrange("g (h t) -> (g h) t", t=TW), recips[:]).then_inc(recips_out, 16)
            sp.wait_ge(recips_out, 16)
            sp.dma_start(by_head[:], recip_scr.rearrange("(b h) t -> h b t", h=H)).then_inc(by_head_in, 16)
            with sp.Fori(1, B) as b:
                for half in range(2):
                    sp.wait_ge(divided, b * 2 * DC + half * DC)
                    load(b, half)
            for dst, src in more_loads:
                sp.dma_start(dst, src).then_inc(more_in, 16)
            sp.wait_ge(more_in, 16 * len(more_loads))

        @block.tensor
        def _(pe):
            pe.wait_ge(consts_in, 48)
            pe.wait_ge(by_head_in, 16)

            def tile(b, half):
                t = b * 2 + half
                for c in range(DC):
                    pe.wait_ge(divided, t * DC + c + 1)
                    by_itself(pe, pe_waited)
                    nc.tensor.matmul(recip_bank[c][:], head_of[:, c * P:(c + 1) * P],
                                     by_head[:, bass.ds(b, 1), half * TW:(half + 1) * TW].rearrange("h a t -> h (a t)"),
                                     start=True, stop=True).then_inc(spread, 1)
                pe.wait_ge(divided, t * DC + 2 * DC)
                for c in range(DC):
                    pe.wait_ge(x_new, t * DC + c + 1)
                    for k in range(DC):
                        mm = nc.tensor.matmul(out_bank[c][:], wo[:, k, c * P:(c + 1) * P], o_n[:, half, k],
                                              start=(k == 0), stop=(k == DC - 1))
                    mm.then_inc(out_ready, 1)

            with pe.Fori(0, B - 1) as b:
                tile(b, 0)
                tile(b, 1)
            norm.start_pe(nc, pe)
            norm.mean(nc, pe, 0)
            tile(B - 1, 0)
            norm.var(nc, pe, 0)
            tile(B - 1, 1)

        @block.gpsimd
        def _(pool):
            norm.start_pool(nc)

        @block.scalar
        def _(act):
            norm.start_act(nc, act)
            norm.square(nc, act, 0)
            norm.guess(nc, act, 0)

        @block.vector
        def _(dve):
            dve.sem_inc(divided, DC)
            dve.sem_inc(x_new, DC)
            dve.wait_ge(sums_in, 16)
            nc.vector.reciprocal(recips[:], sums[:]).then_inc(recips_ready, 1)

            def tile(b, half):
                t = b * 2 + half
                for c in range(DC):
                    dve.wait_ge(spread, t * DC + c + 1)
                    dve.wait_ge(heads_in[half], b * 32 + 32)
                    nc.vector.tensor_tensor(o_n[:, half, c], o_in[:, half, c], recip_bank[c][:], ALU.mult)\
                        .then_inc(divided, 1)
                for c in range(DC):
                    dve.wait_ge(out_ready, t * DC + c + 1)
                    x = xT[:, c, bass.ds(t * TW, TW)]
                    nc.vector.scalar_tensor_tensor(x, out_bank[c][:], bo[:, c:c + 1], x, ALU.add, ALU.add)\
                        .then_inc(x_new, 1)

            norm.start_dve(nc, dve)
            with dve.Fori(0, B - 1) as b:
                tile(b, 0)
                tile(b, 1)
            norm.centre(nc, dve, 0)
            tile(B - 1, 0)
            tile(B - 1, 1)
            norm.finish(nc, dve, 0)


def feed_weights(m, io, tag):
    wfc, wpr, xn = m.sb("wfc" + tag, [P, DC, FF]), m.sb("wpr" + tag, [P, FC, D]), m.sb("xn" + tag, [P, DC, T])
    return wfc, wpr, xn, [(wfc[:], io["W_fcT"].rearrange("(c p) f -> p c f", p=P)),
                          (wpr[:], io["W_projT"].rearrange("(f p) d -> p f d", p=P))]


def feed_forward(nc, io, xT, tag, given=None, out=None, xn_scan=None, more_loads=()):
    BANKS = 4
    MEAN, VAR, TURN = 2, 5, (5, 7)
    with ExitStack() as ctx:
        m = Mem(nc, ctx)
        wfc, wpr, xn, loads = given or feed_weights(m, io, tag)
        relu = m.sb("relu" + tag, [P, 2, TW])
        hid = m.sb("hid" + tag, [P, FC, TW])
        count = m.sb("count" + tag, [P, DC, TW])
        if out is not None:
            ident = m.sb("ident" + tag, [P, P])
            made = m.sb("made" + tag, [P, DC, TW])
            x_out = m.sb("x_out" + tag, [P, TW // P, D])
            ident_in, turned, x_kept, sent = (m.sem(n + tag) for n in ("ident_in", "turned", "x_kept", "sent"))
            out_tiles = out.rearrange("b (i j p) d -> (b i) p j d", j=TW // P, p=P)
        norm = Norm(m, xT, lambda c, t: xn[:, c, bass.ds(t * TW, TW)], tag, done=0 if given is None else 1)
        hid_bank = [m.bank(f"hid_bank{i}" + tag) for i in range(BANKS)]
        y_bank = [m.bank(f"y_bank{c}" + tag) for c in range(DC)]
        turn_bank = norm.mean_bank
        more_in = m.sem("more_in" + tag)
        weights_in, hid_ready, relu_ready, hid_kept, y_ready, fired, x_new = (
            m.sem(n + tag) for n in ("weights_in", "hid_ready", "relu_ready", "hid_kept", "y_ready", "fired", "x_new"))
        block = ctx.enter_context(nc.Block())

        def at_of(t):
            return 0 if isinstance(t, int) and t == NT - 1 else None

        def tiles(eng, tile):
            if out is None:
                with eng.Fori(0, NT - 1) as t:
                    tile(t, False, True)
                tile(NT - 1, False, xn_scan is not None)
            else:
                tile(0, False, True)
                with eng.Fori(1, NT - 1) as t:
                    tile(t, True, True)
                tile(NT - 1, True, False)

        @block.sync
        def _(sp):
            if given is None:
                for dst, src in loads:
                    sp.dma_start(dst, src).then_inc(weights_in, 16)
            for dst, src in more_loads:
                sp.dma_start(dst, src).then_inc(more_in, 16)
            if more_loads:
                sp.wait_ge(more_in, 16 * len(more_loads))
            if out is not None:
                sp.sem_inc(sent, 16)
                sp.dma_start(ident[:], io["ident"]).then_inc(ident_in, 16)
                with sp.Fori(0, NT) as t:
                    sp.wait_ge(x_kept, t * 2 + 3)
                    sp.dma_start(out_tiles[bass.ds(t, 1)].rearrange("a p j d -> (a p) j d"), x_out[:]).then_inc(sent, 16)
                sp.wait_ge(sent, 16 * NT + 16)

        @block.gpsimd
        def _(pool):
            norm.start_pool(nc)

        @block.tensor
        def _(pe):
            norm.start_pe(nc, pe)
            if given is None:
                norm.mean(nc, pe, 0)
                norm.var(nc, pe, 0)
                pe.wait_ge(weights_in, 32)
            if out is not None:
                pe.wait_ge(ident_in, 16)

            def project(t, f):
                pe.wait_ge(hid_kept, t * FC + f + 1 + BANKS)
                for c in range(DC):
                    if f == 0:
                        pe.wait_ge(x_new, t * DC + c + 1)
                    mm = nc.tensor.matmul(y_bank[c][:], wpr[:, f, c * P:(c + 1) * P], hid[:, f],
                                          start=(f == 0), stop=(f == FC - 1))
                    if f == FC - 1:
                        mm.then_inc(y_ready, 1)

            def turn(t, pair):
                pe.wait_ge(x_new, t * DC + 2 * DC)
                pe.wait_ge(x_kept, t * 2 + pair + 1)
                for j in range(2):
                    for c in range(DC):
                        mm = nc.tensor.transpose(turn_bank[:, (j * DC + c) * P:(j * DC + c + 1) * P],
                                                 made[:, c, (2 * pair + j) * P:(2 * pair + j + 1) * P], ident[:])
                mm.then_inc(turned, 1)

            def tile(t, with_last, with_next):
                pe.wait_ge(norm.normed, t * DC + 2 * DC)
                for f in range(FC):
                    pe.wait_ge(hid_kept, t * FC + f + 1)
                    for c in range(DC):
                        mm = nc.tensor.matmul(hid_bank[f % BANKS][:], wfc[:, c, f * P:(f + 1) * P],
                                              xn[:, c, bass.ds(t * TW, TW)], start=(c == 0), stop=(c == DC - 1))
                    mm.then_inc(hid_ready, 1)
                    if f == MEAN and with_next:
                        if with_last:
                            pe.wait_ge(x_kept, t * 2 - 1)
                        norm.mean(nc, pe, t + 1, at_of(t))
                    if f == VAR and with_next:
                        norm.var(nc, pe, t + 1)
                    if f >= 3:
                        project(t, f - 3)
                    if f in TURN and with_last:
                        if with_next:
                            pe.wait_ge(norm.centred, t * DC + 3 * DC)
                        turn(t - 1, TURN.index(f))
                for f in range(FC - 3, FC):
                    if f == FC - 1 and at_of(t) == 0 and with_next:
                        norm.mean(nc, pe, NT + 1, 1)
                    project(t, f)
                if at_of(t) == 0 and with_next:
                    norm.var(nc, pe, NT + 1)

            tiles(pe, tile)
            if out is not None:
                for pair in range(2):
                    turn(NT - 1, pair)

        @block.scalar
        def _(act):
            norm.start_act(nc, act)
            if out is not None:
                act.sem_inc(x_kept, 1)
            if given is None:
                norm.square(nc, act, 0)
                norm.guess(nc, act, 0)

            def keep_turned(t, pair):
                act.wait_ge(sent, t * 16 + 16)
                act.wait_ge(turned, t * 2 + pair + 1)
                nc.scalar.activation(x_out[:, 2 * pair:2 * pair + 2], turn_bank[:].rearrange("p (j d) -> p j d", j=2),
                                     ACT.Copy).then_inc(x_kept, 1)

            def tile(t, with_last, with_next):
                for f in range(FC):
                    act.wait_ge(hid_ready, t * FC + f + 1)
                    act.wait_ge(hid_kept, t * FC + f + BANKS - 1)
                    nc.scalar.activation(relu[:, f % 2], hid_bank[f % BANKS][:], ACT.Relu).then_inc(relu_ready, 1)
                    if f == MEAN + 1 and with_next:
                        norm.square(nc, act, t + 1)
                    if f == VAR + 1 and with_next:
                        norm.guess(nc, act, t + 1)
                    if f in TURN and with_last:
                        keep_turned(t - 1, TURN.index(f))
                if at_of(t) == 0 and with_next:
                    norm.square(nc, act, NT + 1)
                    norm.guess(nc, act, NT + 1)

            tiles(act, tile)
            if out is not None:
                for pair in range(2):
                    keep_turned(NT - 1, pair)

        @block.vector
        def _(dve):
            norm.start_dve(nc, dve)
            dve.sem_inc(hid_kept, BANKS)
            dve.sem_inc(x_new, DC)
            if given is None:
                norm.centre(nc, dve, 0)
                norm.finish(nc, dve, 0)

            def tile(t, with_last, with_next):
                for f in range(FC):
                    dve.wait_ge(relu_ready, t * FC + f + 1)
                    nc.vector.scalar_tensor_tensor(hid[:, f], hid_bank[f % BANKS][:], 0.0, relu[:, f % 2],
                                                   ALU.max, ALU.mult).then_inc(hid_kept, 1)
                    if f == MEAN and with_next:
                        norm.centre(nc, dve, t + 1, at_of(t))
                for_scan = at_of(t) == 0 and with_next
                if with_next:
                    norm.finish(nc, dve, t + 1, (lambda c, t: scan_tokens(c, 0)) if for_scan else None)
                if for_scan:
                    norm.centre(nc, dve, NT + 1, 1)
                n = t * DC * LIF_STEPS
                for k in range(LIF_STEPS):
                    for c in range(DC):
                        if k == 0:
                            dve.wait_ge(y_ready, t * DC + c + 1)
                            nc.vector.tensor_scalar(count[:, c], y_bank[c][:], THETA[0], None, ALU.is_gt)\
                                .then_inc(fired, 1)
                        else:
                            dve.wait_ge(fired, n + DC * (k - 1) + c + 1)
                            nc.vector.scalar_tensor_tensor(count[:, c], y_bank[c][:], THETA[k], count[:, c],
                                                           ALU.is_gt, ALU.add).then_inc(fired, 1)
                if with_last:
                    dve.wait_ge(turned, t * 2)
                for c in range(DC):
                    dve.wait_ge(fired, n + DC * (LIF_STEPS - 1) + c + 1)
                    x = xT[:, c, bass.ds(t * TW, TW)]
                    nc.vector.scalar_tensor_tensor(x if out is None else made[:, c], count[:, c], 1.0 / LIF_STEPS, x,
                                                   ALU.mult, ALU.add).then_inc(x_new, 1)
                if for_scan:
                    norm.finish(nc, dve, NT + 1, lambda c, t: scan_tokens(c, 1))

            def scan_tokens(c, h):
                return xn_scan[:, c, TAPS - 1 + h * TW:TAPS - 1 + (h + 1) * TW]

            tiles(dve, tile)


def scan_weights(m, io):
    w = {n: m.sb(n + "_s", shape) for n, shape in (
        ("wx", [P, DC, D]), ("wz", [P, DC, D]), ("wout", [P, DC, D]), ("wpar", [P, DC, R + 2 * NS]), ("wdt", [R, D]),
        ("wtap", [P, TAPS, DC, D]), ("b_dt", [P, DC]), ("d_par", [P, DC]), ("ident", [P, P]), ("decay", [P, 6, DC, NS]))}
    loads = [(to, io[n].rearrange("(c p) n -> p c n", p=P)) for to, n in
             ((w["wx"][:], "W_xT"), (w["wz"][:], "W_zT"), (w["wout"][:], "W_outT"), (w["wpar"][:], "W_paramsT"),
              (w["decay"][:, 0], "A_log"))]
    loads += [(w["wdt"][:], io["W_dtT"]), (w["b_dt"][:], io["b_dt"]), (w["d_par"][:], io["D_param"]),
              (w["ident"][:], io["ident"])]
    loads += [(w["wtap"][:, :, c, :], io["conv"].partition_broadcast(P)) for c in range(DC)]
    return w, loads


def scan(nc, io, xT, xn, w, bc_scr):
    NU = NS * DC
    BC = 4
    WR = 4
    UF = (2, 8)
    DTF = (4, 6)
    ZF = (10, 12)
    BANKED = 14
    D_UNIT = 10
    with ExitStack() as ctx:
        m = Mem(nc, ctx)
        wx, wz, wout, wtap, wpar, wdt, b_dt, d_par, ident = (w[n] for n in (
            "wx", "wz", "wout", "wtap", "wpar", "wdt", "b_dt", "d_par", "ident"))
        d_diag = m.sb("d_diag", [P, DC, P])
        ones = m.sb("ones_s", [P, 1])
        decay = w["decay"]
        neg_a, a_col, is_small, not_small, a_den, a_rec = (decay[:, i] for i in range(6))
        small_any = m.sb("small_any", [P, 1])
        small_int = m.sb("small_int", [1, 1], I32)
        par = m.sb("par", [R + 2 * NS, 2, TW])
        log_part, exp_part = m.sb("log_part", [P, 2, TW]), m.sb("exp_part", [P, 2, TW])
        dt, u, sz = (m.sb(n, [P, 2, DC, S]) for n in ("dt", "u", "sz"))
        bc = m.sb("bc", [P, BC, 2, S])
        a_t, w_in, h_out = (m.sb(n, [P, WR, S]) for n in ("a_t", "w_in", "h_out"))
        norm = Norm(m, xT, None, "_s", done=TPB)
        work = [m.bank(f"work{i}") for i in range(2)]
        u_bank = (norm.mean_bank, norm.var_bank)
        y_bank = [m.bank(f"ys_bank{i}") for i in range(2 * DC)]

        (exp_a, decay_set, small_summed, zeros_set, taps_set, prep_made, prep_used, par_out, soft_act,
         soft_dve, decays, inputs, scaled, scanned, weighted, summed, gated, out_made, x_new) = (
            m.sem(n + "_s") for n in (
                "exp_a", "decay_set", "small_summed", "zeros_set", "taps_set", "prep_made", "prep_used",
                "par_out", "soft_act", "soft_dve", "decays", "inputs", "scaled", "scanned", "weighted", "summed",
                "gated", "out_made", "x_new"))
        pool_waited, act_waited, dve_waited = (m.sem(n) for n in ("pool_waited_scan", "act_waited_scan", "dve_waited_scan"))
        bc_in = [m.sem(f"bc_in{i}") for i in range(BC)]
        block = ctx.enter_context(nc.Block())

        next_pieces, own_pieces = [], []
        for h, (mean, centre, square, var, guess, finish) in enumerate(((0, 1, 6, 3, 8, 6), (3, 7, 12, 9, 14, 12))):
            next_pieces += [(mean, "pe", "mean", h), (centre, "dve", "centre", h), (square, "act", "square", h),
                            (var, "pe", "var", h), (guess, "act", "guess", h), (finish, "dve", "finish", h)]
        for i, s in enumerate((7, 12, 13, 15, 17, 17, 20, 20, 21, 23)):
            next_pieces.append((s, "pe", "make", i))
            if i // 2 * 2 in UF:
                next_pieces.append((s + 1, "pe", "make_rest", i))
        for name, s, arg in (("keep_par", 12, 0), ("keep_par", 17, 1), ("silu_u", 22, 0), ("soft", 23, 0),
                             ("soft", 27, 1), ("silu_u", 30, 1)):
            next_pieces.append((s, "act", name, arg))
        next_pieces += [(22, "dve", "soft", 0), (25, "dve", "soft", 1)]
        next_pieces.sort(key=lambda piece: piece[0])
        first_pieces = [piece for piece in next_pieces if piece[2] not in ("mean", "centre", "square", "var", "guess", "finish")]
        for i, s in enumerate((0, 0, 2, 2)):
            own_pieces.append((s, "pe", "make", ZF[0] + i))
        own_pieces += [(5, "act", "silu_z", 0), (7, "act", "silu_z", 1)]

        def prepare(engine, run, b, pieces, slot=None):
            for s, e, name, arg in pieces:
                if e == engine and (slot is None or s == slot):
                    run[name](b, arg)

        def batches(eng, body):
            body(0, False, True)
            with eng.Fori(1, B - 1) as b:
                body(b, True, True)
            body(B - 1, True, False)

        def turn(b):
            return bass.ds(b % 2, 1)

        def tile_of(x, b, f, h):
            return x[:, turn(b), f, h * TW:(h + 1) * TW].rearrange("p a t -> p (a t)")

        @block.sync
        def _(sp):
            sp.sem_inc(par_out, 16)

            def bc_out(b):
                sp.wait_ge(prep_used, b * BANKED + 4)
                sp.dma_start(bc_scr[bass.ds(b, 1)].rearrange("a n t -> (a n) t"),
                             par[R:R + 2 * NS].rearrange("p h t -> p (h t)")).then_inc(par_out, 16)

            def body(b, with_last, with_next):
                sp.wait_ge(par_out, b * 16 + 32)
                for n in range(NS):
                    sp.wait_ge(weighted, b * NU + 2 * n + 2)
                    src = bc_scr[bass.ds(b, 1)].rearrange("a (g n) t -> a n g t", n=NS)[:, n]
                    sp.dma_start(bc[:, n % BC], src.rearrange("a g t -> (a g) t").partition_broadcast(P))\
                        .then_inc(bc_in[n % BC], 16)
                    if n == 11 and with_next:
                        bc_out(b + 1)

            bc_out(0)
            batches(sp, body)

        @block.gpsimd
        def _(pool):
            norm.start_pool(nc)
            nc.gpsimd.memset(xn[:, :, 0:TAPS - 1], 0.0).then_inc(zeros_set, 1)
            nc.gpsimd.memset(ones[:], 1.0).then_inc(zeros_set, 1)

            def body(b, with_last, with_next):
                for k in range(NU):
                    n, f = k // DC, k % DC
                    pool.wait_ge(bc_in[n % BC], b * (NS // BC * 16) + (n // BC * 16 + 16))
                    if k < DC:
                        pool.wait_ge(prep_used, b * BANKED + UF[f] + 4)
                    pool.wait_ge(scanned, b * NU + k + 1)
                    by_itself(pool, pool_waited)
                    nc.gpsimd.tensor_tensor(w_in[:, k % WR], u[:, turn(b), f].rearrange("p a t -> p (a t)"),
                                            bc[:, n % BC, 0], ALU.mult).then_inc(inputs, 1)

            batches(pool, body)

        @block.tensor
        def _(pe):
            norm.start_pe(nc, pe)
            pe.sem_inc(prep_made, 1)
            pe.sem_inc(summed, WR)

            def taps_of(b, i, taps):
                if isinstance(b, int) and b == 0:
                    pe.wait_ge(taps_set, TAPS + DC)
                f, h = UF.index(i // 2 * 2), i % 2
                for tap in taps:
                    for c in range(DC):
                        mm = nc.tensor.matmul(u_bank[h][:], wtap[:, tap, c, f * P:(f + 1) * P],
                                              xn[:, c, tap + h * TW:tap + (h + 1) * TW],
                                              start=(tap == 0 and c == 0), stop=(tap == TAPS - 1 and c == DC - 1))
                return mm

            def make(b, i):
                h = i % 2
                first = i - h
                f = [firsts.index(first) for firsts in ((0,), UF, DTF, ZF) if first in firsts][0]
                if first != UF[0]:
                    last = {0: ZF[1] - BANKED, DTF[0]: 0, DTF[1]: DTF[0], UF[1]: UF[0], ZF[0]: DTF[1], ZF[1]: ZF[0]}[first] + h
                    pe.wait_ge(prep_used, b * BANKED + last + 3)
                features, tokens = slice(f * P, (f + 1) * P), slice(TAPS - 1 + h * TW, TAPS - 1 + (h + 1) * TW)
                out = work[h][:]
                if i < 2:
                    pe.wait_ge(x_new, b * 4 + 4)
                    pe.wait_ge(norm.normed, b * 2 * DC + (h + 2) * DC)
                    out = work[h][0:R + 2 * NS]
                    products = [(wpar[:, c], xn[:, c, tokens]) for c in range(DC)]
                elif first in UF:
                    taps_of(b, i, range(TAPS // 2))
                    return
                elif first in DTF:
                    pe.wait_ge(prep_used, b * BANKED + 4)
                    products = [(wdt[:, features], par[0:R, h])]
                else:
                    products = [(wz[:, c, features], xn[:, c, tokens]) for c in range(DC)]
                for n, (w, x) in enumerate(products):
                    mm = nc.tensor.matmul(out, w, x, start=(n == 0), stop=(n == len(products) - 1))
                mm.then_inc(prep_made, 1)

            run = {"mean": lambda b, h: norm.mean(nc, pe, b * 2 + h), "var": lambda b, h: norm.var(nc, pe, b * 2 + h),
                   "make": make,
                   "make_rest": lambda b, i: taps_of(b, i, range(TAPS // 2, TAPS)).then_inc(prep_made, 1)}

            def unit(b, k):
                f = k % DC
                if 0 <= k < DC:
                    pe.wait_ge(gated, b * 4 + 4)
                pe.wait_ge(weighted, b * NU + k + 9)
                for h in range(2):
                    if k - f == D_UNIT:
                        nc.tensor.matmul(y_bank[2 * f + h][:], d_diag[:, f], tile_of(u, b, f, h), start=False, stop=False)
                    mm = nc.tensor.matmul(y_bank[2 * f + h][:], ident[:], h_out[:, k % WR, h * TW:(h + 1) * TW],
                                          start=(0 <= k < DC), stop=(k % NU >= NU - DC))
                mm.then_inc(summed, 1)

            def out(b, q, made):
                c, h = q // 2, q % 2
                pe.wait_ge(gated, b * 4 + 8)
                pe.wait_ge(prep_used, made * BANKED + 2)
                pe.wait_ge(x_new, b * 4 + q + 7)
                for f in range(DC):
                    mm = nc.tensor.matmul(work[q % 2][:], wout[:, f, c * P:(c + 1) * P], tile_of(u, b, f, h),
                                          start=(f == 0), stop=(f == DC - 1))
                mm.then_inc(out_made, 1)

            def body(b, with_last, with_next):
                for k in range(NU):
                    if k or with_last:
                        unit(b, k - 1)
                    if with_last and k in (4, 6):
                        for q in range(2):
                            out(b - 1, (k - 4) + q, b + 1)
                    prepare("pe", run, b, own_pieces, k)
                    if with_next and k == 0:
                        pe.wait_ge(prep_used, b * BANKED + ZF[0] + 2)
                    if with_next:
                        prepare("pe", run, b + 1, next_pieces, k)

            pe.wait_ge(zeros_set, 2)
            prepare("pe", run, 0, first_pieces)
            pe.wait_ge(decay_set, 8)
            nc.tensor.matmul(y_bank[0][0:1, 0:1], small_any[:], ones[:], start=True, stop=True)\
                .then_inc(small_summed, 1)
            batches(pe, body)
            unit(B, -1)
            for q in range(4):
                out(B - 1, q, B)

        @block.scalar
        def _(act):
            norm.start_act(nc, act)

            def keep_par(b, h):
                act.wait_ge(prep_made, b * BANKED + h + 2)
                act.wait_ge(par_out, b * 16 + 16)
                nc.scalar.activation(par[:, h], work[h][0:R + 2 * NS], ACT.Copy).then_inc(prep_used, 1)

            def soft(b, f):
                n = b * 12 + 6 * f
                for h in range(2):
                    act.wait_ge(prep_made, b * BANKED + DTF[f] + h + 2)
                    act.wait_ge(soft_dve, b * 16 + 8 * f + h + 7)
                    by_itself(act, act_waited)
                    nc.scalar.activation(exp_part[:, h], work[h][:], ACT.Abs, bias=b_dt[:, f:f + 1]).then_inc(soft_act, 1)
                    nc.scalar.activation(tile_of(dt, b, f, h), work[h][:], ACT.Relu, bias=b_dt[:, f:f + 1])\
                        .then_inc(prep_used, 1)
                for h in range(2):
                    act.wait_ge(soft_act, n + h + 1)
                    nc.scalar.activation(exp_part[:, h], exp_part[:, h], ACT.Exp, scale=-1.0).then_inc(soft_act, 1)
                for h in range(2):
                    act.wait_ge(soft_act, n + h + 3)
                    nc.scalar.activation(log_part[:, h], exp_part[:, h], ACT.Ln, bias=ones[:]).then_inc(soft_act, 1)

            def silu(b, first, bank, to, f):
                for h in range(2):
                    act.wait_ge(prep_made, b * BANKED + first + h + 2)
                    by_itself(act, act_waited)
                    nc.scalar.activation(tile_of(to, b, f, h), bank[h][:], ACT.Silu).then_inc(prep_used, 1)

            run = {"square": lambda b, h: norm.square(nc, act, b * 2 + h),
                   "guess": lambda b, h: norm.guess(nc, act, b * 2 + h),
                   "keep_par": keep_par, "soft": soft,
                   "silu_u": lambda b, f: silu(b, UF[f], u_bank, u, f), "silu_z": lambda b, f: silu(b, ZF[f], work, sz, f)}

            def body(b, with_last, with_next):
                for k in range(NU):
                    n, f = k // DC, k % DC
                    if k < DC:
                        act.wait_ge(soft_dve, b * 16 + 8 * f + 16)
                    act.wait_ge(scanned, b * NU + k + 1)
                    by_itself(act, act_waited)
                    nc.scalar.activation(a_t[:, k % WR], dt[:, turn(b), f].rearrange("p a t -> p (a t)"), ACT.Exp,
                                         scale=a_col[:, f, n:n + 1]).then_inc(decays, 1)
                    prepare("act", run, b, own_pieces, k)
                    if with_next:
                        prepare("act", run, b + 1, next_pieces, k)

            act.sem_inc(prep_used, 2)
            nc.scalar.activation(a_den, neg_a, ACT.Exp).then_inc(exp_a, 1)
            act.wait_ge(zeros_set, 2)
            prepare("act", run, 0, first_pieces)
            act.wait_ge(decay_set, 1)
            batches(act, body)

        @block.vector
        def _(dve):
            norm.start_dve(nc, dve)
            dve.sem_inc(soft_dve, 8)
            dve.sem_inc(scanned, WR)
            dve.sem_inc(weighted, 8)
            dve.sem_inc(gated, 4)
            dve.sem_inc(x_new, 8)
            def soft(b, f):
                to, ln, e = (lambda h: tile_of(dt, b, f, h)), (lambda h: log_part[:, h]), (lambda h: exp_part[:, h])
                steps = [
                    lambda h: nc.vector.tensor_tensor(to(h), to(h), ln(h), ALU.add),
                    lambda h: nc.vector.tensor_scalar(ln(h), e(h), 1.0, 1.0, ALU.add, ALU.subtract),
                    lambda h: nc.vector.tensor_tensor(e(h), e(h), ln(h), ALU.subtract),
                    lambda h: nc.vector.tensor_tensor(to(h), to(h), e(h), ALU.add)]
                dve.wait_ge(prep_used, b * BANKED + DTF[f] + 4)
                for n, step in enumerate(steps):
                    for h in range(2):
                        if n == 0:
                            dve.wait_ge(soft_act, b * 12 + 6 * f + h + 5)
                        else:
                            dve.wait_ge(soft_dve, b * 16 + 8 * f + 2 * n + h + 7)
                        step(h).then_inc(soft_dve, 1)

            def finish(b, h):
                dve.wait_ge(prep_made, b * BANKED + 1)
                norm.finish(nc, dve, b * 2 + h, lambda c, t: xn[:, c, TAPS - 1 + h * TW:TAPS - 1 + (h + 1) * TW])

            run = {"centre": lambda b, h: norm.centre(nc, dve, b * 2 + h), "finish": finish, "soft": soft}

            def weigh(b, k):
                n, f = k % NU // DC, k % DC
                dve.wait_ge(scanned, b * NU + k + 1 + WR)
                nc.vector.scalar_tensor_tensor(h_out[:, k % WR], h_out[:, k % WR], a_rec[:, f, n:n + 1], bc[:, n % BC, 1],
                                               ALU.mult, ALU.mult).then_inc(weighted, 1)

            for tap in range(TAPS):
                nc.vector.tensor_tensor(wtap[:, tap], wtap[:, tap], wx[:], ALU.mult).then_inc(taps_set, 1)
            for c in range(DC):
                nc.vector.tensor_scalar(d_diag[:, c], ident[:], d_par[:, c:c + 1], None, ALU.mult).then_inc(taps_set, 1)
            dve.wait_ge(exp_a, 1)
            steps = [
                lambda: nc.vector.tensor_scalar(a_col, a_den, -1.0, None, ALU.mult),
                lambda: nc.vector.tensor_scalar(is_small, a_den, 1e-8, None, ALU.is_lt),
                lambda: nc.vector.tensor_scalar(not_small, is_small, -1.0, 1.0, ALU.mult, ALU.add),
                lambda: nc.vector.scalar_tensor_tensor(a_den, a_col, 1e-10, not_small, ALU.add, ALU.mult),
                lambda: nc.vector.tensor_tensor(a_den, a_den, is_small, ALU.add),
                lambda: nc.vector.reciprocal(a_rec, a_den),
                lambda: nc.vector.tensor_copy(neg_a, is_small),
                lambda: nc.vector.tensor_reduce(small_any[:], neg_a.rearrange("p c n -> p (c n)"), AX_X, ALU.add)]
            for n, step in enumerate(steps):
                if n:
                    dve.wait_ge(decay_set, n)
                step().then_inc(decay_set, 1)

            prepare("dve", run, 0, first_pieces)
            dve.wait_ge(small_summed, 1)
            nc.vector.tensor_copy(small_int[:], y_bank[0][0:1, 0:1]).then_inc(decay_set, 1)
            dve.wait_ge(decay_set, len(steps) + 1)
            small = dve.value_load(small_int[:])

            quarters = [(f, h) for f in range(DC) for h in range(2)]

            def gate(b):
                dve.wait_ge(summed, b * NU + NU + WR)
                dve.wait_ge(prep_used, b * BANKED + BANKED + 2)
                for f, h in quarters:
                    nc.vector.tensor_tensor(tile_of(u, b, f, h), y_bank[2 * f + h][:], tile_of(sz, b, f, h), ALU.mult)\
                        .then_inc(gated, 1)

            def add(b, q):
                c, h = q // 2, q % 2
                dve.wait_ge(out_made, b * 4 + q + 1)
                x = xT[:, c, bass.ds(b * S + h * TW, TW)]
                nc.vector.tensor_tensor(x, work[q % 2][:], x, ALU.add).then_inc(x_new, 1)

            def body(b, with_last, with_next):
                for k in range(NU):
                    n, f = k // DC, k % DC
                    dve.wait_ge(decays, b * NU + k + 1)
                    dve.wait_ge(inputs, b * NU + k + 1)
                    dve.wait_ge(summed, b * NU + k + 1)
                    by_itself(dve, dve_waited)
                    with dve.If(small != 0):
                        nc.vector.scalar_tensor_tensor(h_out[:, k % WR], dt[:, turn(b), f].rearrange("p a t -> p (a t)"),
                                                       is_small[:, f, n:n + 1], w_in[:, k % WR], ALU.mult, ALU.mult)
                        dve.drain()
                        nc.vector.scalar_tensor_tensor(w_in[:, k % WR], a_t[:, k % WR], 1.0, w_in[:, k % WR],
                                                       ALU.subtract, ALU.mult)
                        dve.drain()
                        nc.vector.tensor_tensor(w_in[:, k % WR], w_in[:, k % WR], h_out[:, k % WR], ALU.add)\
                            .then_inc(scaled, 1)
                    with dve.Else():
                        nc.vector.scalar_tensor_tensor(w_in[:, k % WR], a_t[:, k % WR], 1.0, w_in[:, k % WR],
                                                       ALU.subtract, ALU.mult).then_inc(scaled, 1)
                    if k or with_last:
                        weigh(b, k - 1)
                    dve.wait_ge(scaled, b * NU + k + 1)
                    nc.vector.tensor_tensor_scan(h_out[:, k % WR], a_t[:, k % WR], w_in[:, k % WR], 0.0,
                                                 ALU.mult, ALU.add).then_inc(scanned, 1)
                    if with_last and k == 1:
                        gate(b - 1)
                    if with_last and k in (5, 7):
                        for q in range(2):
                            add(b - 1, (k - 5) + q)
                    if with_next:
                        prepare("dve", run, b + 1, next_pieces, k)

            batches(dve, body)
            weigh(B, -1)
            gate(B - 1)
            for q in range(4):
                add(B - 1, q)


def lay_out(v):
    a = {k: np.asarray(x) for k, x in v.items()}

    def pairs_swapped(w):
        return w.reshape(*w.shape[:-1], D // 2, 2)[..., ::-1].reshape(w.shape)

    def cols(w):
        return w.reshape(DC, P).T

    at, mb = (lambda n: a["L0_attn_a_" + n]), (lambda n: a["L0_attn_b_" + n])
    q = [cols(x) for x in (at("Wq_r_b"), pairs_swapped(at("Wq_r_b")), at("Wu_q_b"))]
    k = [cols(x) for x in (at("Wk_r_b"), pairs_swapped(at("Wk_r_b")), at("Wu_k_b"))]
    bcol = np.stack([at("Wd_q_b"), at("Wd_kv_b")] + [x[:, c] for side in (q, k) for c in range(DC) for x in side], 1)
    theta = np.float32(10000.0) ** (np.float32(-2.0) * np.arange(D // 2, dtype=np.float32)) / np.float32(D // 2)
    angle = np.arange(S, dtype=np.float32)[:, None] * theta.astype(np.float32)[None, :]
    cos, sin = np.cos(angle), np.sin(angle)
    out = {
        "x": at("x"), "ident": np.eye(P, dtype=np.float32),
        "cos": np.repeat(cos.T, 2, axis=0), "sin": np.stack([-sin.T, sin.T], 1).reshape(D, S),
        "Wd_q": at("Wd_q_w"), "Wd_kv": at("Wd_kv_w"), "Wu_q": at("Wu_q_w"), "Wq_r": at("Wq_r_w"),
        "Wq_r_swap": pairs_swapped(at("Wq_r_w")), "Wu_k": at("Wu_k_w"), "Wk_r": at("Wk_r_w"),
        "Wk_r_swap": pairs_swapped(at("Wk_r_w")), "Wu_v": at("Wu_v_w"),
        "bv": np.broadcast_to(at("Wu_v_b"), (P, D)), "bcol_attn": bcol,
        "Wo": at("Wo_w"), "bo": cols(at("Wo_b")),
        "head_of": np.repeat(np.eye(H, dtype=np.float32), HD, axis=1),
        "W_fcT": a["L0_ffn_W_fc"].T, "W_projT": a["L0_ffn_W_proj"].T,
        "W_xT": mb("W_x").T, "W_zT": mb("W_z").T, "W_paramsT": mb("W_params").T, "W_dtT": mb("W_dt").T,
        "W_outT": mb("W_out").T, "conv": mb("conv_w").reshape(D, TAPS).T, "b_dt": cols(mb("b_dt")),
        "D_param": cols(mb("D_param")), "A_log": mb("A_log"),
    }
    return {k: np.ascontiguousarray(x) for k, x in out.items()}


def program(nc, io, out):
    qk_parts = nc.dram_tensor("qk_parts", (B * 2 * DC, P, 3, S), BF16, kind="Internal").ap()
    o_scr = nc.dram_tensor("o_scr", (B * NG, P, S), F32, kind="Internal").ap()
    recip_scr = nc.dram_tensor("recip_scr", (B * H, S), F32, kind="Internal").ap()
    bc_scr = nc.dram_tensor("bc_scr", (B, 2 * NS, S), F32, kind="Internal").ap()
    with ExitStack() as ctx:
        xT = ctx.enter_context(nc.sbuf_tensor("xT", [P, DC, T], F32))
        with ExitStack() as first:
            vT = first.enter_context(nc.sbuf_tensor("vT", [P, B * NG, QT, G * HD], F32))
            q_stack = first.enter_context(nc.sbuf_tensor("qs0", [P, 2, G, TW], BF16))
            k_stack = first.enter_context(nc.sbuf_tensor("ks0", [P, G, S], BF16))
            project(nc, io, xT, vT, qk_parts, q_stack, k_stack)
            attend(nc, io, vT, qk_parts, q_stack, k_stack, o_scr)
        with ExitStack() as second:
            m = Mem(nc, second)
            xn_scan = m.sb("xn_s", [P, DC, TAPS - 1 + S])
            w, loads = scan_weights(m, io)
            with ExitStack() as feed:
                given = feed_weights(Mem(nc, feed), io, "_f1")
                merge_heads(nc, io, xT, o_scr, recip_scr, given[2], given[3])
                feed_forward(nc, io, xT, "_f1", given=given, xn_scan=xn_scan, more_loads=loads)
            scan(nc, io, xT, xn_scan, w, bc_scr)
        feed_forward(nc, io, xT, "_f2", out=out)


def kernel(**inputs):
    import concourse.bacc as bacc
    from concourse.bass_utils import run_bass_kernel_spmd as run

    nc = bacc.Bacc("TRN2", target_bir_lowering=False, num_devices=1)
    arrays = {f"in_{name}_dram": a for name, a in lay_out(inputs).items()}
    io = {name[3:-5]: nc.dram_tensor(name, a.shape, mybir.dt.from_np(a.dtype), kind="ExternalInput").ap()
          for name, a in arrays.items()}
    out = nc.dram_tensor("out_0_dram", (B, S, D), F32, kind="ExternalOutput").ap()
    program(nc, io, out)
    return run(nc, [arrays], core_ids=[0]).results[0]["out_0_dram"]
```
